# Optimizing a Trainium2 kernel written in Bass

```python
import numpy as np
import jax
import jax.numpy as jnp

def _softmax(x, axis=-1):
    return jax.nn.softmax(x, axis=axis)

def _gelu(x):
    return jax.nn.gelu(x, approximate=True)

def _silu(x):
    return jax.nn.silu(x)

def _sigmoid(x):
    return jax.nn.sigmoid(x)

def _layernorm(x, axis=-1, eps=1e-05):
    m = jnp.mean(x, axis=axis, keepdims=True)
    v = jnp.var(x, axis=axis, keepdims=True)
    return (x - m) / jnp.sqrt(v + eps)

def _scatter_add(tgt, idx, src, axis=0):
    return tgt.at[idx].add(src)

def _segment_sum(src, seg, n):
    return jax.ops.segment_sum(src, seg, n)
kernel_name = 'mk_gnn_resnorm_d2_gnn_r8_2c115c'

def setup_inputs(seed: int=0):
    np.random.seed(seed)
    _w = jnp.asarray

    def _rec_inputs():
        import jax
        import jax.numpy as jnp
        _gk = jax.random.key(seed)
        x = -0.0007083 + 1.001 * jax.random.normal(jax.random.fold_in(_gk, 1), (12500, 48), jnp.float32)
        _s = jax.random.randint(jax.random.fold_in(_gk, 2), (200000,), 0, 12500, jnp.int32)
        _d = jax.random.randint(jax.random.fold_in(_gk, 3), (200000,), 0, 12500, jnp.int32)
        _loop = jnp.arange(12500, dtype=jnp.int32)
        src = jnp.concatenate([_s, _d, _loop])
        dst = jnp.concatenate([_d, _s, _loop])
        _o = jnp.argsort(dst, stable=True)
        src = src[_o]
        dst = dst[_o]
        edge_attr_40 = jax.random.uniform(jax.random.fold_in(_gk, 13), (412500, 40), jnp.float32, 0.0, 1)
        edge_type_8 = jax.random.randint(jax.random.fold_in(_gk, 15), (412500,), 0, 8, jnp.int32)
        edge_weight = jax.random.uniform(jax.random.fold_in(_gk, 16), (412500,), jnp.float32, 0.0, 6.99999)
        edge_weight1 = jax.random.uniform(jax.random.fold_in(_gk, 17), (412500, 1), jnp.float32, 0.0, 1)
        node_type_119 = jax.random.randint(jax.random.fold_in(_gk, 18), (12500,), 0, 119, jnp.int32)
        node_vec = jax.random.uniform(jax.random.fold_in(_gk, 19), (12500,), jnp.float32, 0.0, 1.49999)
        return (x, src, dst, edge_attr_40, edge_type_8, edge_weight, edge_weight1, node_type_119, node_vec)
    x, src, dst, edge_attr_40, edge_type_8, edge_weight, edge_weight1, node_type_119, node_vec = _rec_inputs()

    def _L0_gnn_setup():
        import jax, jax.numpy as jnp
        import numpy as np
        CUTOFF = 6.0
        LN_EPS = 1e-05
        key = jax.random.key(seed)
        ks = jax.random.split(key, 16)
        N, E, H, R, NEL, G = (6250, 100000, 48, 40, 119, 32)
        inp = {'h': jax.random.normal(ks[0], (N, H), jnp.float32), 'edge_index': jax.random.randint(ks[1], (2, E), 0, N, jnp.int64), 'edge_attr': jax.random.uniform(ks[2], (E, R), jnp.float32), 'distances': jax.random.uniform(ks[3], (E,), jnp.float32) * 7.0, 'atom_z': jax.random.randint(ks[4], (N,), 0, NEL, jnp.int64), 'node_mult': jax.random.uniform(ks[5], (N,), jnp.float32) + 0.5, 'batch': jnp.zeros((N,), jnp.int64), 'W1': jax.random.normal(ks[6], (H, R), jnp.float32) / np.sqrt(R), 'b1': jax.random.normal(ks[7], (H,), jnp.float32) * 0.01, 'W2': jax.random.normal(ks[8], (H, H), jnp.float32) / np.sqrt(H), 'b2': jax.random.normal(ks[9], (H,), jnp.float32) * 0.01, 'emb': jax.random.normal(ks[10], (NEL, G), jnp.float32) * 0.01, 'adaptW': jax.random.normal(ks[11], (G, G), jnp.float32) * 0.01, 'gamma': jnp.ones((H,), jnp.float32), 'beta': jnp.zeros((H,), jnp.float32)}
        return inp
    _L0_gnn_all = _L0_gnn_setup()
    _L0_gnn_in = {k: v for k, v in _L0_gnn_all.items() if k in ('W1', 'b1', 'W2', 'b2', 'emb', 'adaptW', 'gamma', 'beta')}
    del _L0_gnn_all

    def _L1_gnn_setup():
        import jax, jax.numpy as jnp
        import numpy as np
        N_NODES = 6250
        N_EDGES = 200000
        IN_FEAT = 48
        OUT_FEAT = 48
        NUM_RELS = 8
        key = jax.random.key(seed)
        ks = jax.random.split(key, 9)
        s1 = float(np.sqrt(2.0) * np.sqrt(6.0 / (IN_FEAT + IN_FEAT)))
        s2 = float(np.sqrt(2.0) * np.sqrt(6.0 / (IN_FEAT + OUT_FEAT)))
        return {'inputs': jax.random.normal(ks[0], (N_NODES, IN_FEAT), dtype=jnp.float32), 'norm': jax.random.uniform(ks[1], (N_EDGES, 1), dtype=jnp.float32), 'weight1': jax.random.uniform(ks[2], (NUM_RELS, IN_FEAT, IN_FEAT), jnp.float32, -s1, s1), 'weight2': jax.random.uniform(ks[3], (NUM_RELS, IN_FEAT, OUT_FEAT), jnp.float32, -s2, s2), 'bias1': jax.random.normal(ks[4], (IN_FEAT,), dtype=jnp.float32) * 0.1, 'bias2': jax.random.normal(ks[5], (OUT_FEAT,), dtype=jnp.float32) * 0.1, 'src': jax.random.randint(ks[6], (N_EDGES,), 0, N_NODES, dtype=jnp.int64) if jax.config.jax_enable_x64 else jax.random.randint(ks[6], (N_EDGES,), 0, N_NODES).astype(jnp.int32), 'dst': jax.random.randint(ks[7], (N_EDGES,), 0, N_NODES).astype(jnp.int32), 'rel_type': jax.random.randint(ks[8], (N_EDGES,), 0, NUM_RELS).astype(jnp.int32)}
    _L1_gnn_all = _L1_gnn_setup()
    _L1_gnn_in = {k: v for k, v in _L1_gnn_all.items() if k in ('weight1', 'weight2', 'bias1', 'bias2')}
    del _L1_gnn_all
    return {'x': x, 'src': src, 'dst': dst, 'edge_attr_40': edge_attr_40, 'edge_type_8': edge_type_8, 'edge_weight': edge_weight, 'edge_weight1': edge_weight1, 'node_type_119': node_type_119, 'node_vec': node_vec, 'L0_gnn_W1': _L0_gnn_in['W1'], 'L0_gnn_b1': _L0_gnn_in['b1'], 'L0_gnn_W2': _L0_gnn_in['W2'], 'L0_gnn_b2': _L0_gnn_in['b2'], 'L0_gnn_emb': _L0_gnn_in['emb'], 'L0_gnn_adaptW': _L0_gnn_in['adaptW'], 'L0_gnn_gamma': _L0_gnn_in['gamma'], 'L0_gnn_beta': _L0_gnn_in['beta'], 'L1_gnn_weight1': _L1_gnn_in['weight1'], 'L1_gnn_weight2': _L1_gnn_in['weight2'], 'L1_gnn_bias1': _L1_gnn_in['bias1'], 'L1_gnn_bias2': _L1_gnn_in['bias2']}

def reference(x, src, dst, edge_attr_40, edge_type_8, edge_weight, edge_weight1, node_type_119, node_vec, L0_gnn_W1, L0_gnn_b1, L0_gnn_W2, L0_gnn_b2, L0_gnn_emb, L0_gnn_adaptW, L0_gnn_gamma, L0_gnn_beta, L1_gnn_weight1, L1_gnn_weight2, L1_gnn_bias1, L1_gnn_bias2):
    import jax
    import jax.numpy as jnp

    def _L0_gnn_ref(h, edge_index, edge_attr, distances, atom_z, node_mult, batch, W1, b1, W2, b2, emb, adaptW, gamma, beta):
        import jax, jax.numpy as jnp
        import numpy as np
        CUTOFF = 6.0
        LN_EPS = 1e-05
        src, dst = (edge_index[0], edge_index[1])
        N = h.shape[0]
        gate = jax.nn.silu(edge_attr @ W1.T + b1) @ W2.T + b2
        ei = emb[atom_z[src]]
        ej = emb[atom_z[dst]]
        adapt_logit = jnp.sum(ei * (ej @ adaptW.T), axis=-1, keepdims=True)
        gate = gate + adapt_logit
        cw = jnp.where(distances < CUTOFF, 0.5 * (jnp.cos(jnp.pi * distances / CUTOFF) + 1.0), 0.0)
        mj = node_mult[dst]
        msg = gate * h[dst] * (cw * mj)[:, None]
        agg = jax.ops.segment_sum(msg, src, num_segments=N)
        tot = jax.ops.segment_sum(mj, src, num_segments=N)
        agg = agg / jnp.clip(tot, 1e-08, None)[:, None]
        x = h + agg
        mu = jnp.mean(x, axis=-1, keepdims=True)
        var = jnp.mean(jnp.square(x - mu), axis=-1, keepdims=True)
        return (x - mu) / jnp.sqrt(var + LN_EPS) * gamma + beta

    def _L1_gnn_ref(inputs, norm, weight1, weight2, bias1, bias2, src, dst, rel_type):
        import jax, jax.numpy as jnp
        import numpy as np
        N_NODES = 6250
        N_EDGES = 200000
        IN_FEAT = 48
        OUT_FEAT = 48
        NUM_RELS = 8
        h1 = jax.nn.relu(jnp.einsum('ni,rij->nrj', inputs, weight1) + bias1)
        h2 = jnp.einsum('nrj,rjo->nro', h1, weight2)
        msg = h2[src, rel_type] * norm
        agg = jax.ops.segment_sum(msg, dst, num_segments=inputs.shape[0])
        return jax.nn.relu(agg + bias2)
    edge_index = jnp.stack([src, dst])
    batch0 = jnp.zeros((12500,), jnp.int32)
    x = _layernorm(x + _L0_gnn_ref(x, edge_index, edge_attr_40, edge_weight, node_type_119, node_vec, batch0, L0_gnn_W1, L0_gnn_b1, L0_gnn_W2, L0_gnn_b2, L0_gnn_emb, L0_gnn_adaptW, L0_gnn_gamma, L0_gnn_beta), axis=-1)
    x = _layernorm(x + _L1_gnn_ref(x, edge_weight1, L1_gnn_weight1, L1_gnn_weight2, L1_gnn_bias1, L1_gnn_bias2, src, dst, edge_type_8), axis=-1)
    return x

_drawn_inputs = setup_inputs


def setup_inputs(seed=0):
    import zlib

    import numpy as np

    out = dict(_drawn_inputs(seed))
    spreads = {'L0_gnn_gamma': (1.0, 0.2), 'L0_gnn_beta': (0.0, 0.1)}
    factors = {'edge_attr_40': 6.344,
     'edge_weight': 5.199,
     'node_vec': 6.772,
     'L0_gnn_W1': 3.705,
     'L0_gnn_b1': 64.0,
     'L0_gnn_W2': 3.538,
     'L0_gnn_b2': 200.0,
     'L0_gnn_emb': 64.0,
     'L0_gnn_adaptW': 64.0,
     'L1_gnn_bias2': 3.002}
    for name, (base, spread) in spreads.items():
        noise = np.random.default_rng([zlib.crc32(name.encode()), seed]).standard_normal(out[name].shape)
        drawn = base * np.exp(spread * noise) if base else spread * noise
        out[name] = jnp.asarray(drawn.astype(out[name].dtype))
    for name, factor in factors.items():
        out[name] = (out[name] * factor).astype(out[name].dtype)
    return out
```

```python
from contextlib import ExitStack

import concourse.bass as bass
from concourse import mybir

F32 = mybir.dt.float32
I32 = mybir.dt.int32
ALU = mybir.AluOpType
ACT = mybir.ActivationFunctionType
AX = mybir.AxisListType

P = 128
N, H, E, R, Z, G, RELS = 12500, 48, 412500, 40, 119, 32, 8
TILES = 8
GE = TILES * P
NG = 2 * -(-E // (2 * GE))
NODE_TILES = 4
NS = NODE_TILES * P
STEPS = -(-(N + P) // NS)
NP = STEPS * NS
PAD_NODE = N
DUMP = NP - P
DW = H + 1 + G
MW = H + 1
PI = 3.141592653589793
CUTOFF = 6.0
EPS = 1e-5


def wait_in_loop(eng, c, sem, value):
    eng.wait_ge(sem, value)
    eng.sem_inc(c["waits_passed"], 1)


def prepare(nc, t, c):
    with ExitStack() as ctx:
        def sb(name, shape, dt=F32):
            return ctx.enter_context(nc.sbuf_tensor("prep_" + name, shape, dt))

        def sem(name):
            return ctx.enter_context(nc.semaphore("prep_" + name))

        zeros = sb("zeros", [P, 4900])
        embT = sb("embT", [G, Z])
        adaptT = sb("adaptT", [G, G])
        embcat = sb("embcat", [Z, 2 * G])
        zrow = sb("zrow", [P, NS], I32)
        onehot = sb("onehot", [P, NS])
        by_dst = sb("by_dst", [P, NODE_TILES, DW])
        by_src = sb("by_src", [P, NODE_TILES, G])
        dist = sb("dist", [P, NG * TILES])
        inside = sb("inside", [P, NG * TILES])
        source = sb("source", [P, NG * TILES], I32)
        rel = sb("rel", [P, NG * TILES], I32)
        row = sb("row", [P, NG * TILES], I32)
        half_pi = sb("half_pi", [P, 1])
        ps_emb = ctx.enter_context(nc.psum_tensor("prep_ps_emb", [P, 512], F32))
        ps_cat = ctx.enter_context(nc.psum_tensor("prep_ps_cat", [P, NODE_TILES, 2 * G], F32))
        consts_in = sem("consts_in")
        emb_in = sem("emb_in")
        edges_in = sem("edges_in")
        rows_out = sem("rows_out")
        iotas = sem("iotas")
        zeroed = sem("zeroed")
        dve = sem("dve_prep")
        dist_clamped = sem("dist_clamped")
        cosine = sem("cosine")
        row_ready = sem("row_ready")
        emb_adapted = sem("emb_adapted")
        embcat_ready = sem("embcat_ready")
        nodes_in = sem("nodes_in")
        onehot_ready = sem("onehot_ready")
        looked_up = sem("looked_up")
        table_ready = sem("table_ready")
        tables_out = sem("tables_out")
        block = ctx.enter_context(nc.Block())

        @block.sync
        def _(sp):
            for dst, src in ((c["w1t"][:], t["w1t"]), (c["b1"][:], t["b1"]), (c["w2b"][0:H, :], t["w2t"]),
                             (c["w2b"][H:H + 1, :], t["b2"]), (c["gamma"][:], t["gamma"].partition_broadcast(P)),
                             (c["beta"][:], t["beta"].partition_broadcast(P)),
                             (c["bias2"][:], t["bias2"].partition_broadcast(P)), (c["wa"][:], t["wa"]),
                             (c["ba"][:], t["ba"])):
                sp.dma_start(dst, src).then_inc(consts_in, 16)
            sp.dma_start(embT[:], t["embT"]).then_inc(emb_in, 16)
            sp.dma_start(adaptT[:], t["adaptT"]).then_inc(emb_in, 16)
            sp.dma_start(embcat[:, 0:G], t["emb"]).then_inc(emb_in, 16)
            sp.dma_start(dist[:].rearrange("p (g k) -> p g k", k=TILES), t["dist"]).then_inc(edges_in, 16)
            sp.dma_start(source[:].rearrange("p (g k) -> p g k", k=TILES), t["src"]).then_inc(edges_in, 16)
            sp.dma_start(rel[:].rearrange("p (g k) -> p g k", k=TILES), t["rel"]).then_inc(edges_in, 16)
            with sp.Fori(0, STEPS) as i:
                sp.dma_start(zrow[:], t["z"][bass.DynSlice(i * NS, NS)].partition_broadcast(P)).then_inc(nodes_in, 16)
                sp.dma_start(by_dst[:, :, 0:H + 1], node_rows(t["x_mult"], i)).then_inc(nodes_in, 16)
                wait_in_loop(sp, c, table_ready, i + 1)
                sp.dma_start(t["tab_dst"][bass.DynSlice(i * NS, NS), :].rearrange("(a p) f -> p a f", p=P),
                             by_dst[:]).then_inc(tables_out, 16)
                sp.dma_start(t["tab_src"][bass.DynSlice(i * NS, NS), :].rearrange("(a p) f -> p a f", p=P),
                             by_src[:]).then_inc(tables_out, 16)
                wait_in_loop(sp, c, tables_out, (i + 1) * 32)
            sp.wait_ge(row_ready, 1)
            sp.dma_start(t["row"], row[:].rearrange("p (g k) -> p g k", k=TILES)).then_inc(rows_out, 16)
            sp.wait_ge(rows_out, 16)
            sp.wait_ge(consts_in, 16 * 9)

        @block.gpsimd
        def _(pool):
            nc.gpsimd.iota(c["iota_p"][:], pattern=[[0, 1]], base=0, channel_multiplier=1).then_inc(iotas, 1)
            nc.gpsimd.iota(c["iota_row"][:], pattern=[[1, P]], base=0, channel_multiplier=0).then_inc(iotas, 1)
            nc.gpsimd.iota(c["dump"][:], pattern=[[0, 1]], base=DUMP, channel_multiplier=1).then_inc(iotas, 1)
            pool.wait_ge(zeroed, 1)
            for k in range(TILES):
                for acc, done, w in ((t["acc0"][k], c["acc0_done"][k], MW), (t["acc1"][k], c["acc1_done"][k], H)):
                    for half in range(2):
                        pool.dma_start(acc.rearrange("(b p a) f -> b p (a f)", b=2, p=P)[half],
                                       zeros[:, 0:NP // (2 * P) * w]).then_inc(done, 16)
            for k in range(TILES):
                pool.wait_ge(c["acc0_done"][k], 32)
                pool.wait_ge(c["acc1_done"][k], 32)

        @block.vector
        def _(v):
            v.memset(zeros[:], 0.0).then_inc(zeroed, 1)
            v.memset(half_pi[:], PI / 2).then_inc(dve, 1)
            v.memset(c["ones"][:], 1.0).then_inc(dve, 1)
            v.memset(c["eps"][:], EPS).then_inc(dve, 1)
            v.memset(c["silu"][:], 1.0).then_inc(dve, 1)
            v.wait_ge(iotas, 3)
            v.tensor_copy(c["iota_pf"][:], c["iota_p"][:]).then_inc(dve, 1)
            v.tensor_copy(c["iota_rowf"][:], c["iota_row"][:]).then_inc(dve, 1)
            v.tensor_copy(c["dumpf"][:], c["dump"][:]).then_inc(dve, 1)
            v.wait_ge(dve, 7)
            v.tensor_scalar(c["before"][:], c["iota_rowf"][:], c["iota_pf"][:], None, ALU.is_lt).then_inc(dve, 1)
            v.tensor_scalar(c["ident"][:], c["iota_rowf"][:], c["iota_pf"][:], None, ALU.is_equal).then_inc(dve, 1)
            v.wait_ge(edges_in, 48)
            v.tensor_scalar(inside[:], dist[:], CUTOFF, None, ALU.is_lt).then_inc(dve, 1)
            v.wait_ge(dve, 10)
            v.scalar_tensor_tensor(dist[:], dist[:], -1.0, dist[:], ALU.mult, ALU.max).then_inc(dve, 1)
            v.wait_ge(dve, 11)
            v.tensor_scalar(dist[:], dist[:], CUTOFF, None, ALU.min).then_inc(dist_clamped, 1)
            v.scalar_tensor_tensor(row[:], source[:], float(RELS), rel[:], ALU.mult, ALU.add).then_inc(row_ready, 1)
            v.wait_ge(emb_adapted, 1)
            v.tensor_copy(embcat[:, G:2 * G], ps_emb[0:Z, 0:G]).then_inc(embcat_ready, 1)
            v.wait_ge(cosine, 1)
            v.tensor_scalar(dist[:], dist[:], 1.0, 0.5, ALU.add, ALU.mult).then_inc(dve, 1)
            v.wait_ge(dve, 12)
            v.tensor_tensor(c["cw"][:], dist[:], inside[:], ALU.mult).then_inc(dve, 1)
            with v.Fori(0, STEPS) as i:
                v.wait_ge(nodes_in, (i + 1) * 32)
                v.tensor_scalar(onehot[:], zrow[:], c["iota_pf"][:], None, ALU.is_equal).then_inc(onehot_ready, 1)
                v.wait_ge(looked_up, i + 1)
                v.tensor_copy(by_src[:], ps_cat[:, :, 0:G])
                v.tensor_copy(by_dst[:, :, H + 1:DW], ps_cat[:, :, G:2 * G]).then_inc(table_ready, 1)

        @block.scalar
        def _(act):
            act.wait_ge(dve, 1)
            act.wait_ge(dist_clamped, 1)
            act.activation(dist[:], dist[:], ACT.Sin, bias=half_pi[:], scale=-PI / CUTOFF).then_inc(cosine, 1)

        @block.tensor
        def _(pe):
            pe.wait_ge(emb_in, 48)
            pe.matmul(ps_emb[0:Z, 0:G], embT[:], adaptT[:], start=True, stop=True).then_inc(emb_adapted, 1)
            pe.wait_ge(embcat_ready, 1)
            with pe.Fori(0, STEPS) as i:
                wait_in_loop(pe, c, onehot_ready, i + 1)
                for a in range(NODE_TILES):
                    last = pe.matmul(ps_cat[:, a, :], onehot[0:Z, a * P:(a + 1) * P], embcat[:], start=True, stop=True)
                last.then_inc(looked_up, 1)


def one_of_equals(v, c, step, base, key_col, key_row, same, earlier, count, dump_off, index):
    v.tensor_tensor(same, key_row.rearrange("p (t j) -> p t j", t=TILES),
                    key_col.unsqueeze(2).broadcast_to([P, TILES, P]), ALU.is_equal).then_inc(step, 1)
    v.tensor_tensor(dump_off, c["dumpf"][:].broadcast_to([P, TILES]), key_col, ALU.subtract).then_inc(step, 1)
    v.wait_ge(step, base + 1)
    v.tensor_tensor(earlier, same, c["before"][:].unsqueeze(1).broadcast_to([P, TILES, P]), ALU.mult).then_inc(step, 1)
    v.wait_ge(step, base + 3)
    v.tensor_reduce(count, earlier, AX.X, ALU.add).then_inc(step, 1)
    v.wait_ge(step, base + 4)
    v.scalar_tensor_tensor(dump_off, count, 0.0, dump_off, ALU.is_gt, ALU.mult).then_inc(step, 1)
    v.wait_ge(step, base + 5)
    return v.tensor_tensor(index, key_col, dump_off, ALU.add)


def layer0_edges(nc, t, c):
    with ExitStack() as ctx:
        def sb(name, shape, dt=F32):
            return ctx.enter_context(nc.sbuf_tensor("e0_" + name, shape, dt))

        def sem(name):
            return ctx.enter_context(nc.semaphore("e0_" + name))

        attr = sb("attr", [R, 2, GE])
        src_row = sb("src_row", [P, 2, GE], I32)
        src_col = [sb(f"src_col{s}", [P, TILES], I32) for s in range(2)]
        dst_col = [sb(f"dst_col{s}", [P, TILES], I32) for s in range(2)]
        of_dst = sb("of_dst", [P, 2, TILES, DW])
        of_src = sb("of_src", [P, 2, TILES, G])
        same = sb("same", [P, 2, TILES, P])
        earlier = sb("earlier", [P, TILES, P])
        count = sb("count", [P, TILES])
        dump_off = sb("dump_off", [P, TILES])
        scatter_at = [sb(f"scatter_at{s}", [P, TILES], I32) for s in range(2)]
        emb_prod = sb("emb_prod", [P, TILES, G])
        adapt = sb("adapt", [P, TILES])
        weight = sb("weight", [P, TILES])
        gated = sb("gated", [P, TILES, H])
        msg = sb("msg", [P, 2, TILES, MW])
        summed = sb("summed", [P, 2, TILES, MW])
        ps_pre = [ctx.enter_context(nc.psum_tensor(f"e0_ps_pre{s}", [H, GE], F32)) for s in range(2)]
        ps_gate = [ctx.enter_context(nc.psum_tensor(f"e0_ps_gate{s}", [P, 512], F32)) for s in range(2)]
        ps_sum = [ctx.enter_context(nc.psum_tensor(f"e0_ps_sum{s}", [P, 512], F32)) for s in range(2)]
        edges_in = [sem(f"edges_in{s}") for s in range(2)]
        slot_free = sem("slot_free")
        gathered = [sem(f"gathered{s}") for s in range(2)]
        pre_ready = sem("pre_ready")
        silu_ready = sem("silu_ready")
        gate_ready = sem("gate_ready")
        step = sem("l0_step")
        index_ready = sem("index_ready")
        msg_ready = sem("msg_ready")
        sum_ready = sem("sum_ready")
        summed_ready = sem("summed_ready")
        block = ctx.enter_context(nc.Block())
        acc_done = c["acc0_done"]
        STEP = 11

        @block.sync
        def _(sp):
            with sp.Fori(0, NG // 2) as i:
                for s in range(2):
                    g = i * 2 + s
                    wait_in_loop(sp, c, slot_free, g + 1)
                    sp.dma_start(attr[:, s, :], t["attr"][:, bass.DynSlice(g * GE, GE)]).then_inc(edges_in[s], 16)
                    sp.dma_start(src_row[:, s, :],
                                 t["src_flat"][bass.DynSlice(g * GE, GE)].partition_broadcast(P)).then_inc(edges_in[s], 16)
                    sp.dma_start(src_col[s][:], t["src"][:, bass.DynSlice(g, 1), :].rearrange("p g k -> p (g k)")).then_inc(edges_in[s], 16)
                    sp.dma_start(dst_col[s][:], t["dst"][:, bass.DynSlice(g, 1), :].rearrange("p g k -> p (g k)")).then_inc(edges_in[s], 16)

        @block.gpsimd
        def _(pool):
            def gathers(i, s):
                wait_in_loop(pool, c, edges_in[s], i * 64 + 64)
                for k in range(TILES):
                    nc.gpsimd.indirect_dma_start(of_dst[:, s, k, :], None, t["tab_dst"],
                                                 bass.IndirectOffsetOnAxis(ap=dst_col[s][:, k:k + 1], axis=0)).then_inc(gathered[s], 16)
                    nc.gpsimd.indirect_dma_start(of_src[:, s, k, :], None, t["tab_src"],
                                                 bass.IndirectOffsetOnAxis(ap=src_col[s][:, k:k + 1], axis=0)).then_inc(gathered[s], 16)

            def scatters(i, s):
                wait_in_loop(pool, c, index_ready, i * 2 + s + 1)
                wait_in_loop(pool, c, summed_ready, i * 2 + s + 1)
                for k in range(TILES):
                    wait_in_loop(pool, c, acc_done[k], (i * 2 + s) * 16 + 32)
                    nc.gpsimd.indirect_dma_start(t["acc0"][k], bass.IndirectOffsetOnAxis(ap=scatter_at[s][:, k:k + 1], axis=0),
                                                 summed[:, s, k, :], None, compute_op=ALU.add).then_inc(acc_done[k], 16)

            gathers(0, 0)
            with pool.Fori(0, NG // 2 - 1) as i:
                gathers(i, 1)
                scatters(i, 0)
                gathers(i + 1, 0)
                scatters(i, 1)
            gathers(NG // 2 - 1, 1)
            scatters(NG // 2 - 1, 0)
            scatters(NG // 2 - 1, 1)
            for k in range(TILES):
                pool.wait_ge(acc_done[k], NG * 16 + 32)

        @block.scalar
        def _(act):
            with act.Fori(0, NG // 2) as i:
                for s in range(2):
                    g = i * 2 + s
                    act.wait_ge(pre_ready, g + 1)
                    for b in range(2):
                        last = act.activation(c["silu"][0:H, s, b * 512:(b + 1) * 512], ps_pre[s][:, b * 512:(b + 1) * 512],
                                              ACT.Silu, bias=c["b1"][:])
                    last.then_inc(silu_ready, 1)
                    act.wait_ge(sum_ready, g + 1)
                    for k in range(TILES):
                        act.wait_ge(acc_done[k], g * 16 + 16)
                    act.activation(summed[:, s, :, :], ps_sum[s][:, 0:TILES * MW].rearrange("p (t f) -> p t f", t=TILES),
                                   ACT.Copy).then_inc(summed_ready, 1)

        @block.tensor
        def _(pe):
            with pe.Fori(0, NG // 2) as i:
                for s in range(2):
                    g = i * 2 + s
                    wait_in_loop(pe, c, edges_in[s], i * 64 + 64)
                    for b in range(2):
                        last = pe.matmul(ps_pre[s][:, b * 512:(b + 1) * 512], c["w1t"][:], attr[:, s, b * 512:(b + 1) * 512],
                                         start=True, stop=True)
                    last.then_inc(pre_ready, 1)
                    wait_in_loop(pe, c, silu_ready, g + 1)
                    for k in range(TILES):
                        last = pe.matmul(ps_gate[s][:, k * H:(k + 1) * H], c["silu"][0:H + 1, s, k * P:(k + 1) * P],
                                         c["w2b"][:], start=True, stop=True)
                    last.then_inc(gate_ready, 1)
                    wait_in_loop(pe, c, msg_ready, g + 1)
                    for k in range(TILES):
                        last = pe.matmul(ps_sum[s][:, k * MW:(k + 1) * MW], same[:, s, k, :], msg[:, s, k, :],
                                         start=True, stop=True)
                    last.then_inc(sum_ready, 1)

        @block.vector
        def _(v):
            v.sem_inc(slot_free, 2)
            with v.Fori(0, NG // 2) as i:
                for s in range(2):
                    g = i * 2 + s
                    base = g * STEP
                    v.wait_ge(edges_in[s], i * 64 + 64)
                    for k in range(TILES):
                        v.wait_ge(acc_done[k], g * 16 + 16)
                    one_of_equals(v, c, step, base, src_col[s][:], src_row[:, s, :], same[:, s, :, :], earlier[:], count[:],
                                  dump_off[:], scatter_at[s][:]).then_inc(index_ready, 1)
                    v.wait_ge(gathered[s], i * 256 + 256)
                    v.tensor_tensor(emb_prod[:], of_dst[:, s, :, H + 1:DW], of_src[:, s, :, :], ALU.mult).then_inc(step, 1)
                    v.tensor_tensor(weight[:], of_dst[:, s, :, H], c["cw"][:, bass.DynSlice(g * TILES, TILES)], ALU.mult).then_inc(step, 1)
                    v.tensor_copy(msg[:, s, :, H], of_dst[:, s, :, H]).then_inc(step, 1)
                    v.wait_ge(step, base + 6)
                    v.tensor_reduce(adapt[:], emb_prod[:], AX.X, ALU.add).then_inc(step, 1)
                    v.wait_ge(step, base + 9)
                    v.wait_ge(gate_ready, g + 1)
                    v.tensor_tensor(gated[:], ps_gate[s][:, 0:TILES * H].rearrange("p (t f) -> p t f", t=TILES),
                                    adapt[:].unsqueeze(2).broadcast_to([P, TILES, H]), ALU.add).then_inc(step, 1)
                    v.wait_ge(step, base + 10)
                    v.tensor_tensor(gated[:], gated[:], of_dst[:, s, :, 0:H], ALU.mult).then_inc(step, 1)
                    v.wait_ge(step, base + 11)
                    v.tensor_tensor(msg[:, s, :, 0:H], gated[:], weight[:].unsqueeze(2).broadcast_to([P, TILES, H]),
                                    ALU.mult).then_inc(msg_ready, 1)
                    v.wait_ge(msg_ready, g + 1)
                    v.sem_inc(slot_free, 1)


def layer1_edges(nc, t, c):
    with ExitStack() as ctx:
        def sb(name, shape, dt=F32):
            return ctx.enter_context(nc.sbuf_tensor("e1_" + name, shape, dt))

        def sem(name):
            return ctx.enter_context(nc.semaphore("e1_" + name))

        row_col = [sb(f"row_col{s}", [P, TILES], I32) for s in range(2)]
        dst_row = sb("dst_row", [P, 2, GE], I32)
        dst_col = [sb(f"dst_col{s}", [P, TILES], I32) for s in range(2)]
        norm = sb("norm", [P, 2, TILES])
        of_src = sb("of_src", [P, 2, TILES, H])
        same = sb("same", [P, 2, TILES, P])
        earlier = sb("earlier", [P, TILES, P])
        count = sb("count", [P, TILES])
        dump_off = sb("dump_off", [P, TILES])
        scatter_at = [sb(f"scatter_at{s}", [P, TILES], I32) for s in range(2)]
        msg = sb("msg", [P, 2, TILES, H])
        summed = sb("summed", [P, 2, TILES, H])
        ps_sum = [ctx.enter_context(nc.psum_tensor(f"e1_ps_sum{s}", [P, 512], F32)) for s in range(2)]
        edges_in = [sem(f"edges_in{s}") for s in range(2)]
        slot_free = sem("slot_free")
        gathered = [sem(f"gathered{s}") for s in range(2)]
        step = sem("l1_step")
        index_ready = sem("index_ready")
        msg_ready = sem("msg_ready")
        sum_ready = sem("sum_ready")
        summed_ready = sem("summed_ready")
        block = ctx.enter_context(nc.Block())
        acc_done = c["acc1_done"]
        STEP = 5

        @block.sync
        def _(sp):
            with sp.Fori(0, NG // 2) as i:
                for s in range(2):
                    g = i * 2 + s
                    wait_in_loop(sp, c, slot_free, g + 1)
                    for dst, src in ((row_col[s], "row"), (dst_col[s], "dst"), (norm[:, s, :], "norm")):
                        sp.dma_start(dst[:] if src != "norm" else dst,
                                     t[src][:, bass.DynSlice(g, 1), :].rearrange("p g k -> p (g k)")).then_inc(edges_in[s], 16)
                    sp.dma_start(dst_row[:, s, :],
                                 t["dst_flat"][bass.DynSlice(g * GE, GE)].partition_broadcast(P)).then_inc(edges_in[s], 16)

        @block.gpsimd
        def _(pool):
            def gathers(i, s):
                wait_in_loop(pool, c, edges_in[s], i * 64 + 64)
                for k in range(TILES):
                    nc.gpsimd.indirect_dma_start(of_src[:, s, k, :], None, t["h2"],
                                                 bass.IndirectOffsetOnAxis(ap=row_col[s][:, k:k + 1], axis=0)).then_inc(gathered[s], 16)

            def scatters(i, s):
                wait_in_loop(pool, c, index_ready, i * 2 + s + 1)
                wait_in_loop(pool, c, summed_ready, i * 2 + s + 1)
                for k in range(TILES):
                    wait_in_loop(pool, c, acc_done[k], (i * 2 + s) * 16 + 32)
                    nc.gpsimd.indirect_dma_start(t["acc1"][k], bass.IndirectOffsetOnAxis(ap=scatter_at[s][:, k:k + 1], axis=0),
                                                 summed[:, s, k, :], None, compute_op=ALU.add).then_inc(acc_done[k], 16)

            gathers(0, 0)
            with pool.Fori(0, NG // 2 - 1) as i:
                gathers(i, 1)
                scatters(i, 0)
                gathers(i + 1, 0)
                scatters(i, 1)
            gathers(NG // 2 - 1, 1)
            scatters(NG // 2 - 1, 0)
            scatters(NG // 2 - 1, 1)
            for k in range(TILES):
                pool.wait_ge(acc_done[k], NG * 16 + 32)

        @block.scalar
        def _(act):
            with act.Fori(0, NG // 2) as i:
                for s in range(2):
                    g = i * 2 + s
                    act.wait_ge(sum_ready, g + 1)
                    for k in range(TILES):
                        act.wait_ge(acc_done[k], g * 16 + 16)
                    act.activation(summed[:, s, :, :], ps_sum[s][:, 0:TILES * H].rearrange("p (t f) -> p t f", t=TILES),
                                   ACT.Copy).then_inc(summed_ready, 1)

        @block.tensor
        def _(pe):
            with pe.Fori(0, NG // 2) as i:
                for s in range(2):
                    g = i * 2 + s
                    wait_in_loop(pe, c, msg_ready, g + 1)
                    if s == 1:
                        wait_in_loop(pe, c, summed_ready, i * 2 + 1)
                    for k in range(TILES):
                        last = pe.matmul(ps_sum[s][:, k * H:(k + 1) * H], same[:, s, k, :], msg[:, s, k, :],
                                         start=True, stop=True)
                    last.then_inc(sum_ready, 1)

        @block.vector
        def _(v):
            v.sem_inc(slot_free, 2)
            with v.Fori(0, NG // 2) as i:
                for s in range(2):
                    g = i * 2 + s
                    base = g * STEP
                    v.wait_ge(edges_in[s], i * 64 + 64)
                    for k in range(TILES):
                        v.wait_ge(acc_done[k], g * 16 + 16)
                    one_of_equals(v, c, step, base, dst_col[s][:], dst_row[:, s, :], same[:, s, :, :], earlier[:], count[:],
                                  dump_off[:], scatter_at[s][:]).then_inc(index_ready, 1)
                    v.wait_ge(gathered[s], i * 128 + 128)
                    v.tensor_tensor(msg[:, s, :, :], of_src[:, s, :, :], norm[:, s, :].unsqueeze(2).broadcast_to([P, TILES, H]),
                                    ALU.mult).then_inc(msg_ready, 1)
                    v.wait_ge(index_ready, g + 1)
                    v.wait_ge(msg_ready, g + 1)
                    v.sem_inc(slot_free, 1)


class Steps:

    def __init__(self, sem, each):
        self.sem, self.each, self.n = sem, each, 0

    def then(self, ins):
        ins.then_inc(self.sem, 1)
        self.n += 1

    def wait(self, eng, i):
        eng.wait_ge(self.sem, i * self.each + self.n)


LN_STEPS = 6


def layer_norm(v, c, st, i, y, out, sq, m, rstd, var_ready, root_ready, count):
    before, of = count
    wide = [P, NODE_TILES, H]
    st.then(v.tensor_reduce(m, y, AX.X, ALU.add))
    st.wait(v, i)
    st.then(v.tensor_scalar(m, m, 1.0 / H, None, ALU.mult))
    st.wait(v, i)
    st.then(v.tensor_tensor(y, y, m.unsqueeze(2).broadcast_to(wide), ALU.subtract))
    st.wait(v, i)
    st.then(v.tensor_tensor(sq, y, y, ALU.mult))
    st.wait(v, i)
    v.tensor_reduce(m, sq, AX.X, ALU.add).then_inc(var_ready, 1)
    v.wait_ge(root_ready, i * of + before + 1)
    st.then(v.reciprocal(rstd, rstd))
    st.wait(v, i)
    st.then(v.tensor_tensor(out, y, rstd.unsqueeze(2).broadcast_to(wide), ALU.mult))
    st.wait(v, i)


def node_rows(ap, i):
    return ap[bass.DynSlice(i * NS, NS), :].rearrange("(a p) f -> p a f", p=P)


def layer0_nodes(nc, t, c):
    with ExitStack() as ctx:
        def sb(name, shape, dt=F32):
            return ctx.enter_context(nc.sbuf_tensor("n0_" + name, shape, dt))

        def sem(name):
            return ctx.enter_context(nc.semaphore("n0_" + name))

        acc = sb("acc", [P, TILES, NODE_TILES, MW])
        x = sb("x", [P, NODE_TILES, H])
        total = sb("total", [P, NODE_TILES, MW])
        y = sb("y", [P, NODE_TILES, H])
        sq = sb("sq", [P, NODE_TILES, H])
        x1 = sb("x1", [P, NODE_TILES, H])
        m = sb("m", [P, NODE_TILES])
        rstd = sb("rstd", [P, NODE_TILES])
        x1T = sb("x1T", [H, NS])
        h1T = sb("h1T", [2 * H, RELS // 2, NS])
        h2 = sb("h2", [P, NODE_TILES, RELS * H])
        ps_t = ctx.enter_context(nc.psum_tensor("n0_ps_t", [H, 512], F32))
        ps_h1 = ctx.enter_context(nc.psum_tensor("n0_ps_h1", [2 * H, 2, 512], F32))
        ps_h2 = ctx.enter_context(nc.psum_tensor("n0_ps_h2", [P, NODE_TILES, 512], F32))
        nodes_in = sem("nodes_in")
        step = sem("n0_step")
        var_ready = sem("var_ready")
        root_ready = sem("root_ready")
        x1_ready = sem("x1_ready")
        x1T_in_psum = sem("x1T_in_psum")
        x1T_ready = sem("x1T_ready")
        h1_in_psum = sem("h1_in_psum")
        h1_ready = sem("h1_ready")
        h2_in_psum = sem("h2_in_psum")
        h2_ready = sem("h2_ready")
        nodes_out = sem("nodes_out")
        wb_in = sem("wb_in")
        block = ctx.enter_context(nc.Block())

        @block.sync
        def _(sp):
            with sp.Fori(0, STEPS) as i:
                for k in range(TILES):
                    sp.dma_start(acc[:, k, :, :], node_rows(t["acc0"][k], i)).then_inc(nodes_in, 16)
                sp.dma_start(x[:], node_rows(t["x"], i)).then_inc(nodes_in, 16)
                wait_in_loop(sp, c, x1_ready, i + 1)
                sp.dma_start(node_rows(t["x1"], i), x1[:]).then_inc(nodes_out, 16)
                wait_in_loop(sp, c, h2_ready, i + 1)
                sp.dma_start(node_rows(t["h2_wide"], i), h2[:]).then_inc(nodes_out, 16)
                wait_in_loop(sp, c, nodes_out, i * 32 + 32)

        @block.vector
        def _(v):
            st = Steps(step, TILES - 1 + 4 + 2 * LN_STEPS + 3)
            wide = [P, NODE_TILES, H]
            v.memset(c["wb"][:], 0.0).then_inc(wb_in, 1)
            with v.Fori(0, STEPS) as i:
                st.n = 0
                v.wait_ge(nodes_in, i * (16 * (TILES + 1)) + 16 * (TILES + 1))
                st.then(v.tensor_tensor(total[:], acc[:, 0, :, :], acc[:, 1, :, :], ALU.add))
                for k in range(2, TILES):
                    st.wait(v, i)
                    st.then(v.tensor_tensor(total[:], total[:], acc[:, k, :, :], ALU.add))
                st.wait(v, i)
                st.then(v.tensor_scalar(m[:], total[:, :, H], 1e-8, None, ALU.max))
                st.wait(v, i)
                st.then(v.reciprocal(m[:], m[:]))
                st.wait(v, i)
                st.then(v.tensor_tensor(y[:], total[:, :, 0:H], m[:].unsqueeze(2).broadcast_to(wide), ALU.mult))
                st.wait(v, i)
                st.then(v.tensor_tensor(y[:], y[:], x[:], ALU.add))
                st.wait(v, i)
                layer_norm(v, c, st, i, y[:], sq[:], sq[:], m[:], rstd[:], var_ready, root_ready, (0, 2))
                st.then(v.tensor_tensor(y[:], sq[:], c["gamma"][:].unsqueeze(1).broadcast_to(wide), ALU.mult))
                st.wait(v, i)
                st.then(v.tensor_tensor(y[:], y[:], c["beta"][:].unsqueeze(1).broadcast_to(wide), ALU.add))
                st.wait(v, i)
                st.then(v.tensor_tensor(y[:], y[:], x[:], ALU.add))
                st.wait(v, i)
                layer_norm(v, c, st, i, y[:], x1[:], sq[:], m[:], rstd[:], var_ready, root_ready, (1, 2))
                v.sem_inc(x1_ready, 1)
                assert st.n == st.each, (st.n, st.each)
                v.wait_ge(x1T_in_psum, i + 1)
                v.tensor_copy(x1T[:], ps_t[:, 0:NS]).then_inc(x1T_ready, 1)
                v.wait_ge(h2_in_psum, i + 1)
                v.tensor_copy(h2[:], ps_h2[:, :, 0:RELS * H]).then_inc(h2_ready, 1)

        @block.scalar
        def _(act):
            act.wait_ge(wb_in, 1)
            for half in range(2):
                act.dma_start(c["wb"][half * H:(half + 1) * H, :, half * H:(half + 1) * H],
                              t["wb"].rearrange("(q b) i o -> b i q o", b=2)[half]).then_inc(c["wb_done"], 16)
            act.wait_ge(c["wb_done"], 32)
            with act.Fori(0, STEPS) as i:
                for n in range(2):
                    act.wait_ge(var_ready, i * 2 + n + 1)
                    act.activation(rstd[:], m[:], ACT.Sqrt, bias=c["eps"][:], scale=1.0 / H).then_inc(root_ready, 1)
                for q in range(RELS // 2):
                    act.wait_ge(h1_in_psum, i * (RELS // 2) + q + 1)
                    act.activation(h1T[:, q, :], ps_h1[:, q % 2, :], ACT.Relu, bias=c["ba"][:]).then_inc(h1_ready, 1)

        @block.tensor
        def _(pe):
            pe.wait_ge(c["wb_done"], 32)
            with pe.Fori(0, STEPS) as i:
                wait_in_loop(pe, c, x1_ready, i + 1)
                for a in range(NODE_TILES):
                    last = pe.transpose(ps_t[:, a * P:(a + 1) * P], x1[:, a, :], c["ident"][:])
                last.then_inc(x1T_in_psum, 1)
                wait_in_loop(pe, c, x1T_ready, i + 1)
                for q in range(RELS // 2):
                    if q >= 2:
                        wait_in_loop(pe, c, h1_ready, i * (RELS // 2) + q - 1)
                    pe.matmul(ps_h1[:, q % 2, :], c["wa"][:, q * 2 * H:(q + 1) * 2 * H], x1T[:], start=True, stop=True)\
                      .then_inc(h1_in_psum, 1)
                wait_in_loop(pe, c, h1_ready, i * (RELS // 2) + RELS // 2)
                for a in range(NODE_TILES):
                    for q in range(RELS // 2):
                        last = pe.matmul(ps_h2[:, a, q * 2 * H:(q + 1) * 2 * H], h1T[:, q, a * P:(a + 1) * P], c["wb"][:, q, :],
                                         start=True, stop=True)
                last.then_inc(h2_in_psum, 1)


def layer1_nodes(nc, t, c):
    with ExitStack() as ctx:
        def sb(name, shape, dt=F32):
            return ctx.enter_context(nc.sbuf_tensor("n1_" + name, shape, dt))

        def sem(name):
            return ctx.enter_context(nc.semaphore("n1_" + name))

        acc = sb("acc", [P, TILES, NODE_TILES, H])
        x1 = sb("x1", [P, NODE_TILES, H])
        y = sb("y", [P, NODE_TILES, H])
        sq = sb("sq", [P, NODE_TILES, H])
        res = sb("res", [P, NODE_TILES, H])
        m = sb("m", [P, NODE_TILES])
        rstd = sb("rstd", [P, NODE_TILES])
        nodes_in = sem("nodes_in")
        step = sem("n1_step")
        var_ready = sem("var_ready")
        root_ready = sem("root_ready")
        result_ready = sem("result_ready")
        nodes_out = sem("nodes_out")
        block = ctx.enter_context(nc.Block())

        @block.sync
        def _(sp):
            with sp.Fori(0, STEPS) as i:
                for k in range(TILES):
                    sp.dma_start(acc[:, k, :, :], node_rows(t["acc1"][k], i)).then_inc(nodes_in, 16)
                sp.dma_start(x1[:], node_rows(t["x1"], i)).then_inc(nodes_in, 16)
                wait_in_loop(sp, c, result_ready, i + 1)
                sp.dma_start(node_rows(t["out"], i), res[:]).then_inc(nodes_out, 16)
                wait_in_loop(sp, c, nodes_out, i * 16 + 16)

        @block.vector
        def _(v):
            st = Steps(step, TILES - 1 + 3 + LN_STEPS)
            wide = [P, NODE_TILES, H]
            with v.Fori(0, STEPS) as i:
                st.n = 0
                v.wait_ge(nodes_in, i * (16 * (TILES + 1)) + 16 * (TILES + 1))
                st.then(v.tensor_tensor(y[:], acc[:, 0, :, :], acc[:, 1, :, :], ALU.add))
                for k in range(2, TILES):
                    st.wait(v, i)
                    st.then(v.tensor_tensor(y[:], y[:], acc[:, k, :, :], ALU.add))
                st.wait(v, i)
                st.then(v.tensor_tensor(y[:], y[:], c["bias2"][:].unsqueeze(1).broadcast_to(wide), ALU.add))
                st.wait(v, i)
                st.then(v.tensor_scalar(y[:], y[:], 0.0, None, ALU.max))
                st.wait(v, i)
                st.then(v.tensor_tensor(y[:], y[:], x1[:], ALU.add))
                st.wait(v, i)
                layer_norm(v, c, st, i, y[:], res[:], sq[:], m[:], rstd[:], var_ready, root_ready, (0, 1))
                v.sem_inc(result_ready, 1)
                assert st.n == st.each, (st.n, st.each)

        @block.scalar
        def _(act):
            with act.Fori(0, STEPS) as i:
                act.wait_ge(var_ready, i + 1)
                act.activation(rstd[:], m[:], ACT.Sqrt, bias=c["eps"][:], scale=1.0 / H).then_inc(root_ready, 1)


def program(nc, t):
    with ExitStack() as ctx:
        def sb(name, shape, dt=F32):
            return ctx.enter_context(nc.sbuf_tensor(name, shape, dt))

        def dram(name, shape, dt=F32):
            return nc.dram_tensor(name, shape, dt).ap()

        t["tab_dst"] = dram("tab_dst", [NP, DW])
        t["tab_src"] = dram("tab_src", [NP, G])
        t["row"] = dram("row_of_edge", [P, NG, TILES], I32)
        t["acc0"] = [dram(f"acc0_{k}", [NP, MW]) for k in range(TILES)]
        t["acc1"] = [dram(f"acc1_{k}", [NP, H]) for k in range(TILES)]
        t["x1"] = dram("x1_rows", [NP, H])
        t["h2_wide"] = dram("h2_rows", [NP, RELS * H])
        t["h2"] = t["h2_wide"].rearrange("n (r f) -> (n r) f", r=RELS)
        c = {
            "iota_p": sb("iota_p", [P, 1], I32), "iota_row": sb("iota_row", [P, P], I32), "dump": sb("dump", [P, 1], I32),
            "iota_pf": sb("iota_pf", [P, 1]), "iota_rowf": sb("iota_rowf", [P, P]), "dumpf": sb("dumpf", [P, 1]),
            "ones": sb("ones", [P, 1]), "eps": sb("eps", [P, 1]), "before": sb("before", [P, P]), "ident": sb("ident", [P, P]),
            "cw": sb("cw", [P, NG * TILES]), "silu": sb("silu", [64, 2, GE]),
            "w1t": sb("w1t", [R, H]), "b1": sb("b1", [H, 1]), "w2b": sb("w2b", [H + 1, H]),
            "gamma": sb("gamma", [P, H]), "beta": sb("beta", [P, H]), "bias2": sb("bias2", [P, H]),
            "wa": sb("wa", [H, RELS * H]), "ba": sb("ba", [2 * H, 1]), "wb": sb("wb", [2 * H, RELS // 2, 2 * H]),
            "acc0_done": [ctx.enter_context(nc.semaphore(f"acc0_done{k}")) for k in range(TILES)],
            "acc1_done": [ctx.enter_context(nc.semaphore(f"acc1_done{k}")) for k in range(TILES)],
            "waits_passed": ctx.enter_context(nc.semaphore("waits_passed")),
            "wb_done": ctx.enter_context(nc.semaphore("wb_done")),
        }
        prepare(nc, t, c)
        layer0_edges(nc, t, c)
        layer0_nodes(nc, t, c)
        layer1_edges(nc, t, c)
        layer1_nodes(nc, t, c)


def kernel(x, src, dst, edge_attr_40, edge_type_8, edge_weight, edge_weight1, node_type_119, node_vec,
           L0_gnn_W1, L0_gnn_b1, L0_gnn_W2, L0_gnn_b2, L0_gnn_emb, L0_gnn_adaptW, L0_gnn_gamma, L0_gnn_beta,
           L1_gnn_weight1, L1_gnn_weight2, L1_gnn_bias1, L1_gnn_bias2):
    import numpy as np
    import concourse.bacc as bacc
    from concourse.bass_utils import run_bass_kernel_spmd as run

    def edges(a, fill):
        flat = np.full(NG * GE, fill, a.dtype)
        flat[:E] = a.reshape(E)
        return np.ascontiguousarray(flat.reshape(NG, TILES, P).transpose(2, 0, 1)), flat

    def nodes(a):
        rows = np.zeros((NP, *a.shape[1:]), a.dtype)
        rows[:N] = a
        return rows

    src_cols, src_flat = edges(np.asarray(src), PAD_NODE)
    dst_cols, dst_flat = edges(np.asarray(dst), PAD_NODE)
    attr = np.zeros((R, NG * GE), np.float32)
    attr[:, :E] = np.asarray(edge_attr_40).T
    wa = np.asarray(L1_gnn_weight1)
    arrays = {
        "src": src_cols, "dst": dst_cols, "src_flat": src_flat, "dst_flat": dst_flat,
        "rel": edges(np.asarray(edge_type_8), 0)[0], "dist": edges(np.asarray(edge_weight), 0)[0],
        "norm": edges(np.asarray(edge_weight1), 0)[0], "attr": attr,
        "x": nodes(np.asarray(x)), "z": nodes(np.asarray(node_type_119)), 
        "x_mult": nodes(np.concatenate([np.asarray(x), np.asarray(node_vec)[:, None]], 1)),
        "w1t": np.asarray(L0_gnn_W1).T, "b1": np.asarray(L0_gnn_b1)[:, None], "w2t": np.asarray(L0_gnn_W2).T,
        "b2": np.asarray(L0_gnn_b2)[None, :], "emb": np.asarray(L0_gnn_emb), "embT": np.asarray(L0_gnn_emb).T,
        "adaptT": np.asarray(L0_gnn_adaptW).T, "gamma": np.asarray(L0_gnn_gamma), "beta": np.asarray(L0_gnn_beta),
        "bias2": np.asarray(L1_gnn_bias2), "ba": np.tile(np.asarray(L1_gnn_bias1), 2)[:, None],
        "wa": wa.transpose(1, 0, 2).reshape(H, RELS * H), "wb": np.asarray(L1_gnn_weight2),
    }
    arrays = {name: np.ascontiguousarray(a) for name, a in arrays.items()}
    nc = bacc.Bacc("TRN2", target_bir_lowering=False, num_devices=1)
    t = {name: nc.dram_tensor(f"in_{name}", a.shape, mybir.dt.from_np(a.dtype), kind="ExternalInput").ap()
         for name, a in arrays.items()}
    t["out"] = nc.dram_tensor("result", (NP, H), F32, kind="ExternalOutput").ap()
    program(nc, t)
    r = run(nc, [{f"in_{name}": a for name, a in arrays.items()}], core_ids=[0])
    return r.results[0]["result"][:N]
```

```python
from contextlib import ExitStack

import concourse.bass as bass
from concourse import mybir

F32 = mybir.dt.float32
I32 = mybir.dt.int32
I16 = mybir.dt.int16
U8 = mybir.dt.uint8
BF16 = mybir.dt.bfloat16
ALU = mybir.AluOpType
ACT = mybir.ActivationFunctionType
AX = mybir.AxisListType

P = 128
N, H, E, R, Z, G, RELS = 12500, 48, 412500, 40, 119, 32, 8
TILES = 8
GE = TILES * P
NG = 4 * -(-E // (4 * GE))
NODE_TILES = 4
NS = NODE_TILES * P
STEPS = 2 * -(-(N + P) // (2 * NS))
NP = STEPS * NS
PAD_NODE = N
DUMP = NP - P
DW = H + 1 + G
PARTS = 3
WW = PARTS * DW
FG = 4
FP = NG // FG
LOW = 128
HIGH = NP // LOW
BLOCKS = NP // P
MW = H + 1
PI = 3.141592653589793
CUTOFF = 6.0
EPS = 1e-5


def wait_in_loop(eng, c, sem, value):
    eng.wait_ge(sem, value)
    eng.sem_inc(c["waits_passed"], 1)


def ways(eng, c, body):
    windowed = eng.value_load(c["sorted"][0:1, 0:1], min_val=0, max_val=1)
    with eng.If(windowed == 1):
        body(True)
    with eng.Else():
        body(False)


def split(v, step, n, whole, rest, parts):
    v.tensor_copy(parts[0], whole).then_inc(step, 1)
    v.wait_ge(step, n + 1)
    v.tensor_tensor(rest, whole, parts[0], ALU.subtract).then_inc(step, 1)
    v.wait_ge(step, n + 2)
    v.tensor_copy(parts[1], rest).then_inc(step, 1)
    v.wait_ge(step, n + 3)
    v.tensor_tensor(whole, rest, parts[1], ALU.subtract).then_inc(step, 1)
    v.wait_ge(step, n + 4)
    v.tensor_copy(parts[2], whole).then_inc(step, 1)


def prepare_edges(nc, t, c):
    with ExitStack() as ctx:
        def sb(name, shape, dt=F32):
            return ctx.enter_context(nc.sbuf_tensor("pe_" + name, shape, dt))

        def sem(name):
            return ctx.enter_context(nc.semaphore("pe_" + name))

        COLS = [P, NG, TILES]
        ROWS = [FP, FG, GE]
        zeros = sb("zeros", [P, NP // (2 * P) * MW])
        dist = sb("dist", COLS)
        inside = sb("inside", COLS)
        col_i = [sb(f"col_i{n}", COLS, I32) for n in range(2)]
        pack0 = sb("pack0", [P, NG, 2, TILES])
        row_i = [sb(f"row_i{n}", ROWS, I32) for n in range(2)]
        ids16 = sb("ids16", [FP, FG, 2, GE], I16)
        ids8 = sb("ids8", [FP, FG, 2, GE], U8)
        half_pi = sb("half_pi", [P, 1])
        top = sb("top", [FP, FG])
        low = sb("low", [FP, FG])
        first = sb("first", [FP, FG])
        worst = sb("worst", [FP, 1])
        base_f = sb("base_f", [1, NG])
        base_i = sb("base_i", [P, NG], I32)
        offset_i = sb("offset_i", [P, NG], I32)
        ps_base = ctx.enter_context(nc.psum_tensor("pe_ps_base", [P, 512], F32))
        ps_bad = ctx.enter_context(nc.psum_tensor("pe_ps_bad", [1, 512], F32))
        consts_in = sem("consts_in")
        src_in = sem("src_in")
        dst_in = sem("dst_in")
        dist_in = sem("dist_in")
        cols_in = sem("cols_in")
        norm_in = sem("norm_in")
        out = sem("out")
        iotas = sem("iotas")
        zeroed = sem("zeroed")
        dve = sem("dve")
        dist_clamped = sem("dist_clamped")
        cosine = sem("cosine")
        ids_ready = sem("ids_ready")
        pack0_ready = sem("pack0_ready")
        pack0_out = sem("pack0_out")
        pack1_ready = sem("pack1_ready")
        row_ready = sem("row_ready")
        worst_ready = sem("worst_ready")
        bad_ready = sem("bad_ready")
        base_ready = sem("base_ready")
        base_all = sem("base_all")
        block = ctx.enter_context(nc.Block())

        def rows(flat):
            return flat.rearrange("(q a e) -> q a e", q=FP, a=FG)

        @block.sync
        def _(sp):
            sp.dma_start(row_i[0][:], rows(t["dst_flat"])).then_inc(dst_in, 16)
            sp.dma_start(row_i[1][:], rows(t["src_flat"])).then_inc(src_in, 16)
            sp.dma_start(dist[:], t["dist"]).then_inc(dist_in, 16)
            sp.dma_start(col_i[0][:], t["src"]).then_inc(cols_in, 16)
            sp.dma_start(col_i[1][:], t["rel"]).then_inc(cols_in, 16)
            for dst, src in ((c["w1t"][:], t["w1t"]), (c["b1"][:], t["b1"]), (c["w2b"][0:H, :], t["w2t"]),
                             (c["w2b"][H:H + 1, :], t["b2"]), (c["gamma"][:], t["gamma"].partition_broadcast(P)),
                             (c["beta"][:], t["beta"].partition_broadcast(P)),
                             (c["bias2"][:], t["bias2"].partition_broadcast(P)), (c["wa"][:], t["wa"]),
                             (c["ba"][:], t["ba"])):
                sp.dma_start(dst, src).then_inc(consts_in, 16)
            sp.wait_ge(ids_ready, 1)
            sp.dma_start(t["ids16"].rearrange("(q a) r e -> q a r e", a=FG), ids16[:]).then_inc(out, 16)
            sp.dma_start(t["ids8"].rearrange("(q a) r e -> q a r e", a=FG), ids8[:]).then_inc(out, 16)
            sp.wait_ge(row_ready, 1)
            sp.dma_start(t["row"], col_i[1][:]).then_inc(out, 16)
            sp.wait_ge(pack0_ready, 1)
            sp.dma_start(t["pack0"], pack0[:]).then_inc(pack0_out, 16)
            sp.wait_ge(pack0_out, 16)
            sp.dma_start(col_i[0][:], t["dst"]).then_inc(norm_in, 16)
            sp.dma_start(pack0[:, :, 1, :], t["norm"]).then_inc(norm_in, 16)
            sp.wait_ge(pack1_ready, 1)
            sp.dma_start(t["pack1"], pack0[:]).then_inc(out, 16)
            sp.wait_ge(out, 64)
            sp.wait_ge(consts_in, 16 * 9)

        @block.gpsimd
        def _(pool):
            nc.gpsimd.iota(c["iota_p"][:], pattern=[[0, 1]], base=0, channel_multiplier=1).then_inc(iotas, 1)
            nc.gpsimd.iota(c["iota_row"][:], pattern=[[1, P]], base=0, channel_multiplier=0).then_inc(iotas, 1)
            nc.gpsimd.iota(c["dump"][:], pattern=[[0, 1]], base=DUMP, channel_multiplier=1).then_inc(iotas, 1)
            pool.wait_ge(zeroed, 1)
            for k in range(TILES):
                for half in range(2):
                    pool.dma_start(t["acc0"][k].rearrange("(b p a) f -> b p (a f)", b=2, p=P)[half],
                                   zeros[:]).then_inc(c["acc0_done"][k], 16)
            for k in range(TILES):
                pool.wait_ge(c["acc0_done"][k], 32)

        @block.vector
        def _(v):
            v.memset(zeros[:], 0.0).then_inc(zeroed, 1)
            v.memset(half_pi[:], PI / 2).then_inc(dve, 1)
            v.memset(c["ones"][:], 1.0).then_inc(dve, 1)
            v.memset(c["ones_bf"][:], 1.0).then_inc(dve, 1)
            v.memset(c["eps"][:], EPS).then_inc(dve, 1)
            v.memset(c["silu"][:], 1.0).then_inc(dve, 1)
            v.wait_ge(iotas, 3)
            v.tensor_copy(c["iota_pf"][:], c["iota_p"][:]).then_inc(dve, 1)
            v.tensor_copy(c["iota_rowf"][:], c["iota_row"][:]).then_inc(dve, 1)
            v.tensor_copy(c["dumpf"][:], c["dump"][:]).then_inc(dve, 1)
            v.wait_ge(dve, 8)
            v.tensor_scalar(c["after"][:], c["iota_rowf"][:], c["iota_pf"][:], None, ALU.is_gt).then_inc(dve, 1)
            v.tensor_scalar(c["earlier_mask"][:], c["iota_rowf"][:], c["iota_pf"][:], None, ALU.is_lt)
            v.tensor_scalar(c["ident"][:], c["iota_rowf"][:], c["iota_pf"][:], None, ALU.is_equal).then_inc(dve, 1)
            v.wait_ge(dist_in, 16)
            v.tensor_scalar(inside[:], dist[:], CUTOFF, None, ALU.is_lt).then_inc(dve, 1)
            v.scalar_tensor_tensor(dist[:].rearrange("p g k -> p (g k)"), dist[:].rearrange("p g k -> p (g k)"), -1.0,
                                   dist[:].rearrange("p g k -> p (g k)"), ALU.mult, ALU.max).then_inc(dve, 1)
            v.wait_ge(dve, 12)
            v.tensor_scalar(dist[:], dist[:], CUTOFF, None, ALU.min).then_inc(dist_clamped, 1)
            v.wait_ge(dst_in, 16)
            v.tensor_reduce(top[:], row_i[0][:], AX.X, ALU.max).then_inc(dve, 1)
            v.tensor_reduce(low[:], row_i[0][:], AX.X, ALU.min).then_inc(dve, 1)
            v.tensor_copy(first[:], row_i[0][:, :, 0]).then_inc(dve, 1)
            v.tensor_copy(ids16[:, :, 1, :], row_i[0][:]).then_inc(dve, 1)
            v.wait_ge(dve, 15)
            v.scalar_tensor_tensor(top[:], top[:], float(1 - P), first[:], ALU.add, ALU.subtract).then_inc(dve, 1)
            v.tensor_tensor(low[:], first[:], low[:], ALU.subtract).then_inc(dve, 1)
            v.wait_ge(dve, 18)
            v.tensor_tensor(top[:], top[:], low[:], ALU.max).then_inc(dve, 1)
            v.wait_ge(dve, 19)
            v.tensor_reduce(worst[:], top[:], AX.X, ALU.max).then_inc(dve, 1)
            v.wait_ge(dve, 20)
            v.tensor_scalar(worst[:], worst[:], 0.0, None, ALU.is_gt).then_inc(worst_ready, 1)
            v.wait_ge(src_in, 16)
            v.tensor_copy(ids16[:, :, 0, :], row_i[1][:]).then_inc(dve, 1)
            v.tensor_scalar(row_i[0][:], row_i[1][:], 7, None, ALU.arith_shift_right).then_inc(dve, 1)
            v.wait_ge(dve, 22)
            v.tensor_copy(ids8[:, :, 0, :], row_i[0][:]).then_inc(dve, 1)
            v.wait_ge(dve, 23)
            v.tensor_scalar(row_i[0][:], row_i[1][:], LOW - 1, None, ALU.bitwise_and).then_inc(dve, 1)
            v.wait_ge(dve, 24)
            v.tensor_copy(ids8[:, :, 1, :], row_i[0][:]).then_inc(ids_ready, 1)
            v.wait_ge(cols_in, 32)
            v.tensor_copy(pack0[:, :, 0, :], col_i[0][:]).then_inc(dve, 1)
            v.scalar_tensor_tensor(col_i[1][:].rearrange("p g k -> p (g k)"), col_i[0][:].rearrange("p g k -> p (g k)"),
                                   float(RELS), col_i[1][:].rearrange("p g k -> p (g k)"), ALU.mult, ALU.add)\
             .then_inc(row_ready, 1)
            v.wait_ge(cosine, 1)
            v.tensor_scalar(dist[:], dist[:], 1.0, 0.5, ALU.add, ALU.mult).then_inc(dve, 1)
            v.wait_ge(dve, 26)
            v.tensor_tensor(pack0[:, :, 1, :], dist[:], inside[:], ALU.mult).then_inc(pack0_ready, 1)
            v.wait_ge(bad_ready, 1)
            v.tensor_scalar(c["sorted"][:], ps_bad[0:1, 0:1], 0.0, None, ALU.is_equal).then_inc(dve, 1)
            v.wait_ge(norm_in, 32)
            v.tensor_copy(base_f[:], col_i[0][0:1, :, 0]).then_inc(base_ready, 1)
            v.wait_ge(base_ready, 1)
            v.tensor_scalar(col_i[0][:], col_i[0][:], P - 1, None, ALU.bitwise_and).then_inc(dve, 1)
            v.wait_ge(dve, 28)
            v.tensor_copy(pack0[:, :, 0, :], col_i[0][:]).then_inc(pack1_ready, 1)
            v.wait_ge(base_all, 1)
            v.tensor_copy(base_i[:], ps_base[:, 0:NG]).then_inc(dve, 1)
            v.wait_ge(dve, 29)
            v.tensor_scalar(c["block"][:], base_i[0:1, :], 7, None, ALU.arith_shift_right).then_inc(dve, 1)
            v.tensor_scalar(offset_i[:], base_i[:], P - 1, None, ALU.bitwise_and).then_inc(dve, 1)
            v.wait_ge(dve, 31)
            v.tensor_scalar(c["in_first"][:], offset_i[:], c["iota_pf"][:], None, ALU.is_le).then_inc(dve, 1)
            v.tensor_scalar(c["in_next"][:], offset_i[:], c["iota_pf"][:], None, ALU.is_gt).then_inc(dve, 1)
            v.wait_ge(dve, 33)

        @block.scalar
        def _(act):
            act.wait_ge(dve, 1)
            act.wait_ge(dist_clamped, 1)
            act.activation(dist[:], dist[:], ACT.Sin, bias=half_pi[:], scale=-PI / CUTOFF).then_inc(cosine, 1)

        @block.tensor
        def _(pe):
            pe.wait_ge(worst_ready, 1)
            pe.matmul(ps_bad[0:1, 0:1], worst[:], c["ones"][0:FP, 0:1], start=True, stop=True).then_inc(bad_ready, 1)
            pe.wait_ge(base_ready, 1)
            pe.matmul(ps_base[:, 0:NG], c["ones"][0:1, :], base_f[:], start=True, stop=True).then_inc(base_all, 1)


def prepare_nodes(nc, t, c):
    with ExitStack() as ctx:
        def sb(name, shape, dt=F32):
            return ctx.enter_context(nc.sbuf_tensor("pn_" + name, shape, dt))

        def sem(name):
            return ctx.enter_context(nc.semaphore("pn_" + name))

        emb = sb("emb", [Z, G])
        rest_e = sb("rest_e", [Z, G])
        embT = sb("embT", [G, Z])
        adaptT = sb("adaptT", [G, G])
        adapted = sb("adapted", [Z, G])
        z_hl = sb("z_hl", [HIGH, LOW], I32)
        zrow = sb("zrow", [P, 2, NS], I32)
        onehot = sb("onehot", [P, 2, NS])
        row = sb("row", [P, 2, NODE_TILES, DW])
        rest = sb("rest", [P, NODE_TILES, DW])
        parts = sb("parts", [P, 2, NODE_TILES, PARTS, DW], BF16)
        ps_emb = ctx.enter_context(nc.psum_tensor("pn_ps_emb", [P, 512], F32))
        ps_ej = ctx.enter_context(nc.psum_tensor("pn_ps_ej", [P, 2, NODE_TILES, 512 // NODE_TILES], F32))
        emb_in = sem("emb_in")
        adapted_in_psum = sem("adapted_in_psum")
        adapted_ready = sem("adapted_ready")
        step = sem("step")
        nodes_in = [sem(f"nodes_in{s}") for s in range(2)]
        onehot_ready = sem("onehot_ready")
        looked_up = sem("looked_up")
        parts_ready = sem("parts_ready")
        parts_out = [sem(f"parts_out{s}") for s in range(2)]
        block = ctx.enter_context(nc.Block())

        def load(sp, n, s):
            sp.dma_start(zrow[:, s, :], t["z"][bass.DynSlice(n * NS, NS)].partition_broadcast(P)).then_inc(nodes_in[s], 16)
            sp.dma_start(row[:, s, :, 0:MW], node_rows(t["x_mult"], n)).then_inc(nodes_in[s], 16)

        def store(sp, i, s):
            wait_in_loop(sp, c, parts_ready, i * 2 + s + 1)
            sp.dma_start(t["window_rows"][bass.DynSlice((i * 2 + s) * NS, NS), :].rearrange("(a p) f -> p a f", p=P),
                         parts[:, s, :, :, :].rearrange("p a r f -> p a (r f)")).then_inc(parts_out[s], 16)

        @block.sync
        def _(sp):
            for dst, src in ((embT[:], t["embT"]), (adaptT[:], t["adaptT"]), (emb[:], t["emb"]),
                             (z_hl[:], t["z"].rearrange("(h l) -> h l", l=LOW))):
                sp.dma_start(dst, src).then_inc(emb_in, 16)
            load(sp, 0, 0)
            load(sp, 1, 1)
            with sp.Fori(0, STEPS // 2 - 1) as i:
                for s in range(2):
                    store(sp, i, s)
                    wait_in_loop(sp, c, parts_out[s], i * 16 + 16)
                    load(sp, i * 2 + s + 2, s)
            for s in range(2):
                store(sp, STEPS // 2 - 1, s)
            for s in range(2):
                sp.wait_ge(parts_out[s], STEPS // 2 * 16)

        @block.vector
        def _(v):
            v.wait_ge(emb_in, 64)
            v.tensor_copy(c["z_table"][:], z_hl[:])
            split(v, step, 0, emb[:], rest_e[:], [c["emb_parts"][:, n, :] for n in range(PARTS)])
            v.wait_ge(adapted_in_psum, 1)
            v.tensor_copy(adapted[:], ps_emb[0:Z, 0:G]).then_inc(adapted_ready, 1)
            with v.Fori(0, STEPS // 2) as i:
                for s in range(2):
                    n = i * 2 + s
                    v.wait_ge(nodes_in[s], i * 32 + 32)
                    v.wait_ge(step, n * 6 + 5)
                    v.tensor_scalar(onehot[:, s, :], zrow[:, s, :], c["iota_pf"][:], None, ALU.is_equal).then_inc(onehot_ready, 1)
                    v.wait_ge(looked_up, n + 1)
                    v.tensor_copy(row[:, s, :, MW:DW], ps_ej[:, s, :, 0:G]).then_inc(step, 1)
                    v.wait_ge(step, n * 6 + 6)
                    split(v, step, n * 6 + 6, row[:, s, :, :], rest[:], [parts[:, s, :, m, :] for m in range(PARTS)])
                    v.wait_ge(step, n * 6 + 11)
                    v.sem_inc(parts_ready, 1)

        @block.tensor
        def _(pe):
            pe.wait_ge(emb_in, 64)
            pe.matmul(ps_emb[0:Z, 0:G], embT[:], adaptT[:], start=True, stop=True).then_inc(adapted_in_psum, 1)
            pe.wait_ge(adapted_ready, 1)
            with pe.Fori(0, STEPS // 2) as i:
                for s in range(2):
                    wait_in_loop(pe, c, onehot_ready, i * 2 + s + 1)
                    for a in range(NODE_TILES):
                        last = pe.matmul(ps_ej[:, s, a, 0:G], onehot[0:Z, s, a * P:(a + 1) * P], adapted[:],
                                         start=True, stop=True)
                    last.then_inc(looked_up, 1)


def one_of_equals(v, c, step, base, key_col, key_row, same, earlier, count, dump_off, index):
    v.tensor_tensor(same, key_row.rearrange("p (t j) -> p t j", t=TILES),
                    key_col.unsqueeze(2).broadcast_to([P, TILES, P]), ALU.is_equal).then_inc(step, 1)
    v.tensor_tensor(dump_off, c["dumpf"][:].broadcast_to([P, TILES]), key_col, ALU.subtract).then_inc(step, 1)
    v.wait_ge(step, base + 1)
    v.tensor_tensor(earlier, same, c["earlier_mask"][:].unsqueeze(1).broadcast_to([P, TILES, P]), ALU.mult).then_inc(step, 1)
    v.wait_ge(step, base + 3)
    v.tensor_reduce(count, earlier, AX.X, ALU.add).then_inc(step, 1)
    v.wait_ge(step, base + 4)
    v.scalar_tensor_tensor(dump_off, count, 0.0, dump_off, ALU.is_gt, ALU.mult).then_inc(step, 1)
    v.wait_ge(step, base + 5)
    return v.tensor_tensor(index, key_col, dump_off, ALU.add)


def layer0_edges(nc, t, c):
    with ExitStack() as ctx:
        def sb(name, shape, dt=F32):
            return ctx.enter_context(nc.sbuf_tensor("e0_" + name, shape, dt))

        def sem(name):
            return ctx.enter_context(nc.semaphore("e0_" + name))

        def ps(name, shape):
            return ctx.enter_context(nc.psum_tensor("e0_" + name, shape, F32))

        HALF = TILES // 2
        attr = sb("attr", [R, 2, GE])
        ids16 = sb("ids16", [P, 2, 2, GE], I16)
        ids8 = sb("ids8", [P, 2, 2, GE], U8)
        src_early = sb("src_early", [P, 2, TILES])
        pack = sb("pack", [P, 2, 2, TILES])
        window = sb("window", [P, 2, WW], BF16)
        dst_col = [sb(f"dst_col{s}", [P, TILES], I32) for s in range(2)]
        raw = sb("raw", [P, 2, TILES, WW], BF16)
        node_of = sb("node_of", [P, 1])
        in_window = sb("in_window", [P, 2, GE], BF16)
        is_high = sb("is_high", [P, GE], BF16)
        z_masked = sb("z_masked", [P, GE], BF16)
        is_type = sb("is_type", [Z, GE], BF16)
        same = sb("same", [P, 2, TILES, P], BF16)
        same_f = sb("same_f", [P, 2, TILES, P])
        before = sb("before", [P, 2, TILES, P], BF16)
        of_dst = sb("of_dst", [P, 2, TILES, DW])
        emb_prod = sb("emb_prod", [P, TILES, G])
        adapt = sb("adapt", [P, TILES])
        weight = sb("weight", [P, TILES])
        gated = sb("gated", [P, TILES, H])
        msg = sb("msg", [P, 2, TILES, MW])
        dump_off = sb("dump_off", [P, TILES])
        index_f = sb("index_f", [P, 2, TILES])
        index = [sb(f"index{s}", [P, TILES], I32) for s in range(2)]
        summed = sb("summed", [P, 2, TILES, MW])
        ps_pre = ps("ps_pre", [H, 512])
        ps_gate = ps("ps_gate", [P, 512])
        ps_z = ps("ps_z", [P, GE])
        ps_row = ps("ps_row", [P, 2, 512])
        ps_emb = ps("ps_emb", [P, TILES * G])
        ps_sum = ps("ps_sum", [P, 512])
        ps_count = ps_gate[:, TILES * H:TILES * (H + 1)]

        ids_in = [sem(f"ids_in{s}") for s in range(2)]
        attr_in = [sem(f"attr_in{s}") for s in range(2)]
        pack_in = [sem(f"pack_in{s}") for s in range(2)]
        ids_free = sem("ids_free")
        attr_free = sem("attr_free")
        pack_free = sem("pack_free")
        gathered = [sem(f"gathered{s}") for s in range(2)]
        high_ready = sem("high_ready")
        z_rows = sem("z_rows")
        z_masked_ready = sem("z_masked_ready")
        z_spread = sem("z_spread")
        type_ready = sem("type_ready")
        same_ready = sem("same_ready")
        before_ready = sem("before_ready")
        window_ready = sem("window_ready")
        pre_ready = sem("pre_ready")
        silu_ready = sem("silu_ready")
        gate_ready = sem("gate_ready")
        gate_used = sem("gate_used")
        same_f_ready = sem("same_f_ready")
        rows_in_psum = sem("rows_in_psum")
        of_dst_ready = sem("of_dst_ready")
        emb_ready = sem("emb_ready")
        emb_used = sem("emb_used")
        msg_ready = sem("msg_ready")
        sum_ready = sem("sum_ready")
        summed_ready = sem("summed_ready")
        step = sem("step")
        block = ctx.enter_context(nc.Block())
        acc_done = c["acc0_done"]

        def wide(x, n):
            return x.unsqueeze(2).broadcast_to([P, TILES, n])

        def load(sp, i, s, windowed):
            g = i * 2 + s
            wait_in_loop(sp, c, ids_free, g + 1)
            sp.dma_start(ids8[:, s, :, :].rearrange("p r e -> p (r e)"),
                         t["ids8"][bass.DynSlice(g, 1), :, :].rearrange("g r e -> (g r e)").partition_broadcast(P)).then_inc(ids_in[s], 16)
            sp.dma_start(ids16[:, s, :, :].rearrange("p r e -> p (r e)"),
                         t["ids16"][bass.DynSlice(g, 1), :, :].rearrange("g r e -> (g r e)").partition_broadcast(P)).then_inc(ids_in[s], 16)
            sp.dma_start(src_early[:, s, :], t["pack0"][:, bass.DynSlice(g, 1), 0, :].rearrange("p g k -> p (g k)")).then_inc(ids_in[s], 16)
            wait_in_loop(sp, c, attr_free, g + 1)
            sp.dma_start(attr[:, s, :], t["attr"][:, bass.DynSlice(g * GE, GE)]).then_inc(attr_in[s], 16)
            if windowed:
                start = sp.value_load(t["dst_flat"][bass.DynSlice(g * GE, 1)].unsqueeze(0), min_val=0, max_val=PAD_NODE)
                sp.dma_start(window[:, s, :], t["window_rows"][bass.DynSlice(start, P), :]).then_inc(attr_in[s], 16)
            wait_in_loop(sp, c, pack_free, g + 1)
            sp.dma_start(pack[:, s, :, :], t["pack0"][:, bass.DynSlice(g, 1), :, :].rearrange("p g r k -> p (g r) k")).then_inc(pack_in[s], 16)
            if not windowed:
                sp.dma_start(dst_col[s][:], t["dst"][:, bass.DynSlice(g, 1), :].rearrange("p g k -> p (g k)")).then_inc(pack_in[s], 16)

        def loads(sp, windowed):
            with sp.Fori(0, NG // 2) as i:
                for s in range(2):
                    load(sp, i, s, windowed)

        def scatters_of_all(pool, windowed):
            def gathers(i, s):
                wait_in_loop(pool, c, pack_in[s], i * 32 + 32)
                for k in range(TILES):
                    nc.gpsimd.indirect_dma_start(raw[:, s, k, :], None, t["window_rows"],
                                                 bass.IndirectOffsetOnAxis(ap=dst_col[s][:, k:k + 1], axis=0)).then_inc(gathered[s], 16)

            def scatters(i, s):
                wait_in_loop(pool, c, summed_ready, i * 2 + s + 1)
                for k in range(TILES):
                    wait_in_loop(pool, c, acc_done[k], (i * 2 + s) * 16 + 32)
                    nc.gpsimd.indirect_dma_start(t["acc0"][k], bass.IndirectOffsetOnAxis(ap=index[s][:, k:k + 1], axis=0),
                                                 summed[:, s, k, :], None, compute_op=ALU.add).then_inc(acc_done[k], 16)

            if windowed:
                with pool.Fori(0, NG // 2) as i:
                    scatters(i, 0)
                    scatters(i, 1)
            else:
                gathers(0, 0)
                with pool.Fori(0, NG // 2 - 1) as i:
                    gathers(i, 1)
                    scatters(i, 0)
                    gathers(i + 1, 0)
                    scatters(i, 1)
                gathers(NG // 2 - 1, 1)
                scatters(NG // 2 - 1, 0)
                scatters(NG // 2 - 1, 1)
            for k in range(TILES):
                pool.wait_ge(acc_done[k], NG * 16 + 32)


        def turns(eng, turn):
            turn(0, 0, 0, True)
            turn(1, 1, 0, False)
            with eng.Fori(1, NG // 2) as i:
                turn(i * 2, 0, i, False)
                turn(i * 2 + 1, 1, i, False)

        def act_all(act, windowed):
            def silu(g, s, half):
                act.wait_ge(pre_ready, g * 2 + half + 1)
                act.activation(c["silu"][0:H, s, half * 512:(half + 1) * 512], ps_pre[:], ACT.Silu,
                               bias=c["b1"][:]).then_inc(silu_ready, 1)

            def take_sum(g, s):
                act.wait_ge(sum_ready, g + 1)
                for k in range(TILES):
                    act.wait_ge(acc_done[k], g * 16 + 16)
                act.activation(index[s][:], index_f[:, s, :], ACT.Copy)
                act.activation(summed[:, s, :, :], ps_sum[:, 0:TILES * MW].rearrange("p (t f) -> p t f", t=TILES),
                               ACT.Copy).then_inc(summed_ready, 1)

            def turn(g, s, i, first):
                silu(g, s, 0)
                if not isinstance(g, int) or g >= 2:
                    take_sum(g - 2, s)
                act.wait_ge(same_ready, g + 1)
                act.activation(same_f[:, s, :, :], same[:, s, :, :], ACT.Copy).then_inc(same_f_ready, 1)
                if windowed:
                    act.wait_ge(rows_in_psum, g + 1)
                    act.activation(of_dst[:, s, :, :].rearrange("p (b t) f -> p b t f", b=2),
                                   ps_row[:, :, 0:HALF * DW].rearrange("p b (t f) -> p b t f", t=HALF), ACT.Copy).then_inc(of_dst_ready, 1)
                silu(g, s, 1)

            turns(act, turn)
            take_sum(NG - 2, 0)
            take_sum(NG - 1, 1)

        def pe_all(pe, windowed):
            def pre(g, s, half, first):
                if not (first and half == 0):
                    wait_in_loop(pe, c, silu_ready, g * 2 + half)
                pe.matmul(ps_pre[:], c["w1t"][:], attr[:, s, half * 512:(half + 1) * 512], start=True, stop=True)\
                  .then_inc(pre_ready, 1)

            def emb_of_src(g, s, first):
                wait_in_loop(pe, c, type_ready, g + 1)
                if not first:
                    wait_in_loop(pe, c, emb_used, g)
                for k in range(TILES):
                    for n in range(PARTS):
                        last = pe.matmul(ps_emb[:, k * G:(k + 1) * G], is_type[:, k * P:(k + 1) * P], c["emb_parts"][:, n, :],
                                         start=(n == 0), stop=(n == PARTS - 1))
                last.then_inc(emb_ready, 1)

            def sums(g, s):
                wait_in_loop(pe, c, msg_ready, g + 1)
                wait_in_loop(pe, c, same_f_ready, g + 1)
                if not (isinstance(g, int) and g == 0):
                    wait_in_loop(pe, c, summed_ready, g)
                for k in range(TILES):
                    last = pe.matmul(ps_sum[:, k * MW:(k + 1) * MW], same_f[:, s, k, :], msg[:, s, k, :], start=True, stop=True)
                last.then_inc(sum_ready, 1)

            def turn(g, s, i, first):
                wait_in_loop(pe, c, high_ready, g + 1)
                if not first:
                    wait_in_loop(pe, c, type_ready, g)
                for b in range(2):
                    last = pe.matmul(ps_z[:, b * 512:(b + 1) * 512], c["z_table"][:], is_high[0:HIGH, b * 512:(b + 1) * 512],
                                     start=True, stop=True)
                last.then_inc(z_rows, 1)
                if not first:
                    emb_of_src(g - 1, 1 - s, isinstance(g, int) and g == 1)
                wait_in_loop(pe, c, attr_in[s], i * (32 if windowed else 16) + (32 if windowed else 16))
                pre(g, s, 0, first)
                wait_in_loop(pe, c, z_masked_ready, g + 1)
                for b in range(2):
                    last = pe.matmul(ps_z[0:Z, b * 512:(b + 1) * 512], c["ones_bf"][:, 0:Z], z_masked[:, b * 512:(b + 1) * 512],
                                     start=True, stop=True)
                last.then_inc(z_spread, 1)
                if not isinstance(g, int) or g >= 2:
                    sums(g - 2, s)
                if windowed:
                    wait_in_loop(pe, c, window_ready, g + 1)
                    if not first:
                        wait_in_loop(pe, c, of_dst_ready, g)
                    for k in range(TILES):
                        for n in range(PARTS):
                            last = pe.matmul(ps_row[:, k // HALF, k % HALF * DW:(k % HALF + 1) * DW], in_window[:, s, k * P:(k + 1) * P],
                                             window[:, s, n * DW:(n + 1) * DW], start=(n == 0), stop=(n == PARTS - 1))
                    last.then_inc(rows_in_psum, 1)
                pre(g, s, 1, False)
                wait_in_loop(pe, c, silu_ready, g * 2 + 2)
                if not first:
                    wait_in_loop(pe, c, gate_used, g)
                for k in range(TILES):
                    last = pe.matmul(ps_gate[:, k * H:(k + 1) * H], c["silu"][0:H + 1, s, k * P:(k + 1) * P], c["w2b"][:],
                                     start=True, stop=True)
                wait_in_loop(pe, c, before_ready, g + 1)
                for k in range(TILES):
                    last = pe.matmul(ps_count[:, k:k + 1], before[:, s, k, :], c["ones_bf"][:, 0:1], start=True, stop=True)
                last.then_inc(gate_ready, 1)
                wait_in_loop(pe, c, gate_ready, g + 1)
                pe.sem_inc(attr_free, 1)

            pe.sem_inc(attr_free, 2)
            turns(pe, turn)
            emb_of_src(NG - 1, 1, False)
            sums(NG - 2, 0)
            sums(NG - 1, 1)

        def vector_all(v, windowed):
            def embeddings(g, s):
                if windowed:
                    v.wait_ge(of_dst_ready, g + 1)
                else:
                    v.tensor_tensor(of_dst[:, s, :, :], raw[:, s, :, 0:DW], raw[:, s, :, DW:2 * DW], ALU.add).then_inc(c["gather_sums"], 1)
                    v.wait_ge(c["gather_sums"], g * 2 + 1)
                    v.tensor_tensor(of_dst[:, s, :, :], of_dst[:, s, :, :], raw[:, s, :, 2 * DW:WW], ALU.add).then_inc(c["gather_sums"], 1)
                    v.wait_ge(c["gather_sums"], g * 2 + 2)
                v.tensor_tensor(weight[:], of_dst[:, s, :, H], pack[:, s, 1, :], ALU.mult).then_inc(step, 1)
                v.tensor_copy(msg[:, s, :, H], of_dst[:, s, :, H]).then_inc(step, 1)
                v.wait_ge(emb_ready, g + 1)
                v.tensor_tensor(emb_prod[:], of_dst[:, s, :, MW:DW], ps_emb[:].rearrange("p (t f) -> p t f", t=TILES), ALU.mult).then_inc(emb_used, 1)
                v.wait_ge(emb_used, g + 1)
                v.tensor_reduce(adapt[:], emb_prod[:], AX.X, ALU.add).then_inc(step, 1)

            def message(g, s, base):
                v.tensor_tensor(dump_off[:], c["dumpf"][:].broadcast_to([P, TILES]), pack[:, s, 0, :], ALU.subtract).then_inc(step, 1)
                v.wait_ge(step, base + 4)
                v.wait_ge(gate_ready, g + 1)
                v.scalar_tensor_tensor(dump_off[:], ps_count, 0.0, dump_off[:], ALU.is_gt, ALU.mult).then_inc(step, 1)
                v.tensor_tensor(gated[:], ps_gate[:, 0:TILES * H].rearrange("p (t f) -> p t f", t=TILES), wide(adapt[:], H),
                                ALU.add).then_inc(gate_used, 1)
                v.wait_ge(gate_used, g + 1)
                v.tensor_tensor(gated[:], gated[:], of_dst[:, s, :, 0:H], ALU.mult).then_inc(step, 1)
                v.tensor_tensor(index_f[:, s, :], pack[:, s, 0, :], dump_off[:], ALU.add).then_inc(step, 1)
                v.wait_ge(step, base + 6)
                v.tensor_tensor(msg[:, s, :, 0:H], gated[:], wide(weight[:], H), ALU.mult).then_inc(step, 1)
                v.wait_ge(step, base + 8)
                v.sem_inc(msg_ready, 1)
                v.sem_inc(pack_free, 1)

            def turn(g, s, i, first):
                v.wait_ge(ids_in[s], i * 48 + 48)
                v.tensor_scalar(is_high[0:HIGH, :], ids8[0:HIGH, s, 0, :], c["iota_pf"][0:HIGH, :], None, ALU.is_equal).then_inc(high_ready, 1)
                v.tensor_tensor(same[:, s, :, :], ids16[:, s, 0, :].rearrange("p (t j) -> p t j", t=TILES), wide(src_early[:, s, :], P),
                                ALU.is_equal).then_inc(same_ready, 1)
                v.wait_ge(z_rows, g + 1)
                v.scalar_tensor_tensor(z_masked[:], ids8[:, s, 1, :], c["iota_pf"][:], ps_z[:], ALU.is_equal, ALU.mult)\
                 .then_inc(z_masked_ready, 1)
                v.wait_ge(same_ready, g + 1)
                v.tensor_tensor(before[:, s, :, :], same[:, s, :, :], c["after"][:].unsqueeze(1).broadcast_to([P, TILES, P]), ALU.mult)\
                 .then_inc(before_ready, 1)
                if windowed:
                    v.tensor_tensor(node_of[:], c["iota_pf"][:], ids16[:, s, 1, 0:1], ALU.add).then_inc(c["node_of_ready"], 1)
                    v.wait_ge(c["node_of_ready"], g + 1)
                    v.tensor_scalar(in_window[:, s, :], ids16[:, s, 1, :], node_of[:], None, ALU.is_equal).then_inc(window_ready, 1)
                    v.wait_ge(window_ready, g + 1)
                v.wait_ge(before_ready, g + 1)
                v.wait_ge(z_masked_ready, g + 1)
                v.sem_inc(ids_free, 1)
                if not first:
                    if isinstance(g, int):
                        j = (g - 1) // 2
                    else:
                        j = i - 1 if s == 0 else i
                    v.wait_ge(pack_in[1 - s], j * (16 if windowed else 32) + (16 if windowed else 32))
                    if not windowed:
                        v.wait_ge(gathered[1 - s], j * 128 + 128)
                    embeddings(g - 1, 1 - s)
                v.wait_ge(z_spread, g + 1)
                v.tensor_scalar(is_type[:], ps_z[0:Z, :], c["iota_pf"][0:Z, :], None, ALU.is_equal).then_inc(type_ready, 1)
                if not first:
                    message(g - 1, 1 - s, (g - 1) * 8)

            v.sem_inc(ids_free, 2)
            v.sem_inc(pack_free, 2)
            turns(v, turn)
            last_in = NG // 2 * (16 if windowed else 32)
            v.wait_ge(pack_in[1], last_in)
            if not windowed:
                v.wait_ge(gathered[1], NG // 2 * 128)
            embeddings(NG - 1, 1)
            message(NG - 1, 1, (NG - 1) * 8)

        @block.sync
        def _(sp):
            ways(sp, c, lambda windowed: loads(sp, windowed))

        @block.gpsimd
        def _(pool):
            ways(pool, c, lambda windowed: scatters_of_all(pool, windowed))

        @block.scalar
        def _(act):
            ways(act, c, lambda windowed: act_all(act, windowed))

        @block.tensor
        def _(pe):
            ways(pe, c, lambda windowed: pe_all(pe, windowed))

        @block.vector
        def _(v):
            ways(v, c, lambda windowed: vector_all(v, windowed))


class Steps:

    def __init__(self, sem, each):
        self.sem, self.each, self.n = sem, each, 0

    def then(self, ins):
        ins.then_inc(self.sem, 1)
        self.n += 1

    def wait(self, eng, i):
        eng.wait_ge(self.sem, i * self.each + self.n)


LN_STEPS = 6


def layer_norm(v, c, st, i, y, out, sq, m, rstd, var_ready, root_ready, count):
    before, of = count
    wide = [P, NODE_TILES, H]
    st.then(v.tensor_reduce(m, y, AX.X, ALU.add))
    st.wait(v, i)
    st.then(v.tensor_scalar(m, m, 1.0 / H, None, ALU.mult))
    st.wait(v, i)
    st.then(v.tensor_tensor(y, y, m.unsqueeze(2).broadcast_to(wide), ALU.subtract))
    st.wait(v, i)
    st.then(v.tensor_tensor(sq, y, y, ALU.mult))
    st.wait(v, i)
    v.tensor_reduce(m, sq, AX.X, ALU.add).then_inc(var_ready, 1)
    v.wait_ge(root_ready, i * of + before + 1)
    st.then(v.reciprocal(rstd, rstd))
    st.wait(v, i)
    st.then(v.tensor_tensor(out, y, rstd.unsqueeze(2).broadcast_to(wide), ALU.mult))
    st.wait(v, i)


def node_rows(ap, i):
    return ap[bass.DynSlice(i * NS, NS), :].rearrange("(a p) f -> p a f", p=P)


def layer0_nodes(nc, t, c):
    with ExitStack() as ctx:
        def sb(name, shape, dt=F32):
            return ctx.enter_context(nc.sbuf_tensor("n0_" + name, shape, dt))

        def sem(name):
            return ctx.enter_context(nc.semaphore("n0_" + name))

        acc = sb("acc", [P, TILES, NODE_TILES, MW])
        x = sb("x", [P, NODE_TILES, H])
        total = sb("total", [P, NODE_TILES, MW])
        y = sb("y", [P, NODE_TILES, H])
        sq = sb("sq", [P, NODE_TILES, H])
        x1 = sb("x1", [P, NODE_TILES, H])
        m = sb("m", [P, NODE_TILES])
        rstd = sb("rstd", [P, NODE_TILES])
        x1T = sb("x1T", [H, NS])
        h1T = sb("h1T", [2 * H, RELS // 2, NS])
        h2 = sb("h2", [P, NODE_TILES, RELS * H])
        ps_t = ctx.enter_context(nc.psum_tensor("n0_ps_t", [H, 512], F32))
        ps_h1 = ctx.enter_context(nc.psum_tensor("n0_ps_h1", [2 * H, 2, 512], F32))
        ps_h2 = ctx.enter_context(nc.psum_tensor("n0_ps_h2", [P, NODE_TILES, 512], F32))
        nodes_in = sem("nodes_in")
        step = sem("n0_step")
        var_ready = sem("var_ready")
        root_ready = sem("root_ready")
        x1_ready = sem("x1_ready")
        x1T_in_psum = sem("x1T_in_psum")
        x1T_ready = sem("x1T_ready")
        h1_in_psum = sem("h1_in_psum")
        h1_ready = sem("h1_ready")
        h2_in_psum = sem("h2_in_psum")
        h2_ready = sem("h2_ready")
        nodes_out = sem("nodes_out")
        wb_in = sem("wb_in")
        block = ctx.enter_context(nc.Block())

        @block.sync
        def _(sp):
            with sp.Fori(0, STEPS) as i:
                for k in range(TILES):
                    sp.dma_start(acc[:, k, :, :], node_rows(t["acc0"][k], i)).then_inc(nodes_in, 16)
                sp.dma_start(x[:], node_rows(t["x"], i)).then_inc(nodes_in, 16)
                wait_in_loop(sp, c, x1_ready, i + 1)
                sp.dma_start(node_rows(t["x1"], i), x1[:]).then_inc(nodes_out, 16)
                wait_in_loop(sp, c, h2_ready, i + 1)
                sp.dma_start(node_rows(t["h2_wide"], i), h2[:]).then_inc(nodes_out, 16)
                wait_in_loop(sp, c, nodes_out, i * 32 + 32)

        @block.vector
        def _(v):
            st = Steps(step, TILES - 1 + 4 + 2 * LN_STEPS + 3)
            wide = [P, NODE_TILES, H]
            v.memset(c["wb"][:], 0.0).then_inc(wb_in, 1)
            with v.Fori(0, STEPS) as i:
                st.n = 0
                v.wait_ge(nodes_in, i * (16 * (TILES + 1)) + 16 * (TILES + 1))
                st.then(v.tensor_tensor(total[:], acc[:, 0, :, :], acc[:, 1, :, :], ALU.add))
                for k in range(2, TILES):
                    st.wait(v, i)
                    st.then(v.tensor_tensor(total[:], total[:], acc[:, k, :, :], ALU.add))
                st.wait(v, i)
                st.then(v.tensor_scalar(m[:], total[:, :, H], 1e-8, None, ALU.max))
                st.wait(v, i)
                st.then(v.reciprocal(m[:], m[:]))
                st.wait(v, i)
                st.then(v.tensor_tensor(y[:], total[:, :, 0:H], m[:].unsqueeze(2).broadcast_to(wide), ALU.mult))
                st.wait(v, i)
                st.then(v.tensor_tensor(y[:], y[:], x[:], ALU.add))
                st.wait(v, i)
                layer_norm(v, c, st, i, y[:], sq[:], sq[:], m[:], rstd[:], var_ready, root_ready, (0, 2))
                st.then(v.tensor_tensor(y[:], sq[:], c["gamma"][:].unsqueeze(1).broadcast_to(wide), ALU.mult))
                st.wait(v, i)
                st.then(v.tensor_tensor(y[:], y[:], c["beta"][:].unsqueeze(1).broadcast_to(wide), ALU.add))
                st.wait(v, i)
                st.then(v.tensor_tensor(y[:], y[:], x[:], ALU.add))
                st.wait(v, i)
                layer_norm(v, c, st, i, y[:], x1[:], sq[:], m[:], rstd[:], var_ready, root_ready, (1, 2))
                v.sem_inc(x1_ready, 1)
                assert st.n == st.each, (st.n, st.each)
                v.wait_ge(x1T_in_psum, i + 1)
                v.tensor_copy(x1T[:], ps_t[:, 0:NS]).then_inc(x1T_ready, 1)
                v.wait_ge(h2_in_psum, i + 1)
                v.tensor_copy(h2[:], ps_h2[:, :, 0:RELS * H]).then_inc(h2_ready, 1)

        @block.scalar
        def _(act):
            act.wait_ge(wb_in, 1)
            for half in range(2):
                act.dma_start(c["wb"][half * H:(half + 1) * H, :, half * H:(half + 1) * H],
                              t["wb"].rearrange("(q b) i o -> b i q o", b=2)[half]).then_inc(c["wb_done"], 16)
            act.wait_ge(c["wb_done"], 32)
            with act.Fori(0, STEPS) as i:
                for n in range(2):
                    act.wait_ge(var_ready, i * 2 + n + 1)
                    act.activation(rstd[:], m[:], ACT.Sqrt, bias=c["eps"][:], scale=1.0 / H).then_inc(root_ready, 1)
                for q in range(RELS // 2):
                    act.wait_ge(h1_in_psum, i * (RELS // 2) + q + 1)
                    act.activation(h1T[:, q, :], ps_h1[:, q % 2, :], ACT.Relu, bias=c["ba"][:]).then_inc(h1_ready, 1)

        @block.tensor
        def _(pe):
            pe.wait_ge(c["wb_done"], 32)
            with pe.Fori(0, STEPS) as i:
                wait_in_loop(pe, c, x1_ready, i + 1)
                for a in range(NODE_TILES):
                    last = pe.transpose(ps_t[:, a * P:(a + 1) * P], x1[:, a, :], c["ident"][:])
                last.then_inc(x1T_in_psum, 1)
                wait_in_loop(pe, c, x1T_ready, i + 1)
                for q in range(RELS // 2):
                    if q >= 2:
                        wait_in_loop(pe, c, h1_ready, i * (RELS // 2) + q - 1)
                    pe.matmul(ps_h1[:, q % 2, :], c["wa"][:, q * 2 * H:(q + 1) * 2 * H], x1T[:], start=True, stop=True)\
                      .then_inc(h1_in_psum, 1)
                wait_in_loop(pe, c, h1_ready, i * (RELS // 2) + RELS // 2)
                for a in range(NODE_TILES):
                    for q in range(RELS // 2):
                        last = pe.matmul(ps_h2[:, a, q * 2 * H:(q + 1) * 2 * H], h1T[:, q, a * P:(a + 1) * P], c["wb"][:, q, :],
                                         start=True, stop=True)
                last.then_inc(h2_in_psum, 1)


def zero_tables(nc, t, c):
    with ExitStack() as ctx:
        zeros = ctx.enter_context(nc.sbuf_tensor("zt_zeros", [P, NP // (2 * P) * H], F32))
        zeroed = ctx.enter_context(nc.semaphore("zt_zeroed"))
        block = ctx.enter_context(nc.Block())

        def fills(pool):
            pool.wait_ge(zeroed, 1)
            for k in range(TILES):
                for half in range(2):
                    pool.dma_start(t["acc1"][k].rearrange("(b p a) f -> b p (a f)", b=2, p=P)[half],
                                   zeros[:]).then_inc(c["acc1_done"][k], 16)
            for k in range(TILES):
                pool.wait_ge(c["acc1_done"][k], 32)

        @block.gpsimd
        def _(pool):
            ways(pool, c, lambda windowed: None if windowed else fills(pool))

        @block.vector
        def _(v):
            ways(v, c, lambda windowed: None if windowed else v.memset(zeros[:], 0.0).then_inc(zeroed, 1))


def layer1_edges(nc, t, c):
    with ExitStack() as ctx:
        def sb(name, shape, dt=F32):
            return ctx.enter_context(nc.sbuf_tensor("e1_" + name, shape, dt))

        def sem(name):
            return ctx.enter_context(nc.semaphore("e1_" + name))

        row_col = [sb(f"row_col{s}", [P, TILES], I32) for s in range(2)]
        pack = sb("pack", [P, 2, 2, TILES])
        dst_row = sb("dst_row", [P, 2, GE], I32)
        dst_col = sb("dst_col", [P, 2, TILES], I32)
        of_src = sb("of_src", [P, 2, TILES, H])
        same = sb("same", [P, 2, TILES, P])
        earlier = sb("earlier", [P, TILES, P])
        count = sb("count", [P, TILES])
        dump_off = sb("dump_off", [P, TILES])
        index = [sb(f"index{s}", [P, TILES], I32) for s in range(2)]
        msg = sb("msg", [P, 2, TILES, H])
        summed = sb("summed", [P, 2, TILES, H])
        ps_sum = [ctx.enter_context(nc.psum_tensor(f"e1_ps_sum{s}", [P, 512], F32)) for s in range(2)]
        edges_in = [sem(f"edges_in{s}") for s in range(2)]
        slot_free = sem("slot_free")
        gathered = [sem(f"gathered{s}") for s in range(2)]
        zeroed = sem("zeroed")
        step = sem("step")
        index_ready = sem("index_ready")
        onehot_ready = sem("onehot_ready")
        msg_ready = sem("msg_ready")
        sum_ready = sem("sum_ready")
        summed_ready = sem("summed_ready")
        first_added = sem("first_added")
        next_added = sem("next_added")
        block = ctx.enter_context(nc.Block())
        acc_done = c["acc1_done"]

        def cols(name, g):
            return t[name][:, bass.DynSlice(g, 1), :].rearrange("p g k -> p (g k)")

        def loads(sp, windowed):
            with sp.Fori(0, NG // 2) as i:
                for s in range(2):
                    g = i * 2 + s
                    wait_in_loop(sp, c, slot_free, g + 1)
                    sp.dma_start(row_col[s][:], cols("row", g)).then_inc(edges_in[s], 16)
                    sp.dma_start(pack[:, s, :, :], t["pack1"][:, bass.DynSlice(g, 1), :, :].rearrange("p g r k -> p (g r) k")).then_inc(edges_in[s], 16)
                    if not windowed:
                        sp.dma_start(dst_col[:, s, :], cols("dst", g)).then_inc(edges_in[s], 16)
                        sp.dma_start(dst_row[:, s, :],
                                     t["dst_flat"][bass.DynSlice(g * GE, GE)].partition_broadcast(P)).then_inc(edges_in[s], 16)

        def pool_all(pool, windowed):
            each = 32 if windowed else 64

            def gathers(i, s):
                wait_in_loop(pool, c, edges_in[s], i * each + each)
                for k in range(TILES):
                    nc.gpsimd.indirect_dma_start(of_src[:, s, k, :], None, t["h2"],
                                                 bass.IndirectOffsetOnAxis(ap=row_col[s][:, k:k + 1], axis=0)).then_inc(gathered[s], 16)

            def scatters(i, s):
                wait_in_loop(pool, c, index_ready, i * 2 + s + 1)
                wait_in_loop(pool, c, summed_ready, i * 2 + s + 1)
                for k in range(TILES):
                    wait_in_loop(pool, c, acc_done[k], (i * 2 + s) * 16 + 32)
                    nc.gpsimd.indirect_dma_start(t["acc1"][k], bass.IndirectOffsetOnAxis(ap=index[s][:, k:k + 1], axis=0),
                                                 summed[:, s, k, :], None, compute_op=ALU.add).then_inc(acc_done[k], 16)

            if windowed:
                with pool.Fori(0, NG // 2) as i:
                    gathers(i, 0)
                    gathers(i, 1)
                return
            gathers(0, 0)
            with pool.Fori(0, NG // 2 - 1) as i:
                gathers(i, 1)
                scatters(i, 0)
                gathers(i + 1, 0)
                scatters(i, 1)
            gathers(NG // 2 - 1, 1)
            scatters(NG // 2 - 1, 0)
            scatters(NG // 2 - 1, 1)
            for k in range(TILES):
                pool.wait_ge(acc_done[k], NG * 16 + 32)

        def act_all(act):
            with act.Fori(0, NG // 2) as i:
                for s in range(2):
                    g = i * 2 + s
                    act.wait_ge(sum_ready, g + 1)
                    for k in range(TILES):
                        act.wait_ge(acc_done[k], g * 16 + 16)
                    act.activation(summed[:, s, :, :], ps_sum[s][:, 0:TILES * H].rearrange("p (t f) -> p t f", t=TILES),
                                   ACT.Copy).then_inc(summed_ready, 1)

        def pe_all(pe, windowed):
            with pe.Fori(0, NG // 2) as i:
                for s in range(2):
                    g = i * 2 + s
                    wait_in_loop(pe, c, msg_ready, g + 1)
                    for k in range(TILES):
                        at = 0 if windowed else k * H
                        last = pe.matmul(ps_sum[s][:, at:at + H], same[:, s, k, :], msg[:, s, k, :],
                                         start=(k == 0 or not windowed), stop=(k == TILES - 1 or not windowed))
                    last.then_inc(sum_ready, 1)

        def add_to_blocks(v, g, s, at):
            v.wait_ge(sum_ready, g + 1)
            if not (isinstance(g, int) and g == 0):
                v.wait_ge(next_added, g)
            part = ps_sum[s][:, 0:H]
            one = c["agg"][:, bass.DynSlice(at, 1), :].rearrange("p b f -> p (b f)")
            two = c["agg"][:, bass.DynSlice(at + 1, 1), :].rearrange("p b f -> p (b f)")
            v.scalar_tensor_tensor(one, part, c["in_first"][:, bass.DynSlice(g, 1)], one, ALU.mult, ALU.add).then_inc(first_added, 1)
            v.scalar_tensor_tensor(two, part, c["in_next"][:, bass.DynSlice(g, 1)], two, ALU.mult, ALU.add).then_inc(next_added, 1)

        def block_of(v, g):
            return v.value_load(c["block"][0:1, bass.DynSlice(g, 1)], min_val=0, max_val=BLOCKS - 2)

        def windowed_sums(v):
            def messages(g, s, i):
                v.wait_ge(edges_in[s], i * 32 + 32)
                v.tensor_tensor(same[:, s, :, :], c["iota_rowf"][:].unsqueeze(1).broadcast_to([P, TILES, P]),
                                pack[:, s, 0, :].unsqueeze(2).broadcast_to([P, TILES, P]), ALU.is_equal).then_inc(onehot_ready, 1)
                v.wait_ge(gathered[s], i * 128 + 128)
                v.tensor_tensor(msg[:, s, :, :], of_src[:, s, :, :], pack[:, s, 1, :].unsqueeze(2).broadcast_to([P, TILES, H]),
                                ALU.mult).then_inc(onehot_ready, 1)
                v.wait_ge(onehot_ready, g * 2 + 2)
                v.sem_inc(msg_ready, 1)
                v.sem_inc(slot_free, 1)

            v.memset(c["agg"][:], 0.0).then_inc(zeroed, 1)
            v.wait_ge(zeroed, 1)
            v.sem_inc(slot_free, 2)
            messages(0, 0, 0)
            messages(1, 1, 0)
            with v.Fori(1, NG // 2) as i:
                for s in range(2):
                    add_to_blocks(v, i * 2 + (s - 2), s, block_of(v, i * 2 + (s - 2)))
                    messages(i * 2 + s, s, i)
            for s in range(2):
                add_to_blocks(v, NG - 2 + s, s, block_of(v, NG - 2 + s))

        def table_sums(v):
            v.sem_inc(slot_free, 2)
            with v.Fori(0, NG // 2) as i:
                for s in range(2):
                    g = i * 2 + s
                    base = g * 5
                    v.wait_ge(edges_in[s], i * 64 + 64)
                    for k in range(TILES):
                        v.wait_ge(acc_done[k], g * 16 + 16)
                    one_of_equals(v, c, step, base, dst_col[:, s, :], dst_row[:, s, :], same[:, s, :, :], earlier[:], count[:],
                                  dump_off[:], index[s][:]).then_inc(index_ready, 1)
                    v.wait_ge(gathered[s], i * 128 + 128)
                    v.tensor_tensor(msg[:, s, :, :], of_src[:, s, :, :], pack[:, s, 1, :].unsqueeze(2).broadcast_to([P, TILES, H]),
                                    ALU.mult).then_inc(msg_ready, 1)
                    v.wait_ge(index_ready, g + 1)
                    v.wait_ge(msg_ready, g + 1)
                    v.sem_inc(slot_free, 1)

        @block.sync
        def _(sp):
            ways(sp, c, lambda windowed: loads(sp, windowed))

        @block.gpsimd
        def _(pool):
            ways(pool, c, lambda windowed: pool_all(pool, windowed))

        @block.scalar
        def _(act):
            ways(act, c, lambda windowed: None if windowed else act_all(act))

        @block.tensor
        def _(pe):
            ways(pe, c, lambda windowed: pe_all(pe, windowed))

        @block.vector
        def _(v):
            ways(v, c, lambda windowed: windowed_sums(v) if windowed else table_sums(v))


def collect_tables(nc, t, c):
    with ExitStack() as ctx:
        acc = ctx.enter_context(nc.sbuf_tensor("ct_acc", [P, TILES, NODE_TILES, H], F32))
        acc_in = ctx.enter_context(nc.semaphore("ct_acc_in"))
        step = ctx.enter_context(nc.semaphore("ct_step"))
        summed = ctx.enter_context(nc.semaphore("ct_summed"))
        block = ctx.enter_context(nc.Block())

        def loads(sp):
            sp.sem_inc(summed, 1)
            with sp.Fori(0, STEPS) as i:
                wait_in_loop(sp, c, summed, i + 1)
                for k in range(TILES):
                    sp.dma_start(acc[:, k, :, :], node_rows(t["acc1"][k], i)).then_inc(acc_in, 16)

        def sums(v):
            with v.Fori(0, STEPS) as i:
                v.wait_ge(acc_in, i * (16 * TILES) + 16 * TILES)
                total = c["agg"][:, bass.DynSlice(i * NODE_TILES, NODE_TILES), :]
                v.tensor_tensor(total, acc[:, 0, :, :], acc[:, 1, :, :], ALU.add).then_inc(step, 1)
                for k in range(2, TILES):
                    v.wait_ge(step, i * (TILES - 1) + k - 1)
                    v.tensor_tensor(total, total, acc[:, k, :, :], ALU.add).then_inc(step, 1)
                v.wait_ge(step, i * (TILES - 1) + TILES - 1)
                v.sem_inc(summed, 1)

        @block.sync
        def _(sp):
            ways(sp, c, lambda windowed: None if windowed else loads(sp))

        @block.vector
        def _(v):
            ways(v, c, lambda windowed: None if windowed else sums(v))


def layer1_nodes(nc, t, c):
    with ExitStack() as ctx:
        def sb(name, shape, dt=F32):
            return ctx.enter_context(nc.sbuf_tensor("n1_" + name, shape, dt))

        def sem(name):
            return ctx.enter_context(nc.semaphore("n1_" + name))

        x1 = sb("x1", [P, NODE_TILES, H])
        y = sb("y", [P, NODE_TILES, H])
        sq = sb("sq", [P, NODE_TILES, H])
        res = sb("res", [P, NODE_TILES, H])
        m = sb("m", [P, NODE_TILES])
        rstd = sb("rstd", [P, NODE_TILES])
        nodes_in = sem("nodes_in")
        step = sem("n1_step")
        var_ready = sem("var_ready")
        root_ready = sem("root_ready")
        result_ready = sem("result_ready")
        nodes_out = sem("nodes_out")
        block = ctx.enter_context(nc.Block())

        @block.sync
        def _(sp):
            with sp.Fori(0, STEPS) as i:
                sp.dma_start(x1[:], node_rows(t["x1"], i)).then_inc(nodes_in, 16)
                wait_in_loop(sp, c, result_ready, i + 1)
                sp.dma_start(node_rows(t["out"], i), res[:]).then_inc(nodes_out, 16)
                wait_in_loop(sp, c, nodes_out, i * 16 + 16)

        @block.vector
        def _(v):
            st = Steps(step, 3 + LN_STEPS)
            wide = [P, NODE_TILES, H]
            with v.Fori(0, STEPS) as i:
                st.n = 0
                v.wait_ge(nodes_in, i * 16 + 16)
                st.then(v.tensor_tensor(y[:], c["agg"][:, bass.DynSlice(i * NODE_TILES, NODE_TILES), :], c["bias2"][:].unsqueeze(1).broadcast_to(wide), ALU.add))
                st.wait(v, i)
                st.then(v.tensor_scalar(y[:], y[:], 0.0, None, ALU.max))
                st.wait(v, i)
                st.then(v.tensor_tensor(y[:], y[:], x1[:], ALU.add))
                st.wait(v, i)
                layer_norm(v, c, st, i, y[:], res[:], sq[:], m[:], rstd[:], var_ready, root_ready, (0, 1))
                v.sem_inc(result_ready, 1)
                assert st.n == st.each, (st.n, st.each)

        @block.scalar
        def _(act):
            with act.Fori(0, STEPS) as i:
                act.wait_ge(var_ready, i + 1)
                act.activation(rstd[:], m[:], ACT.Sqrt, bias=c["eps"][:], scale=1.0 / H).then_inc(root_ready, 1)


def program(nc, t):
    with ExitStack() as ctx:
        def sb(name, shape, dt=F32):
            return ctx.enter_context(nc.sbuf_tensor(name, shape, dt))

        def dram(name, shape, dt=F32):
            return nc.dram_tensor(name, shape, dt).ap()

        t["window_rows"] = dram("window_rows", [NP, WW], BF16)
        t["ids16"] = dram("ids16", [NG, 2, GE], I16)
        t["ids8"] = dram("ids8", [NG, 2, GE], U8)
        t["pack0"] = dram("pack0", [P, NG, 2, TILES])
        t["pack1"] = dram("pack1", [P, NG, 2, TILES])
        t["row"] = dram("row_of_edge", [P, NG, TILES], I32)
        t["acc0"] = [dram(f"acc0_{k}", [NP, MW]) for k in range(TILES)]
        t["acc1"] = [dram(f"acc1_{k}", [NP, H]) for k in range(TILES)]
        t["x1"] = dram("x1_rows", [NP, H])
        t["h2_wide"] = dram("h2_rows", [NP, RELS * H])
        t["h2"] = t["h2_wide"].rearrange("n (r f) -> (n r) f", r=RELS)
        c = {
            "iota_p": sb("iota_p", [P, 1], I32), "iota_row": sb("iota_row", [P, P], I32), "dump": sb("dump", [P, 1], I32),
            "iota_pf": sb("iota_pf", [P, 1]), "iota_rowf": sb("iota_rowf", [P, P]), "dumpf": sb("dumpf", [P, 1]),
            "ones": sb("ones", [P, P]), "ones_bf": sb("ones_bf", [P, P], BF16), "eps": sb("eps", [P, 1]), "after": sb("after", [P, P], BF16),
            "earlier_mask": sb("earlier_mask", [P, P]), "ident": sb("ident", [P, P]),
            "sorted": sb("sorted", [1, 1], I32), "z_table": sb("z_table", [HIGH, LOW], BF16),
            "emb_parts": sb("emb_parts", [Z, PARTS, G], BF16), "block": sb("block", [1, NG], I32),
            "in_first": sb("in_first", [P, NG]), "in_next": sb("in_next", [P, NG]), "agg": sb("agg", [P, BLOCKS, H]),
            "gather_sums": ctx.enter_context(nc.semaphore("gather_sums")),
            "node_of_ready": ctx.enter_context(nc.semaphore("node_of_ready")),
            "silu": sb("silu", [64, 2, GE]),
            "w1t": sb("w1t", [R, H]), "b1": sb("b1", [H, 1]), "w2b": sb("w2b", [H + 1, H]),
            "gamma": sb("gamma", [P, H]), "beta": sb("beta", [P, H]), "bias2": sb("bias2", [P, H]),
            "wa": sb("wa", [H, RELS * H]), "ba": sb("ba", [2 * H, 1]), "wb": sb("wb", [2 * H, RELS // 2, 2 * H]),
            "acc0_done": [ctx.enter_context(nc.semaphore(f"acc0_done{k}")) for k in range(TILES)],
            "acc1_done": [ctx.enter_context(nc.semaphore(f"acc1_done{k}")) for k in range(TILES)],
            "waits_passed": ctx.enter_context(nc.semaphore("waits_passed")),
            "wb_done": ctx.enter_context(nc.semaphore("wb_done")),
        }
        prepare_edges(nc, t, c)
        prepare_nodes(nc, t, c)
        layer0_edges(nc, t, c)
        layer0_nodes(nc, t, c)
        zero_tables(nc, t, c)
        layer1_edges(nc, t, c)
        collect_tables(nc, t, c)
        layer1_nodes(nc, t, c)


def kernel(x, src, dst, edge_attr_40, edge_type_8, edge_weight, edge_weight1, node_type_119, node_vec,
           L0_gnn_W1, L0_gnn_b1, L0_gnn_W2, L0_gnn_b2, L0_gnn_emb, L0_gnn_adaptW, L0_gnn_gamma, L0_gnn_beta,
           L1_gnn_weight1, L1_gnn_weight2, L1_gnn_bias1, L1_gnn_bias2):
    import numpy as np
    import concourse.bacc as bacc
    from concourse.bass_utils import run_bass_kernel_spmd as run

    def edges(a, fill):
        flat = np.full(NG * GE, fill, a.dtype)
        flat[:E] = a.reshape(E)
        return np.ascontiguousarray(flat.reshape(NG, TILES, P).transpose(2, 0, 1)), flat

    def nodes(a):
        rows = np.zeros((NP, *a.shape[1:]), a.dtype)
        rows[:N] = a
        return rows

    src_cols, src_flat = edges(np.asarray(src), PAD_NODE)
    dst_cols, dst_flat = edges(np.asarray(dst), PAD_NODE)
    attr = np.zeros((R, NG * GE), np.float32)
    attr[:, :E] = np.asarray(edge_attr_40).T
    wa = np.asarray(L1_gnn_weight1)
    arrays = {
        "src": src_cols, "dst": dst_cols, "src_flat": src_flat, "dst_flat": dst_flat,
        "rel": edges(np.asarray(edge_type_8), 0)[0], "dist": edges(np.asarray(edge_weight), 0)[0],
        "norm": edges(np.asarray(edge_weight1), 0)[0], "attr": attr,
        "x": nodes(np.asarray(x)), "z": nodes(np.asarray(node_type_119)), 
        "x_mult": nodes(np.concatenate([np.asarray(x), np.asarray(node_vec)[:, None]], 1)),
        "w1t": np.asarray(L0_gnn_W1).T, "b1": np.asarray(L0_gnn_b1)[:, None], "w2t": np.asarray(L0_gnn_W2).T,
        "b2": np.asarray(L0_gnn_b2)[None, :], "emb": np.asarray(L0_gnn_emb), "embT": np.asarray(L0_gnn_emb).T,
        "adaptT": np.asarray(L0_gnn_adaptW).T, "gamma": np.asarray(L0_gnn_gamma), "beta": np.asarray(L0_gnn_beta),
        "bias2": np.asarray(L1_gnn_bias2), "ba": np.tile(np.asarray(L1_gnn_bias1), 2)[:, None],
        "wa": wa.transpose(1, 0, 2).reshape(H, RELS * H), "wb": np.asarray(L1_gnn_weight2),
    }
    arrays = {name: np.ascontiguousarray(a) for name, a in arrays.items()}
    nc = bacc.Bacc("TRN2", target_bir_lowering=False, num_devices=1)
    t = {name: nc.dram_tensor(f"in_{name}", a.shape, mybir.dt.from_np(a.dtype), kind="ExternalInput").ap()
         for name, a in arrays.items()}
    t["out"] = nc.dram_tensor("result", (NP, H), F32, kind="ExternalOutput").ap()
    program(nc, t)
    r = run(nc, [{f"in_{name}": a for name, a in arrays.items()}], core_ids=[0])
    return r.results[0]["result"][:N]
```

```python
from contextlib import ExitStack

import concourse.bass as bass
from concourse import mybir

F32 = mybir.dt.float32
I32 = mybir.dt.int32
I16 = mybir.dt.int16
U8 = mybir.dt.uint8
BF16 = mybir.dt.bfloat16
ALU = mybir.AluOpType
ACT = mybir.ActivationFunctionType
AX = mybir.AxisListType

P = 128
N, H, E, R, Z, G, RELS = 12500, 48, 412500, 40, 119, 32, 8
TILES = 8
GE = TILES * P
NG = 4 * -(-E // (4 * GE))
NODE_TILES = 4
NS = NODE_TILES * P
STEPS = 2 * -(-(N + P) // (2 * NS))
NORM_TILES = 2 * NODE_TILES
NORM_NODES = NORM_TILES * P
NORM_STEPS = STEPS // 2
LAST_STEPS = 4
NP = STEPS * NS
PAD_NODE = N
DUMP = NP - P
DW = H + 1 + G
PARTS = 3
WW = PARTS * DW
FG = 4
FP = NG // FG
LOW = 128
HIGH = NP // LOW
BLOCKS = NP // P
MW = H + 1
SIDE = 64
PI = 3.141592653589793
CUTOFF = 6.0
EPS = 1e-5


def wait_in_loop(eng, c, sem, value):
    eng.wait_ge(sem, value)
    eng.sem_inc(c["waits_passed"], 1)


def ways(eng, c, body):
    windowed = eng.value_load(c["sorted"][0:1, 0:1], min_val=0, max_val=1)
    with eng.If(windowed == 1):
        body(True)
    with eng.Else():
        body(False)


def split(v, step, n, whole, rest, parts):
    v.tensor_copy(parts[0], whole).then_inc(step, 1)
    v.wait_ge(step, n + 1)
    v.tensor_tensor(rest, whole, parts[0], ALU.subtract).then_inc(step, 1)
    v.wait_ge(step, n + 2)
    v.tensor_copy(parts[1], rest).then_inc(step, 1)
    v.wait_ge(step, n + 3)
    v.tensor_tensor(whole, rest, parts[1], ALU.subtract).then_inc(step, 1)
    v.wait_ge(step, n + 4)
    v.tensor_copy(parts[2], whole).then_inc(step, 1)


def prepare_edges(nc, t, c):
    with ExitStack() as ctx:
        def sb(name, shape, dt=F32):
            return ctx.enter_context(nc.sbuf_tensor("pe_" + name, shape, dt))

        def sem(name):
            return ctx.enter_context(nc.semaphore("pe_" + name))

        COLS = [P, NG, TILES]
        ROWS = [FP, FG, GE]
        zeros = c["agg"][:].rearrange("p b f -> p (b f)")[:, 0:NP // (2 * P) * MW]
        dist = sb("dist", COLS)
        inside = sb("inside", COLS)
        col_i = [sb(f"col_i{n}", COLS, I32) for n in range(2)]
        pack0 = sb("pack0", [P, NG, 2, TILES])
        row_i = [sb(f"row_i{n}", ROWS, I32) for n in range(2)]
        ids16 = sb("ids16", [FP, FG, 3, GE], I16)
        ids8 = sb("ids8", [FP, FG, GE], U8)
        half_pi = sb("half_pi", [P, 1])
        top = sb("top", [FP, FG])
        low = sb("low", [FP, FG])
        first = sb("first", [FP, FG])
        worst = sb("worst", [FP, 1])
        base_f = sb("base_f", [1, NG])
        base_i = sb("base_i", [P, NG], I32)
        offset_i = sb("offset_i", [P, NG], I32)
        ps_base = ctx.enter_context(nc.psum_tensor("pe_ps_base", [P, 512], F32))
        ps_bad = ctx.enter_context(nc.psum_tensor("pe_ps_bad", [1, 512], F32))
        consts_in = sem("consts_in")
        src_in = sem("src_in")
        dst_in = sem("dst_in")
        dist_in = sem("dist_in")
        cols_in = sem("cols_in")
        norm_in = sem("norm_in")
        dst_cols_in = sem("dst_cols_in")
        out = sem("out")
        iotas = sem("iotas")
        zero_weights = sem("zero_weights")
        zeroed = sem("zeroed")
        dve = sem("dve")
        dist_clamped = sem("dist_clamped")
        cosine = sem("cosine")
        ids_ready = sem("ids_ready")
        pack0_ready = sem("pack0_ready")
        pack0_out = sem("pack0_out")
        pack1_ready = sem("pack1_ready")
        row_ready = sem("row_ready")
        worst_ready = sem("worst_ready")
        bad_ready = sem("bad_ready")
        base_ready = sem("base_ready")
        base_all = sem("base_all")
        block = ctx.enter_context(nc.Block())

        def rows(flat):
            return flat.rearrange("(q a e) -> q a e", q=FP, a=FG)

        @block.sync
        def _(sp):
            sp.dma_start(row_i[0][:], rows(t["dst_flat"])).then_inc(dst_in, 16)
            sp.dma_start(row_i[1][:], rows(t["src_flat"])).then_inc(src_in, 16)
            sp.dma_start(dist[:], t["dist"]).then_inc(dist_in, 16)
            sp.dma_start(col_i[0][:], t["src"]).then_inc(cols_in, 16)
            sp.dma_start(col_i[1][:], t["rel"]).then_inc(cols_in, 16)
            sp.wait_ge(zero_weights, 1)
            for n in range(2):
                for dst, src in ((c["w1t"][n * SIDE:n * SIDE + R, n * SIDE:n * SIDE + H], t["w1t"]),
                                 (c["b1"][n * SIDE:n * SIDE + H, :], t["b1"]),
                                 (c["w2b"][n * SIDE:n * SIDE + H, n * H:(n + 1) * H], t["w2t"]),
                                 (c["w2b"][SIDE + H:SIDE + H + 1, n * H:(n + 1) * H], t["b2"])):
                    sp.dma_start(dst, src).then_inc(consts_in, 16)
            for dst, src in ((c["gamma"][:], t["gamma"].partition_broadcast(P)),
                             (c["beta"][:], t["beta"].partition_broadcast(P)),
                             (c["bias2"][:], t["bias2"].partition_broadcast(P)), (c["wa"][:], t["wa"]),
                             (c["powers"][:], t["powers"]),
                             (c["ba"][:], t["ba"])):
                sp.dma_start(dst, src).then_inc(consts_in, 16)
            sp.wait_ge(ids_ready, 1)
            sp.dma_start(t["ids16"].rearrange("(q a) r e -> q a r e", a=FG), ids16[:]).then_inc(out, 16)
            sp.dma_start(t["ids8"].rearrange("(q a) e -> q a e", a=FG), ids8[:]).then_inc(out, 16)
            sp.wait_ge(row_ready, 1)
            sp.dma_start(col_i[0][:], t["dst"]).then_inc(dst_cols_in, 16)
            sp.wait_ge(pack0_ready, 1)
            sp.dma_start(t["pack0"], pack0[:]).then_inc(pack0_out, 16)
            sp.dma_start(dist[:], t["norm"]).then_inc(norm_in, 16)
            sp.dma_start(t["row"], col_i[1][:]).then_inc(out, 16)
            sp.wait_ge(pack1_ready, 1)
            sp.dma_start(t["pack1"], pack0[:]).then_inc(out, 16)
            sp.wait_ge(out, 64)
            sp.wait_ge(consts_in, 16 * 14)

        @block.gpsimd
        def _(pool):
            nc.gpsimd.iota(c["iota_p"][:], pattern=[[0, 1]], base=0, channel_multiplier=1).then_inc(iotas, 1)
            nc.gpsimd.iota(c["iota_row"][:], pattern=[[1, P]], base=0, channel_multiplier=0).then_inc(iotas, 1)
            nc.gpsimd.iota(c["dump"][:], pattern=[[0, 1]], base=DUMP, channel_multiplier=1).then_inc(iotas, 1)
            pool.wait_ge(zeroed, 1)
            for k in range(TILES):
                for half in range(2):
                    pool.dma_start(t["acc0"][k].rearrange("(b p a) f -> b p (a f)", b=2, p=P)[half],
                                   zeros).then_inc(c["acc0_done"][k], 16)

        @block.vector
        def _(v):
            v.memset(c["agg"][:], 0.0).then_inc(zeroed, 1)
            v.memset(c["w1t"][:], 0.0).then_inc(dve, 1)
            v.memset(c["b1"][:], 0.0).then_inc(dve, 1)
            v.memset(c["w2b"][:], 0.0).then_inc(dve, 1)
            v.wait_ge(dve, 3)
            v.sem_inc(zero_weights, 1)
            v.memset(half_pi[:], PI / 2).then_inc(dve, 1)
            v.memset(c["ones"][:], 1.0).then_inc(dve, 1)
            v.memset(c["ones_bf"][:], 1.0).then_inc(dve, 1)
            v.memset(c["eps"][:], EPS).then_inc(dve, 1)
            v.memset(c["silu"][:], 1.0).then_inc(dve, 1)
            v.wait_ge(iotas, 3)
            v.tensor_copy(c["iota_pf"][:], c["iota_p"][:]).then_inc(dve, 1)
            v.tensor_copy(c["iota_rowf"][:], c["iota_row"][:]).then_inc(dve, 1)
            v.tensor_copy(c["dumpf"][:], c["dump"][:]).then_inc(dve, 1)
            v.wait_ge(dve, 11)
            v.tensor_scalar(c["earlier_mask"][:], c["iota_rowf"][:], c["iota_pf"][:], None, ALU.is_lt)
            v.tensor_scalar(c["ident"][:], c["iota_rowf"][:], c["iota_pf"][:], None, ALU.is_equal).then_inc(dve, 1)
            v.wait_ge(dist_in, 16)
            v.tensor_scalar(inside[:], dist[:], CUTOFF, None, ALU.is_lt).then_inc(dve, 1)
            v.scalar_tensor_tensor(dist[:].rearrange("p g k -> p (g k)"), dist[:].rearrange("p g k -> p (g k)"), -1.0,
                                   dist[:].rearrange("p g k -> p (g k)"), ALU.mult, ALU.max).then_inc(dve, 1)
            v.wait_ge(dve, 14)
            v.tensor_scalar(dist[:], dist[:], CUTOFF, None, ALU.min).then_inc(dist_clamped, 1)
            v.wait_ge(dst_in, 16)
            v.tensor_reduce(top[:], row_i[0][:], AX.X, ALU.max).then_inc(dve, 1)
            v.tensor_reduce(low[:], row_i[0][:], AX.X, ALU.min).then_inc(dve, 1)
            v.tensor_copy(first[:], row_i[0][:, :, 0]).then_inc(dve, 1)
            v.tensor_copy(ids16[:, :, 1, :], row_i[0][:]).then_inc(dve, 1)
            v.wait_ge(dve, 17)
            v.scalar_tensor_tensor(top[:], top[:], float(1 - P), first[:], ALU.add, ALU.subtract).then_inc(dve, 1)
            v.tensor_tensor(low[:], first[:], low[:], ALU.subtract).then_inc(dve, 1)
            v.wait_ge(dve, 20)
            v.tensor_tensor(top[:], top[:], low[:], ALU.max).then_inc(dve, 1)
            v.wait_ge(dve, 21)
            v.tensor_reduce(worst[:], top[:], AX.X, ALU.max).then_inc(dve, 1)
            v.wait_ge(dve, 22)
            v.tensor_scalar(worst[:], worst[:], 0.0, None, ALU.is_gt).then_inc(worst_ready, 1)
            v.wait_ge(src_in, 16)
            v.tensor_copy(ids16[:, :, 0, :], row_i[1][:]).then_inc(dve, 1)
            v.tensor_scalar(row_i[0][:], row_i[1][:], 7, None, ALU.arith_shift_right).then_inc(dve, 1)
            v.wait_ge(dve, 24)
            v.tensor_copy(ids16[:, :, 2, :], row_i[0][:]).then_inc(dve, 1)
            v.wait_ge(dve, 25)
            v.tensor_scalar(row_i[0][:], row_i[1][:], LOW - 1, None, ALU.bitwise_and).then_inc(dve, 1)
            v.wait_ge(dve, 26)
            v.tensor_copy(ids8[:], row_i[0][:]).then_inc(ids_ready, 1)
            v.wait_ge(cols_in, 32)
            v.tensor_copy(pack0[:, :, 0, :], col_i[0][:]).then_inc(dve, 1)
            v.scalar_tensor_tensor(col_i[1][:].rearrange("p g k -> p (g k)"), col_i[0][:].rearrange("p g k -> p (g k)"),
                                   float(RELS), col_i[1][:].rearrange("p g k -> p (g k)"), ALU.mult, ALU.add)\
             .then_inc(row_ready, 1)
            v.wait_ge(cosine, 1)
            v.tensor_scalar(dist[:], dist[:], 1.0, 0.5, ALU.add, ALU.mult).then_inc(dve, 1)
            v.wait_ge(dve, 28)
            v.tensor_tensor(pack0[:, :, 1, :], dist[:], inside[:], ALU.mult).then_inc(pack0_ready, 1)
            v.wait_ge(bad_ready, 1)
            v.tensor_scalar(c["sorted"][:], ps_bad[0:1, 0:1], 0.0, None, ALU.is_equal).then_inc(dve, 1)
            v.wait_ge(dst_cols_in, 16)
            v.tensor_copy(base_f[:], col_i[0][0:1, :, 0]).then_inc(base_ready, 1)
            v.wait_ge(base_ready, 1)
            v.tensor_scalar(col_i[0][:], col_i[0][:], P - 1, None, ALU.bitwise_and).then_inc(dve, 1)
            v.wait_ge(dve, 30)
            v.wait_ge(base_all, 1)
            v.tensor_copy(base_i[:], ps_base[:, 0:NG]).then_inc(dve, 1)
            v.wait_ge(dve, 31)
            v.tensor_scalar(c["block"][:], base_i[0:1, :], 7, None, ALU.arith_shift_right).then_inc(dve, 1)
            v.tensor_scalar(offset_i[:], base_i[:], P - 1, None, ALU.bitwise_and).then_inc(dve, 1)
            v.wait_ge(dve, 33)
            v.tensor_scalar(c["in_first"][:], offset_i[:], c["iota_pf"][:], None, ALU.is_le).then_inc(dve, 1)
            v.tensor_scalar(c["in_next"][:], offset_i[:], c["iota_pf"][:], None, ALU.is_gt).then_inc(dve, 1)
            v.wait_ge(pack0_out, 16)
            v.tensor_copy(pack0[:, :, 0, :], col_i[0][:]).then_inc(dve, 1)
            v.wait_ge(norm_in, 16)
            v.tensor_copy(pack0[:, :, 1, :], dist[:]).then_inc(dve, 1)
            v.wait_ge(dve, 37)
            v.sem_inc(pack1_ready, 1)

        @block.scalar
        def _(act):
            act.wait_ge(dve, 4)
            act.wait_ge(dist_clamped, 1)
            act.activation(dist[:], dist[:], ACT.Sin, bias=half_pi[:], scale=-PI / CUTOFF).then_inc(cosine, 1)

        @block.tensor
        def _(pe):
            pe.wait_ge(worst_ready, 1)
            pe.matmul(ps_bad[0:1, 0:1], worst[:], c["ones"][0:FP, 0:1], start=True, stop=True).then_inc(bad_ready, 1)
            pe.wait_ge(base_ready, 1)
            pe.matmul(ps_base[:, 0:NG], c["ones"][0:1, :], base_f[:], start=True, stop=True).then_inc(base_all, 1)


def prepare_nodes(nc, t, c):
    with ExitStack() as ctx:
        def sb(name, shape, dt=F32):
            return ctx.enter_context(nc.sbuf_tensor("pn_" + name, shape, dt))

        def sem(name):
            return ctx.enter_context(nc.semaphore("pn_" + name))

        emb = sb("emb", [Z, G])
        rest_e = sb("rest_e", [Z, G])
        embT = sb("embT", [G, Z])
        adaptT = sb("adaptT", [G, G])
        adapted = sb("adapted", [Z, G])
        z_hl = sb("z_hl", [HIGH, LOW], I32)
        zrow = sb("zrow", [P, NP], I32)
        x_mult = sb("x_mult", [P, STEPS * NODE_TILES, MW])
        onehot = sb("onehot", [P, 2, NS])
        row = sb("row", [P, NODE_TILES, DW])
        rest = sb("rest", [P, NODE_TILES, DW])
        parts = sb("parts", [P, 2, NODE_TILES, PARTS, DW], BF16)
        CHUNKS = (0, 2, 10, STEPS)
        ps_emb = ctx.enter_context(nc.psum_tensor("pn_ps_emb", [P, 512], F32))
        ps_ej = ctx.enter_context(nc.psum_tensor("pn_ps_ej", [P, 2, NODE_TILES, 512 // NODE_TILES], F32))
        emb_in = sem("emb_in")
        adapted_in_psum = sem("adapted_in_psum")
        adapted_ready = sem("adapted_ready")
        step = sem("step")
        nodes_in = [sem(f"nodes_in{n}") for n in range(3)]
        onehot_ready = sem("onehot_ready")
        looked_up = sem("looked_up")
        parts_ready = sem("parts_ready")
        parts_out = [sem(f"parts_out{s}") for s in range(2)]
        block = ctx.enter_context(nc.Block())

        def store(sp, i, s):
            wait_in_loop(sp, c, parts_ready, i * 2 + s + 1)
            sp.dma_start(t["window_rows"][bass.DynSlice((i * 2 + s) * NS, NS), :].rearrange("(p a) f -> p (a f)", p=P),
                         parts[:, s, :, :, :].rearrange("p a r f -> p (a r f)")).then_inc(parts_out[s], 16)

        @block.sync
        def _(sp):
            for dst, src in ((embT[:], t["embT"]), (adaptT[:], t["adaptT"]), (emb[:], t["emb"]),
                             (z_hl[:], t["z"].rearrange("(h l) -> h l", l=LOW))):
                sp.dma_start(dst, src).then_inc(emb_in, 16)
            for s in range(2):
                sp.sem_inc(parts_out[s], 16)
            for n in range(3):
                some = slice(CHUNKS[n] * NS, CHUNKS[n + 1] * NS)
                sp.dma_start(zrow[:, some], t["z"][some].partition_broadcast(P)).then_inc(nodes_in[n], 16)
                sp.dma_start(x_mult[:, some.start // P:some.stop // P, :].rearrange("p (n a) f -> p n (a f)", a=NODE_TILES),
                             t["x_mult"][some, :].rearrange("(n p a) f -> p n (a f)", p=P, a=NODE_TILES)).then_inc(nodes_in[n], 16)
            with sp.Fori(0, STEPS // 2) as i:
                for s in range(2):
                    store(sp, i, s)
            for s in range(2):
                sp.wait_ge(parts_out[s], STEPS // 2 * 16 + 16)


        @block.vector
        def _(v):
            v.tensor_copy(c["powers_bf"][:], c["powers"][:])
            v.tensor_scalar(c["bounds"][:], c["powers"][:], 2.5, None, ALU.mult)
            v.wait_ge(emb_in, 64)
            v.tensor_copy(c["z_table"][:], z_hl[:])
            split(v, step, 0, emb[:], rest_e[:], [c["emb_parts"][:, n, :] for n in range(PARTS)])
            v.wait_ge(adapted_in_psum, 1)
            v.tensor_copy(adapted[:], ps_emb[0:Z, 0:G]).then_inc(adapted_ready, 1)

            def compare(n, s):
                v.tensor_scalar(onehot[:, s, :], zrow[:, bass.DynSlice(n * NS, NS)], c["iota_pf"][:], None, ALU.is_equal)\
                 .then_inc(onehot_ready, 1)

            def turn(n, i, s, last=False):
                if not last:
                    compare(n + 1, 1 - s)
                v.wait_ge(step, n * 8 + 5)
                own = x_mult[:, bass.DynSlice(n * NODE_TILES, NODE_TILES), :]
                v.tensor_tensor(row[:, :, 0:H], own[:, :, 0:H], own[:, :, H:MW].broadcast_to([P, NODE_TILES, H]), ALU.mult).then_inc(step, 1)
                v.tensor_copy(row[:, :, H:MW], own[:, :, H:MW]).then_inc(step, 1)
                v.wait_ge(looked_up, n + 1)
                v.tensor_copy(row[:, :, MW:DW], ps_ej[:, s, :, 0:G]).then_inc(step, 1)
                v.wait_ge(step, n * 8 + 8)
                v.wait_ge(parts_out[s], i * 16 + 16)
                split(v, step, n * 8 + 8, row[:], rest[:], [parts[:, s, :, m, :] for m in range(PARTS)])
                v.wait_ge(step, n * 8 + 13)
                v.sem_inc(parts_ready, 1)

            v.wait_ge(nodes_in[0], 32)
            compare(0, 0)
            turn(0, 0, 0)
            v.wait_ge(nodes_in[1], 32)
            turn(1, 0, 1)
            with v.Fori(1, CHUNKS[2] // 2 - 1) as i:
                for s in range(2):
                    turn(i * 2 + s, i, s)
            turn(CHUNKS[2] - 2, CHUNKS[2] // 2 - 1, 0)
            v.wait_ge(nodes_in[2], 32)
            turn(CHUNKS[2] - 1, CHUNKS[2] // 2 - 1, 1)
            with v.Fori(CHUNKS[2] // 2, STEPS // 2 - 1) as i:
                for s in range(2):
                    turn(i * 2 + s, i, s)
            turn(STEPS - 2, STEPS // 2 - 1, 0)
            turn(STEPS - 1, STEPS // 2 - 1, 1, last=True)

        @block.tensor
        def _(pe):
            pe.wait_ge(emb_in, 64)
            pe.matmul(ps_emb[0:Z, 0:G], embT[:], adaptT[:], start=True, stop=True).then_inc(adapted_in_psum, 1)
            pe.wait_ge(adapted_ready, 1)
            with pe.Fori(0, STEPS // 2) as i:
                for s in range(2):
                    wait_in_loop(pe, c, onehot_ready, i * 2 + s + 1)
                    for a in range(NODE_TILES):
                        last = pe.matmul(ps_ej[:, s, a, 0:G], onehot[0:Z, s, :].rearrange("z (p a) -> z a p", a=NODE_TILES)[:, a, :],
                                         adapted[:], start=True, stop=True)
                    last.then_inc(looked_up, 1)


def one_of_equals(v, c, step, base, key_col, key_row, same, earlier, count, dump_off, index):
    v.tensor_tensor(same, key_row.rearrange("p (t j) -> p t j", t=TILES),
                    key_col.unsqueeze(2).broadcast_to([P, TILES, P]), ALU.is_equal).then_inc(step, 1)
    v.tensor_tensor(dump_off, c["dumpf"][:].broadcast_to([P, TILES]), key_col, ALU.subtract).then_inc(step, 1)
    v.wait_ge(step, base + 1)
    v.tensor_tensor(earlier, same, c["earlier_mask"][:].unsqueeze(1).broadcast_to([P, TILES, P]), ALU.mult).then_inc(step, 1)
    v.wait_ge(step, base + 3)
    v.tensor_reduce(count, earlier, AX.X, ALU.add).then_inc(step, 1)
    v.wait_ge(step, base + 4)
    v.scalar_tensor_tensor(dump_off, count, 0.0, dump_off, ALU.is_gt, ALU.mult).then_inc(step, 1)
    v.wait_ge(step, base + 5)
    return v.tensor_tensor(index, key_col, dump_off, ALU.add)


def layer0_edges(nc, t, c):
    with ExitStack() as ctx:
        def sb(name, shape, dt=F32):
            return ctx.enter_context(nc.sbuf_tensor("e0_" + name, shape, dt))

        def sem(name):
            return ctx.enter_context(nc.semaphore("e0_" + name))

        def ps(name, shape):
            return ctx.enter_context(nc.psum_tensor("e0_" + name, shape, F32))

        HALF = TILES // 2
        attr = sb("attr", [SIDE + R, 2, GE // 2])
        ids16 = sb("ids16", [P, 2, 3, GE], I16)
        ids8 = sb("ids8", [P, 2, GE], U8)
        src_early = sb("src_early", [P, 2, TILES])
        pack = sb("pack", [P, 2, 2, TILES])
        window = sb("window", [P, 2, WW], BF16)
        dst_col = [sb(f"dst_col{s}", [P, TILES], I32) for s in range(2)]
        raw = sb("raw", [P, 2, TILES, WW], BF16)
        node_of = sb("node_of", [P, 1])
        in_window = sb("in_window", [P, 2, GE], BF16)
        is_high = sb("is_high", [P, GE], BF16)
        z_masked = sb("z_masked", [P, GE], BF16)
        type_row = sb("type_row", [Z, GE], BF16)
        is_type = sb("is_type", [Z, GE], BF16)
        same = sb("same", [P, 2, TILES, P], BF16)
        of_dst = sb("of_dst", [P, 2, TILES, DW])
        emb_prod = sb("emb_prod", [P, TILES, G])
        adapt = sb("adapt", [P, TILES])
        cw_adapt = sb("cw_adapt", [P, TILES])
        gated = sb("gated", [P, TILES, H])
        msg = sb("msg", [P, TILES, MW])
        msg_rest = sb("msg_rest", [P, TILES, MW])
        msg_parts = sb("msg_parts", [P, PARTS, TILES, MW], BF16)
        dump_off = sb("dump_off", [P, TILES])
        index_f = sb("index_f", [P, 2, TILES])
        index = [sb(f"index{s}", [P, TILES], I32) for s in range(2)]
        summed = sb("summed", [P, 2, TILES, MW])
        ps_pre = ps("ps_pre", [SIDE + H, GE // 2])
        ps_gate = ps("ps_gate", [P, 512])
        ps_z = ps("ps_z", [P, GE])
        ps_row = ps("ps_row", [P, 2, 512])
        ps_emb = ps("ps_emb", [P, TILES * G])
        ps_sum = ps("ps_sum", [P, 512])
        ps_count = ps_gate[:, TILES * H:TILES * (H + 1)]

        ids_in = [sem(f"ids_in{s}") for s in range(2)]
        attr_in = [sem(f"attr_in{s}") for s in range(2)]
        pack_in = [sem(f"pack_in{s}") for s in range(2)]
        ids_free = sem("ids_free")
        attr_free = sem("attr_free")
        pack_free = sem("pack_free")
        gathered = [sem(f"gathered{s}") for s in range(2)]
        high_ready = sem("high_ready")
        z_rows = sem("z_rows")
        z_masked_ready = sem("z_masked_ready")
        z_spread = sem("z_spread")
        type_ready = sem("type_ready")
        same_ready = sem("same_ready")
        window_ready = sem("window_ready")
        pre_ready = sem("pre_ready")
        silu_ready = sem("silu_ready")
        adapt_ready = sem("adapt_ready")
        gated_ready = sem("gated_ready")
        type_row_ready = sem("type_row_ready")
        part0_ready = sem("part0_ready")
        rest_ready = sem("rest_ready")
        part1_ready = sem("part1_ready")
        parts_ready = sem("parts_ready")
        counted = sem("counted")
        attr_zeroed = sem("attr_zeroed")
        rows_in_psum = sem("rows_in_psum")
        of_dst_ready = sem("of_dst_ready")
        emb_ready = sem("emb_ready")
        emb_used = sem("emb_used")
        msg_ready = sem("msg_ready")
        sum_ready = sem("sum_ready")
        summed_ready = sem("summed_ready")
        step = sem("step")
        block = ctx.enter_context(nc.Block())
        acc_done = c["acc0_done"]

        def wide(x, n):
            return x.unsqueeze(2).broadcast_to([P, TILES, n])

        def load(sp, i, s, windowed):
            g = i * 2 + s
            wait_in_loop(sp, c, ids_free, g + 1)
            sp.dma_start(ids8[:, s, :], t["ids8"][bass.DynSlice(g, 1), :].rearrange("g e -> (g e)").partition_broadcast(P)).then_inc(ids_in[s], 16)
            sp.dma_start(ids16[:, s, :, :].rearrange("p r e -> p (r e)"),
                         t["ids16"][bass.DynSlice(g, 1), :, :].rearrange("g r e -> (g r e)").partition_broadcast(P)).then_inc(ids_in[s], 16)
            sp.dma_start(src_early[:, s, :], t["pack0"][:, bass.DynSlice(g, 1), 0, :].rearrange("p g k -> p (g k)")).then_inc(ids_in[s], 16)
            wait_in_loop(sp, c, attr_free, g + 1)
            for half in range(2):
                sp.dma_start(attr[half * SIDE:half * SIDE + R, s, :],
                             t["attr"][:, bass.DynSlice(g * GE + half * (GE // 2), GE // 2)]).then_inc(attr_in[s], 16)
            if windowed:
                start = sp.value_load(t["dst_flat"][bass.DynSlice(g * GE, 1)].unsqueeze(0), min_val=0, max_val=PAD_NODE)
                sp.dma_start(window[:, s, :], t["window_rows"][bass.DynSlice(start, P), :]).then_inc(attr_in[s], 16)
            wait_in_loop(sp, c, pack_free, g + 1)
            sp.dma_start(pack[:, s, :, :], t["pack0"][:, bass.DynSlice(g, 1), :, :].rearrange("p g r k -> p (g r) k")).then_inc(pack_in[s], 16)
            if not windowed:
                sp.dma_start(dst_col[s][:], t["dst"][:, bass.DynSlice(g, 1), :].rearrange("p g k -> p (g k)")).then_inc(pack_in[s], 16)

        def loads(sp, windowed):
            sp.wait_ge(attr_zeroed, 1)
            with sp.Fori(0, NG // 2) as i:
                for s in range(2):
                    load(sp, i, s, windowed)

        def scatters_of_all(pool, windowed):
            def gathers(i, s):
                wait_in_loop(pool, c, pack_in[s], i * 32 + 32)
                for k in range(TILES):
                    nc.gpsimd.indirect_dma_start(raw[:, s, k, :], None, t["window_rows"],
                                                 bass.IndirectOffsetOnAxis(ap=dst_col[s][:, k:k + 1], axis=0)).then_inc(gathered[s], 16)

            def scatters(i, s):
                wait_in_loop(pool, c, summed_ready, i * 2 + s + 1)
                for k in range(TILES):
                    wait_in_loop(pool, c, acc_done[k], (i * 2 + s) * 16 + 32)
                    nc.gpsimd.indirect_dma_start(t["acc0"][k], bass.IndirectOffsetOnAxis(ap=index[s][:, k:k + 1], axis=0),
                                                 summed[:, s, k, :], None, compute_op=ALU.add).then_inc(acc_done[k], 16)

            if windowed:
                with pool.Fori(0, NG // 4) as q:
                    for u in range(4):
                        scatters(q * 2 + u // 2, u % 2)
            else:
                gathers(0, 0)
                with pool.Fori(0, NG // 2 - 1) as i:
                    gathers(i, 1)
                    scatters(i, 0)
                    gathers(i + 1, 0)
                    scatters(i, 1)
                gathers(NG // 2 - 1, 1)
                scatters(NG // 2 - 1, 0)
                scatters(NG // 2 - 1, 1)
            for k in range(TILES):
                pool.wait_ge(acc_done[k], NG * 16 + 32)


        def turns(eng, turn):
            turn(0, 0, 0, True)
            turn(1, 1, 0, False)
            with eng.Fori(0, NG // 4 - 1) as q:
                for u in range(4):
                    turn(q * 4 + (u + 2), u % 2, q * 2 + (u // 2 + 1), False)
            turn(NG - 2, 0, NG // 2 - 1, False)
            turn(NG - 1, 1, NG // 2 - 1, False)

        def act_all(act, windowed):
            def part(g, m):
                act.wait_ge(msg_ready if m == 0 else rest_ready, g + 1)
                act.activation(msg_parts[:, m, :, :], (msg if m == 0 else msg_rest)[:], ACT.Copy)\
                   .then_inc(part0_ready if m == 0 else part1_ready, 1)

            def gate(g, s):
                act.wait_ge(adapt_ready, g + 1)
                for k in range(TILES):
                    last = act.activation(gated[:, k, :], ps_gate[:, k * H:(k + 1) * H], ACT.Identity,
                                          bias=cw_adapt[:, k:k + 1], scale=pack[:, s, 1, k:k + 1])
                last.then_inc(gated_ready, 1)

            def take_sum(g, s):
                act.wait_ge(sum_ready, g + 1)
                for k in range(TILES):
                    act.wait_ge(acc_done[k], g * 16 + 16)
                act.activation(index[s][:], index_f[:, s, :], ACT.Copy)
                act.activation(summed[:, s, :, :], ps_sum[:, 0:TILES * MW].rearrange("p (t f) -> p t f", t=TILES),
                               ACT.Copy).then_inc(summed_ready, 1)

            def turn(g, s, i, first):
                has_sums = not isinstance(g, int) or g >= 2
                if has_sums:
                    part(g - 2, 0)
                    part(g - 2, 1)
                act.wait_ge(z_spread, g + 1)
                act.activation(type_row[:], ps_z[0:Z, :], ACT.Copy).then_inc(type_row_ready, 1)
                if not first:
                    gate(g - 1, 1 - s)
                act.wait_ge(pre_ready, g + 1)
                act.activation(c["silu"][0:SIDE + H, s, :], ps_pre[:], ACT.Silu, bias=c["b1"][:]).then_inc(silu_ready, 1)
                if has_sums:
                    take_sum(g - 2, s)
                if windowed:
                    act.wait_ge(rows_in_psum, g + 1)
                    act.activation(of_dst[:, s, :, :].rearrange("p (b t) f -> p b t f", b=2),
                                   ps_row[:, :, 0:HALF * DW].rearrange("p b (t f) -> p b t f", t=HALF), ACT.Copy).then_inc(of_dst_ready, 1)

            turns(act, turn)
            part(NG - 2, 0)
            part(NG - 2, 1)
            gate(NG - 1, 1)
            take_sum(NG - 2, 0)
            part(NG - 1, 0)
            part(NG - 1, 1)
            take_sum(NG - 1, 1)

        def pe_all(pe, windowed):
            def emb_of_src(g, s, first):
                wait_in_loop(pe, c, type_ready, g + 1)
                if not first:
                    wait_in_loop(pe, c, emb_used, g)
                for k in range(TILES):
                    for n in range(PARTS):
                        last = pe.matmul(ps_emb[:, k * G:(k + 1) * G], is_type[:, k * P:(k + 1) * P], c["emb_parts"][:, n, :],
                                         start=(n == 0), stop=(n == PARTS - 1))
                last.then_inc(emb_ready, 1)

            def sums(g, s):
                wait_in_loop(pe, c, parts_ready, g + 1)
                if not (isinstance(g, int) and g == 0):
                    wait_in_loop(pe, c, summed_ready, g)
                for k in range(TILES):
                    for n in range(PARTS):
                        last = pe.matmul(ps_sum[:, k * MW:(k + 1) * MW], same[:, s, k, :], msg_parts[:, n, k, :],
                                         start=(n == 0), stop=(n == PARTS - 1))
                last.then_inc(sum_ready, 1)

            def counts(g, s):
                wait_in_loop(pe, c, same_ready, g + 1)
                for k in range(TILES):
                    last = pe.matmul(ps_count[:, k:k + 1], same[:, s, k, :], c["powers_bf"][:], start=True, stop=True)
                last.then_inc(counted, 1)

            def gates(g, s, first):
                wait_in_loop(pe, c, silu_ready, g + 1)
                if not first:
                    wait_in_loop(pe, c, gated_ready, g)
                for k in range(HALF):
                    pe.matmul(ps_gate[:, 0:TILES * H].rearrange("p (b k f) -> p b k f", b=2, k=HALF)[:, :, k, :],
                              c["silu"][:, s, k * P:(k + 1) * P], c["w2b"][:], start=True, stop=True)

            def turn(g, s, i, first):
                wait_in_loop(pe, c, high_ready, g + 1)
                if not first:
                    wait_in_loop(pe, c, type_row_ready, g)
                for b in range(2):
                    last = pe.matmul(ps_z[:, b * 512:(b + 1) * 512], c["z_table"][:], is_high[0:HIGH, b * 512:(b + 1) * 512],
                                     start=True, stop=True)
                last.then_inc(z_rows, 1)
                if not first:
                    gates(g - 1, 1 - s, isinstance(g, int) and g == 1)
                    emb_of_src(g - 1, 1 - s, isinstance(g, int) and g == 1)
                    counts(g - 1, 1 - s)
                wait_in_loop(pe, c, z_masked_ready, g + 1)
                for b in range(2):
                    last = pe.matmul(ps_z[0:Z, b * 512:(b + 1) * 512], c["ones_bf"][:, 0:Z], z_masked[:, b * 512:(b + 1) * 512],
                                     start=True, stop=True)
                last.then_inc(z_spread, 1)
                if not isinstance(g, int) or g >= 2:
                    sums(g - 2, s)
                each = 48 if windowed else 32
                wait_in_loop(pe, c, attr_in[s], i * each + each)
                if not first:
                    wait_in_loop(pe, c, silu_ready, g)
                pe.matmul(ps_pre[:], c["w1t"][:], attr[:, s, :], start=True, stop=True).then_inc(pre_ready, 1)
                if windowed:
                    wait_in_loop(pe, c, window_ready, g + 1)
                    if not first:
                        wait_in_loop(pe, c, of_dst_ready, g)
                    for k in range(TILES):
                        for n in range(PARTS):
                            last = pe.matmul(ps_row[:, k // HALF, k % HALF * DW:(k % HALF + 1) * DW], in_window[:, s, k * P:(k + 1) * P],
                                             window[:, s, n * DW:(n + 1) * DW], start=(n == 0), stop=(n == PARTS - 1))
                    last.then_inc(rows_in_psum, 1)
                    wait_in_loop(pe, c, rows_in_psum, g + 1)
                wait_in_loop(pe, c, pre_ready, g + 1)
                pe.sem_inc(attr_free, 1)

            pe.sem_inc(attr_free, 2)
            turns(pe, turn)
            gates(NG - 1, 1, False)
            emb_of_src(NG - 1, 1, False)
            counts(NG - 1, 1)
            sums(NG - 2, 0)
            sums(NG - 1, 1)

        def vector_all(v, windowed):
            def embeddings(g, s, base):
                if not (isinstance(g, int) and g == 0):
                    v.wait_ge(step, base)
                if windowed:
                    v.wait_ge(of_dst_ready, g + 1)
                else:
                    v.tensor_tensor(of_dst[:, s, :, :], raw[:, s, :, 0:DW], raw[:, s, :, DW:2 * DW], ALU.add).then_inc(c["gather_sums"], 1)
                    v.wait_ge(c["gather_sums"], g * 2 + 1)
                    v.tensor_tensor(of_dst[:, s, :, :], of_dst[:, s, :, :], raw[:, s, :, 2 * DW:WW], ALU.add).then_inc(c["gather_sums"], 1)
                    v.wait_ge(c["gather_sums"], g * 2 + 2)
                v.tensor_copy(msg[:, :, H], of_dst[:, s, :, H]).then_inc(step, 1)
                v.wait_ge(emb_ready, g + 1)
                v.tensor_tensor(emb_prod[:], of_dst[:, s, :, MW:DW], ps_emb[:].rearrange("p (t f) -> p t f", t=TILES), ALU.mult).then_inc(emb_used, 1)
                v.tensor_tensor(dump_off[:], c["dumpf"][:].broadcast_to([P, TILES]), pack[:, s, 0, :], ALU.subtract).then_inc(step, 1)

            def adapts(g, s, base):
                v.wait_ge(emb_used, g + 1)
                v.tensor_reduce(adapt[:], emb_prod[:], AX.X, ALU.add).then_inc(step, 1)
                v.wait_ge(counted, g + 1)
                v.wait_ge(step, base + 2)
                v.scalar_tensor_tensor(dump_off[:], ps_count, c["bounds"][:], dump_off[:], ALU.is_gt, ALU.mult).then_inc(step, 1)
                v.wait_ge(step, base + 3)
                v.tensor_tensor(cw_adapt[:], adapt[:], pack[:, s, 1, :], ALU.mult).then_inc(step, 1)
                v.wait_ge(step, base + 4)
                v.tensor_tensor(index_f[:, s, :], pack[:, s, 0, :], dump_off[:], ALU.add).then_inc(adapt_ready, 1)

            def message(g, s):
                v.wait_ge(gated_ready, g + 1)
                v.tensor_tensor(msg[:, :, 0:H], gated[:], of_dst[:, s, :, 0:H], ALU.mult).then_inc(msg_ready, 1)
                v.wait_ge(adapt_ready, g + 1)
                v.wait_ge(msg_ready, g + 1)
                v.sem_inc(pack_free, 1)

            def rest_of(g):
                v.wait_ge(part0_ready, g + 1)
                v.tensor_tensor(msg_rest[:], msg[:], msg_parts[:, 0, :, :], ALU.subtract).then_inc(rest_ready, 1)

            def last_part(g):
                v.wait_ge(part1_ready, g + 1)
                v.tensor_tensor(msg_parts[:, 2, :, :], msg_rest[:], msg_parts[:, 1, :, :], ALU.subtract).then_inc(parts_ready, 1)
                v.wait_ge(parts_ready, g + 1)

            def turn(g, s, i, first):
                has_sums = not isinstance(g, int) or g >= 2
                v.wait_ge(ids_in[s], i * 48 + 48)
                v.tensor_scalar(is_high[0:HIGH, :], ids16[0:HIGH, s, 2, :], c["iota_pf"][0:HIGH, :], None, ALU.is_equal).then_inc(high_ready, 1)
                if windowed:
                    v.tensor_tensor(node_of[:], c["iota_pf"][:], ids16[:, s, 1, 0:1], ALU.add).then_inc(c["node_of_ready"], 1)
                    v.wait_ge(c["node_of_ready"], g + 1)
                    v.tensor_scalar(in_window[:, s, :], ids16[:, s, 1, :], node_of[:], None, ALU.is_equal).then_inc(window_ready, 1)
                    v.wait_ge(window_ready, g + 1)
                if has_sums:
                    message(g - 2, s)
                v.wait_ge(z_rows, g + 1)
                v.scalar_tensor_tensor(z_masked[:], ids8[:, s, :], c["iota_pf"][:], ps_z[:], ALU.is_equal, ALU.mult)\
                 .then_inc(z_masked_ready, 1)
                if has_sums:
                    rest_of(g - 2)
                    v.wait_ge(rest_ready, g - 1)
                if not first:
                    if isinstance(g, int):
                        j = (g - 1) // 2
                    else:
                        j = i - 1 if s == 0 else i
                    v.wait_ge(pack_in[1 - s], j * (16 if windowed else 32) + (16 if windowed else 32))
                    if not windowed:
                        v.wait_ge(gathered[1 - s], j * 128 + 128)
                    embeddings(g - 1, 1 - s, (g - 1) * 5)
                if has_sums:
                    last_part(g - 2)
                if not first:
                    adapts(g - 1, 1 - s, (g - 1) * 5)
                v.wait_ge(type_row_ready, g + 1)
                v.tensor_scalar(is_type[:], type_row[:], c["iota_pf"][0:Z, :], None, ALU.is_equal).then_inc(type_ready, 1)
                if has_sums:
                    v.wait_ge(sum_ready, g - 1)
                v.tensor_tensor(same[:, s, :, :], ids16[:, s, 0, :].rearrange("p (t j) -> p t j", t=TILES), wide(src_early[:, s, :], P),
                                ALU.is_equal).then_inc(same_ready, 1)
                v.wait_ge(same_ready, g + 1)
                v.wait_ge(z_masked_ready, g + 1)
                v.sem_inc(ids_free, 1)

            v.memset(attr[:], 0.0).then_inc(attr_zeroed, 1)
            v.sem_inc(ids_free, 2)
            v.sem_inc(pack_free, 2)
            turns(v, turn)
            last_in = NG // 2 * (16 if windowed else 32)
            v.wait_ge(pack_in[1], last_in)
            if not windowed:
                v.wait_ge(gathered[1], NG // 2 * 128)
            message(NG - 2, 0)
            rest_of(NG - 2)
            last_part(NG - 2)
            embeddings(NG - 1, 1, (NG - 1) * 5)
            adapts(NG - 1, 1, (NG - 1) * 5)
            message(NG - 1, 1)
            rest_of(NG - 1)
            last_part(NG - 1)

        @block.sync
        def _(sp):
            ways(sp, c, lambda windowed: loads(sp, windowed))

        @block.gpsimd
        def _(pool):
            ways(pool, c, lambda windowed: scatters_of_all(pool, windowed))

        @block.scalar
        def _(act):
            ways(act, c, lambda windowed: act_all(act, windowed))

        @block.tensor
        def _(pe):
            ways(pe, c, lambda windowed: pe_all(pe, windowed))

        @block.vector
        def _(v):
            ways(v, c, lambda windowed: vector_all(v, windowed))


class Steps:

    def __init__(self, sem, each):
        self.sem, self.each, self.n = sem, each, 0

    def then(self, ins):
        ins.then_inc(self.sem, 1)
        self.n += 1

    def wait(self, eng, i):
        eng.wait_ge(self.sem, i * self.each + self.n)


LN_STEPS = 6


def layer_norm(v, c, st, i, y, out, sq, m, rstd, var_ready, root_ready, count):
    before, of = count
    wide = [P, m.shape[1], H]
    st.then(v.tensor_reduce(m, y, AX.X, ALU.add))
    st.wait(v, i)
    st.then(v.tensor_scalar(m, m, 1.0 / H, None, ALU.mult))
    st.wait(v, i)
    st.then(v.tensor_tensor(y, y, m.unsqueeze(2).broadcast_to(wide), ALU.subtract))
    st.wait(v, i)
    st.then(v.tensor_tensor(sq, y, y, ALU.mult))
    st.wait(v, i)
    v.tensor_reduce(m, sq, AX.X, ALU.add).then_inc(var_ready, 1)
    v.wait_ge(root_ready, i * of + before + 1)
    st.then(v.reciprocal(rstd, rstd))
    st.wait(v, i)
    st.then(v.tensor_tensor(out, y, rstd.unsqueeze(2).broadcast_to(wide), ALU.mult))
    st.wait(v, i)


def node_rows(ap, i):
    return ap[bass.DynSlice(i * NS, NS), :].rearrange("(a p) f -> p a f", p=P)


def norm_rows(ap, j, tiles=NORM_TILES, first=0):
    return ap[bass.DynSlice(j * NORM_NODES, NORM_NODES), :].rearrange("(p a) f -> p a f", p=P)[:, first:first + tiles, :]


def layer0_nodes(nc, t, c):
    with ExitStack() as ctx:
        def sb(name, shape, dt=F32):
            return ctx.enter_context(nc.sbuf_tensor("n0_" + name, shape, dt))

        def sem(name):
            return ctx.enter_context(nc.semaphore("n0_" + name))

        PAIRS = RELS // 2
        acc = sb("acc", [P, 2, TILES, NORM_TILES, MW])
        x = sb("x", [P, 2, NORM_TILES, H])
        total = sb("total", [P, NORM_TILES, MW])
        y = sb("y", [P, NORM_TILES, H])
        sq = sb("sq", [P, NORM_TILES, H])
        x1 = sb("x1", [P, 2, NORM_TILES, H])
        m = sb("m", [P, NORM_TILES])
        rstd = sb("rstd", [P, NORM_TILES])
        x1T = sb("x1T", [H, 2, NS])
        h1T = sb("h1T", [2 * H, 2, PAIRS, NS])
        h2 = sb("h2", [P, 2, NODE_TILES, RELS * H])
        ps_t = ctx.enter_context(nc.psum_tensor("n0_ps_t", [H, 512], F32))
        ps_h1 = ctx.enter_context(nc.psum_tensor("n0_ps_h1", [2 * H, 2, 512], F32))
        ps_h2 = ctx.enter_context(nc.psum_tensor("n0_ps_h2", [P, NODE_TILES, 512], F32))
        nodes_in = [sem(f"nodes_in{s}") for s in range(2)]
        step = sem("step")
        var_ready = sem("var_ready")
        root_ready = sem("root_ready")
        x1_ready = sem("x1_ready")
        x1_out = [sem(f"x1_out{s}") for s in range(2)]
        x1T_in_psum = sem("x1T_in_psum")
        x1T_ready = sem("x1T_ready")
        h1_in_psum = sem("h1_in_psum")
        h1_ready = sem("h1_ready")
        h2_in_psum = sem("h2_in_psum")
        h2_copied = sem("h2_copied")
        h2_out = [sem(f"h2_out{h}") for h in range(2)]
        wb_zero = sem("wb_zero")
        block = ctx.enter_context(nc.Block())
        LAST = NORM_STEPS - 1

        def steps(eng, turn):
            with eng.Fori(0, LAST // 2) as i:
                for s in range(2):
                    turn(i * 2 + s, i, s)
            turn(LAST, LAST // 2, 0)

        @block.sync
        def _(sp):
            def load(j, s):
                for k in range(TILES):
                    sp.dma_start(acc[:, s, k, :, :], norm_rows(t["acc0"][k], j)).then_inc(nodes_in[s], 16)
                sp.dma_start(x[:, s, :, :], norm_rows(t["x"], j)).then_inc(nodes_in[s], 16)

            def store(j, s):
                wait_in_loop(sp, c, x1_ready, j + 1)
                sp.dma_start(norm_rows(t["x1"], j), x1[:, s, :, :]).then_inc(x1_out[s], 16)

            for s in range(2):
                sp.sem_inc(x1_out[s], 16)
            load(0, 0)
            load(1, 1)
            with sp.Fori(0, LAST // 2 - 1) as i:
                for s in range(2):
                    store(i * 2 + s, s)
                    load(i * 2 + s + 2, s)
            store(LAST - 2, 0)
            load(LAST, 0)
            store(LAST - 1, 1)
            store(LAST, 0)
            sp.wait_ge(x1_out[0], 16 * (LAST // 2 + 2))
            sp.wait_ge(x1_out[1], 16 * (LAST // 2 + 1))

        @block.vector
        def _(v):
            v.memset(c["wb"][:], 0.0).then_inc(wb_zero, 1)
            st = Steps(step, 3 + 4 + 2 * LN_STEPS + 3)
            wide = [P, NORM_TILES, H]

            def turn(j, i, s):
                st.n = 0
                v.wait_ge(nodes_in[s], i * (16 * (TILES + 1)) + 16 * (TILES + 1))
                st.then(v.tensor_tensor(acc[:, s, 0:4], acc[:, s, 0:4], acc[:, s, 4:8], ALU.add))
                st.wait(v, j)
                st.then(v.tensor_tensor(acc[:, s, 0:2], acc[:, s, 0:2], acc[:, s, 2:4], ALU.add))
                st.wait(v, j)
                st.then(v.tensor_tensor(total[:], acc[:, s, 0], acc[:, s, 1], ALU.add))
                st.wait(v, j)
                st.then(v.tensor_scalar(m[:], total[:, :, H], 1e-8, None, ALU.max))
                st.wait(v, j)
                st.then(v.reciprocal(m[:], m[:]))
                st.wait(v, j)
                st.then(v.tensor_tensor(y[:], total[:, :, 0:H], m[:].unsqueeze(2).broadcast_to(wide), ALU.mult))
                st.wait(v, j)
                st.then(v.tensor_tensor(y[:], y[:], x[:, s], ALU.add))
                st.wait(v, j)
                layer_norm(v, c, st, j, y[:], sq[:], sq[:], m[:], rstd[:], var_ready, root_ready, (0, 2))
                st.then(v.tensor_tensor(y[:], sq[:], c["gamma"][:].unsqueeze(1).broadcast_to(wide), ALU.mult))
                st.wait(v, j)
                st.then(v.tensor_tensor(y[:], y[:], c["beta"][:].unsqueeze(1).broadcast_to(wide), ALU.add))
                st.wait(v, j)
                st.then(v.tensor_tensor(y[:], y[:], x[:, s], ALU.add))
                st.wait(v, j)
                v.wait_ge(x1_out[s], i * 16 + 16)
                layer_norm(v, c, st, j, y[:], x1[:, s], sq[:], m[:], rstd[:], var_ready, root_ready, (1, 2))
                v.sem_inc(x1_ready, 1)
                assert st.n == st.each, (st.n, st.each)

            steps(v, turn)

        @block.scalar
        def _(act):
            act.wait_ge(wb_zero, 1)
            for half in range(2):
                act.dma_start(c["wb"][half * H:(half + 1) * H, :, half * H:(half + 1) * H],
                              t["wb"].rearrange("(q b) i o -> b i q o", b=2)[half]).then_inc(c["wb_done"], 16)
            act.sem_inc(h2_copied, NODE_TILES)
            for h in range(2):
                act.sem_inc(h2_out[h], 16)

            def root(j, n):
                act.wait_ge(var_ready, j * 2 + n + 1)
                act.activation(rstd[:], m[:], ACT.Sqrt, bias=c["eps"][:], scale=1.0 / H).then_inc(root_ready, 1)

            def take_x1T(j, h):
                act.wait_ge(x1T_in_psum, j * 2 + h + 1)
                act.activation(x1T[:, h, :], ps_t[:, 0:NS], ACT.Copy).then_inc(x1T_ready, 1)

            def turn(j, i, s, last=False):
                for h in range(2):
                    if not last:
                        root(j + 1, h)
                    for q in range(PAIRS):
                        act.wait_ge(h1_in_psum, j * (2 * PAIRS) + h * PAIRS + q + 1)
                        act.activation(h1T[:, h, q, :], ps_h1[:, q % 2, :], ACT.Relu, bias=c["ba"][:]).then_inc(h1_ready, 1)
                    if h == 0:
                        take_x1T(j, 1)
                    elif not last:
                        take_x1T(j + 1, 0)
                    act.wait_ge(h2_out[h], j * 16 + 16)
                    for a in range(NODE_TILES):
                        act.wait_ge(h2_in_psum, j * (2 * NODE_TILES) + h * NODE_TILES + a + 1)
                        act.activation(h2[:, h, a, :], ps_h2[:, a, 0:RELS * H], ACT.Copy).then_inc(h2_copied, 1)
                    act.wait_ge(h2_copied, j * (2 * NODE_TILES) + (h + 2) * NODE_TILES)
                    act.dma_start(norm_rows(t["h2_wide"], j, NODE_TILES, h * NODE_TILES), h2[:, h]).then_inc(h2_out[h], 16)

            root(0, 0)
            root(0, 1)
            take_x1T(0, 0)
            with act.Fori(0, LAST // 2) as i:
                for s in range(2):
                    turn(i * 2 + s, i, s)
            turn(LAST, LAST // 2, 0, last=True)
            for h in range(2):
                act.wait_ge(h2_out[h], 16 * (NORM_STEPS + 1))

        @block.tensor
        def _(pe):
            def transpose(j, s, h):
                for a in range(NODE_TILES):
                    last = pe.transpose(ps_t[:, a * P:(a + 1) * P], x1[:, s, h * NODE_TILES + a, :], c["ident"][:])
                last.then_inc(x1T_in_psum, 1)

            def turn(j, s, last=False):
                for h in range(2):
                    wait_in_loop(pe, c, x1T_ready, j * 2 + h + 1)
                    for q in range(PAIRS):
                        if q >= 2:
                            wait_in_loop(pe, c, h1_ready, j * (2 * PAIRS) + h * PAIRS + q - 1)
                        pe.matmul(ps_h1[:, q % 2, :], c["wa"][:, q * 2 * H:(q + 1) * 2 * H], x1T[:, h, :],
                                  start=True, stop=True).then_inc(h1_in_psum, 1)
                    if h == 0:
                        transpose(j, s, 1)
                    elif not last:
                        wait_in_loop(pe, c, x1_ready, j + 2)
                        transpose(j + 1, 1 - s, 0)
                    wait_in_loop(pe, c, h1_ready, j * (2 * PAIRS) + (h + 1) * PAIRS)
                    wait_in_loop(pe, c, h2_copied, j * (2 * NODE_TILES) + (h + 1) * NODE_TILES)
                    for a in range(NODE_TILES):
                        for q in range(PAIRS):
                            product = pe.matmul(ps_h2[:, a, q * 2 * H:(q + 1) * 2 * H], h1T[:, h, q, a * P:(a + 1) * P],
                                                c["wb"][:, q, :], start=True, stop=True)
                        product.then_inc(h2_in_psum, 1)

            pe.wait_ge(c["wb_done"], 32)
            pe.wait_ge(x1_ready, 1)
            transpose(0, 0, 0)
            with pe.Fori(0, LAST // 2) as i:
                for s in range(2):
                    turn(i * 2 + s, s)
            turn(LAST, 0, last=True)


def zero_tables(nc, t, c):
    with ExitStack() as ctx:
        zeros = ctx.enter_context(nc.sbuf_tensor("zt_zeros", [P, NP // (2 * P) * H], F32))
        zeroed = ctx.enter_context(nc.semaphore("zt_zeroed"))
        block = ctx.enter_context(nc.Block())

        def fills(pool):
            pool.wait_ge(zeroed, 1)
            for k in range(TILES):
                for half in range(2):
                    pool.dma_start(t["acc1"][k].rearrange("(b p a) f -> b p (a f)", b=2, p=P)[half],
                                   zeros[:]).then_inc(c["acc1_done"][k], 16)
            for k in range(TILES):
                pool.wait_ge(c["acc1_done"][k], 32)

        @block.gpsimd
        def _(pool):
            ways(pool, c, lambda windowed: None if windowed else fills(pool))

        @block.vector
        def _(v):
            ways(v, c, lambda windowed: None if windowed else v.memset(zeros[:], 0.0).then_inc(zeroed, 1))


def layer1_edges(nc, t, c):
    with ExitStack() as ctx:
        def sb(name, shape, dt=F32):
            return ctx.enter_context(nc.sbuf_tensor("e1_" + name, shape, dt))

        def sem(name):
            return ctx.enter_context(nc.semaphore("e1_" + name))

        row_col = [sb(f"row_col{s}", [P, TILES], I32) for s in range(2)]
        pack = sb("pack", [P, 2, 2, TILES])
        dst_row = sb("dst_row", [P, 2, GE], I32)
        dst_col = sb("dst_col", [P, 2, TILES], I32)
        of_src = sb("of_src", [P, 2, TILES, H])
        same = sb("same", [P, 2, TILES, P])
        earlier = sb("earlier", [P, TILES, P])
        count = sb("count", [P, TILES])
        dump_off = sb("dump_off", [P, TILES])
        index = [sb(f"index{s}", [P, TILES], I32) for s in range(2)]
        msg = sb("msg", [P, 2, TILES, H])
        summed = sb("summed", [P, 2, TILES, H])
        ps_sum = [ctx.enter_context(nc.psum_tensor(f"e1_ps_sum{s}", [P, 512], F32)) for s in range(2)]
        edges_in = [sem(f"edges_in{s}") for s in range(2)]
        slot_free = sem("slot_free")
        gathered = [sem(f"gathered{s}") for s in range(2)]
        zeroed = sem("zeroed")
        step = sem("step")
        index_ready = sem("index_ready")
        onehot_ready = sem("onehot_ready")
        msg_ready = sem("msg_ready")
        sum_ready = sem("sum_ready")
        summed_ready = sem("summed_ready")
        first_added = sem("first_added")
        next_added = sem("next_added")
        block = ctx.enter_context(nc.Block())
        acc_done = c["acc1_done"]

        def cols(name, g):
            return t[name][:, bass.DynSlice(g, 1), :].rearrange("p g k -> p (g k)")

        def loads(sp, windowed):
            with sp.Fori(0, NG // 2) as i:
                for s in range(2):
                    g = i * 2 + s
                    wait_in_loop(sp, c, slot_free, g + 1)
                    sp.dma_start(row_col[s][:], cols("row", g)).then_inc(edges_in[s], 16)
                    sp.dma_start(pack[:, s, :, :], t["pack1"][:, bass.DynSlice(g, 1), :, :].rearrange("p g r k -> p (g r) k")).then_inc(edges_in[s], 16)
                    if not windowed:
                        sp.dma_start(dst_col[:, s, :], cols("dst", g)).then_inc(edges_in[s], 16)
                        sp.dma_start(dst_row[:, s, :],
                                     t["dst_flat"][bass.DynSlice(g * GE, GE)].partition_broadcast(P)).then_inc(edges_in[s], 16)

        def pool_all(pool, windowed):
            each = 32 if windowed else 64

            def gathers(i, s):
                wait_in_loop(pool, c, edges_in[s], i * each + each)
                for k in range(TILES):
                    nc.gpsimd.indirect_dma_start(of_src[:, s, k, :], None, t["h2"],
                                                 bass.IndirectOffsetOnAxis(ap=row_col[s][:, k:k + 1], axis=0)).then_inc(gathered[s], 16)

            def scatters(i, s):
                wait_in_loop(pool, c, index_ready, i * 2 + s + 1)
                wait_in_loop(pool, c, summed_ready, i * 2 + s + 1)
                for k in range(TILES):
                    wait_in_loop(pool, c, acc_done[k], (i * 2 + s) * 16 + 32)
                    nc.gpsimd.indirect_dma_start(t["acc1"][k], bass.IndirectOffsetOnAxis(ap=index[s][:, k:k + 1], axis=0),
                                                 summed[:, s, k, :], None, compute_op=ALU.add).then_inc(acc_done[k], 16)

            if windowed:
                with pool.Fori(0, NG // 2) as i:
                    gathers(i, 0)
                    gathers(i, 1)
                return
            gathers(0, 0)
            with pool.Fori(0, NG // 2 - 1) as i:
                gathers(i, 1)
                scatters(i, 0)
                gathers(i + 1, 0)
                scatters(i, 1)
            gathers(NG // 2 - 1, 1)
            scatters(NG // 2 - 1, 0)
            scatters(NG // 2 - 1, 1)
            for k in range(TILES):
                pool.wait_ge(acc_done[k], NG * 16 + 32)

        def act_all(act):
            with act.Fori(0, NG // 2) as i:
                for s in range(2):
                    g = i * 2 + s
                    act.wait_ge(sum_ready, g + 1)
                    for k in range(TILES):
                        act.wait_ge(acc_done[k], g * 16 + 16)
                    act.activation(summed[:, s, :, :], ps_sum[s][:, 0:TILES * H].rearrange("p (t f) -> p t f", t=TILES),
                                   ACT.Copy).then_inc(summed_ready, 1)

        def pe_all(pe, windowed):
            with pe.Fori(0, NG // 2) as i:
                for s in range(2):
                    g = i * 2 + s
                    wait_in_loop(pe, c, msg_ready, g + 1)
                    for k in range(TILES):
                        at = 0 if windowed else k * H
                        last = pe.matmul(ps_sum[s][:, at:at + H], same[:, s, k, :], msg[:, s, k, :],
                                         start=(k == 0 or not windowed), stop=(k == TILES - 1 or not windowed))
                    last.then_inc(sum_ready, 1)

        def add_to_blocks(v, g, s, at):
            v.wait_ge(sum_ready, g + 1)
            if not (isinstance(g, int) and g == 0):
                v.wait_ge(next_added, g)
            part = ps_sum[s][:, 0:H]
            one = c["agg"][:, bass.DynSlice(at, 1), :].rearrange("p b f -> p (b f)")
            two = c["agg"][:, bass.DynSlice(at + 1, 1), :].rearrange("p b f -> p (b f)")
            v.scalar_tensor_tensor(one, part, c["in_first"][:, bass.DynSlice(g, 1)], one, ALU.mult, ALU.add).then_inc(first_added, 1)
            v.scalar_tensor_tensor(two, part, c["in_next"][:, bass.DynSlice(g, 1)], two, ALU.mult, ALU.add).then_inc(next_added, 1)

        def block_of(v, g):
            return v.value_load(c["block"][0:1, bass.DynSlice(g, 1)], min_val=0, max_val=BLOCKS - 2)

        def windowed_sums(v):
            def messages(g, s, i):
                v.wait_ge(edges_in[s], i * 32 + 32)
                v.tensor_tensor(same[:, s, :, :], c["iota_rowf"][:].unsqueeze(1).broadcast_to([P, TILES, P]),
                                pack[:, s, 0, :].unsqueeze(2).broadcast_to([P, TILES, P]), ALU.is_equal).then_inc(onehot_ready, 1)
                v.wait_ge(gathered[s], i * 128 + 128)
                v.tensor_tensor(msg[:, s, :, :], of_src[:, s, :, :], pack[:, s, 1, :].unsqueeze(2).broadcast_to([P, TILES, H]),
                                ALU.mult).then_inc(onehot_ready, 1)
                v.wait_ge(onehot_ready, g * 2 + 2)
                v.sem_inc(msg_ready, 1)
                v.sem_inc(slot_free, 1)

            v.memset(c["agg"][:], 0.0).then_inc(zeroed, 1)
            v.wait_ge(zeroed, 1)
            v.sem_inc(slot_free, 2)
            messages(0, 0, 0)
            messages(1, 1, 0)
            with v.Fori(1, NG // 2) as i:
                for s in range(2):
                    add_to_blocks(v, i * 2 + (s - 2), s, block_of(v, i * 2 + (s - 2)))
                    messages(i * 2 + s, s, i)
            for s in range(2):
                add_to_blocks(v, NG - 2 + s, s, block_of(v, NG - 2 + s))

        def table_sums(v):
            v.sem_inc(slot_free, 2)
            with v.Fori(0, NG // 2) as i:
                for s in range(2):
                    g = i * 2 + s
                    base = g * 5
                    v.wait_ge(edges_in[s], i * 64 + 64)
                    for k in range(TILES):
                        v.wait_ge(acc_done[k], g * 16 + 16)
                    one_of_equals(v, c, step, base, dst_col[:, s, :], dst_row[:, s, :], same[:, s, :, :], earlier[:], count[:],
                                  dump_off[:], index[s][:]).then_inc(index_ready, 1)
                    v.wait_ge(gathered[s], i * 128 + 128)
                    v.tensor_tensor(msg[:, s, :, :], of_src[:, s, :, :], pack[:, s, 1, :].unsqueeze(2).broadcast_to([P, TILES, H]),
                                    ALU.mult).then_inc(msg_ready, 1)
                    v.wait_ge(index_ready, g + 1)
                    v.wait_ge(msg_ready, g + 1)
                    v.sem_inc(slot_free, 1)

        @block.sync
        def _(sp):
            sp.dma_start(c["x1"][:], t["x1"].rearrange("(a p) f -> p a f", p=P)).then_inc(c["x1_loaded"], 16)
            ways(sp, c, lambda windowed: loads(sp, windowed))

        @block.gpsimd
        def _(pool):
            ways(pool, c, lambda windowed: pool_all(pool, windowed))

        @block.scalar
        def _(act):
            ways(act, c, lambda windowed: None if windowed else act_all(act))

        @block.tensor
        def _(pe):
            ways(pe, c, lambda windowed: pe_all(pe, windowed))

        @block.vector
        def _(v):
            ways(v, c, lambda windowed: windowed_sums(v) if windowed else table_sums(v))


def collect_tables(nc, t, c):
    with ExitStack() as ctx:
        acc = ctx.enter_context(nc.sbuf_tensor("ct_acc", [P, TILES, NODE_TILES, H], F32))
        acc_in = ctx.enter_context(nc.semaphore("ct_acc_in"))
        step = ctx.enter_context(nc.semaphore("ct_step"))
        summed = ctx.enter_context(nc.semaphore("ct_summed"))
        block = ctx.enter_context(nc.Block())

        def loads(sp):
            sp.sem_inc(summed, 1)
            with sp.Fori(0, STEPS) as i:
                wait_in_loop(sp, c, summed, i + 1)
                for k in range(TILES):
                    sp.dma_start(acc[:, k, :, :], node_rows(t["acc1"][k], i)).then_inc(acc_in, 16)

        def sums(v):
            with v.Fori(0, STEPS) as i:
                v.wait_ge(acc_in, i * (16 * TILES) + 16 * TILES)
                total = c["agg"][:, bass.DynSlice(i * NODE_TILES, NODE_TILES), :]
                v.tensor_tensor(total, acc[:, 0, :, :], acc[:, 1, :, :], ALU.add).then_inc(step, 1)
                for k in range(2, TILES):
                    v.wait_ge(step, i * (TILES - 1) + k - 1)
                    v.tensor_tensor(total, total, acc[:, k, :, :], ALU.add).then_inc(step, 1)
                v.wait_ge(step, i * (TILES - 1) + TILES - 1)
                v.sem_inc(summed, 1)

        @block.sync
        def _(sp):
            ways(sp, c, lambda windowed: None if windowed else loads(sp))

        @block.vector
        def _(v):
            ways(v, c, lambda windowed: None if windowed else sums(v))


def layer1_nodes(nc, t, c):
    with ExitStack() as ctx:
        def sb(name, shape, dt=F32):
            return ctx.enter_context(nc.sbuf_tensor("n1_" + name, shape, dt))

        def sem(name):
            return ctx.enter_context(nc.semaphore("n1_" + name))

        tiles = BLOCKS // LAST_STEPS
        y = [sb(f"y{n}", [P, tiles, H]) for n in range(LAST_STEPS)]
        sq = [sb(f"sq{n}", [P, tiles, H]) for n in range(2)]
        m = [sb(f"m{n}", [P, tiles]) for n in range(LAST_STEPS)]
        rstd = [sb(f"rstd{n}", [P, tiles]) for n in range(LAST_STEPS)]
        step = sem("step")
        biased = sem("biased")
        relued = sem("relued")
        centered = sem("centered")
        squared = sem("squared")
        var_ready = sem("var_ready")
        root_ready = sem("root_ready")
        result_ready = sem("result_ready")
        nodes_out = sem("nodes_out")
        block = ctx.enter_context(nc.Block())
        wide = [P, tiles, H]

        def of(buffer, n):
            return buffer[:, n * tiles:(n + 1) * tiles, :]

        @block.sync
        def _(sp):
            for n in range(LAST_STEPS):
                sp.wait_ge(result_ready, n + 1)
                sp.dma_start(of(t["out"], n), y[n][:]).then_inc(nodes_out, 16)
            sp.wait_ge(nodes_out, 16 * LAST_STEPS)

        @block.vector
        def _(v):
            done = 0

            def wait_own(ins):
                nonlocal done
                ins.then_inc(step, 1)
                done += 1
                v.wait_ge(step, done)

            def center(n):
                v.wait_ge(relued, n + 1)
                wait_own(v.tensor_tensor(y[n][:], y[n][:], of(c["x1"], n), ALU.add))
                wait_own(v.tensor_reduce(m[n][:], y[n][:], AX.X, ALU.add))
                wait_own(v.tensor_scalar(m[n][:], m[n][:], 1.0 / H, None, ALU.mult))
                v.tensor_tensor(y[n][:], y[n][:], m[n][:].unsqueeze(2).broadcast_to(wide), ALU.subtract).then_inc(centered, 1)

            def scale(n):
                v.wait_ge(squared, n + 1)
                v.tensor_reduce(m[n][:], sq[n % 2][:], AX.X, ALU.add).then_inc(var_ready, 1)
                v.wait_ge(root_ready, n + 1)
                wait_own(v.reciprocal(rstd[n][:], rstd[n][:]))
                v.tensor_tensor(y[n][:], y[n][:], rstd[n][:].unsqueeze(2).broadcast_to(wide), ALU.mult).then_inc(result_ready, 1)

            v.wait_ge(c["x1_loaded"], 16)
            for n in range(LAST_STEPS):
                v.tensor_tensor(y[n][:], of(c["agg"], n), c["bias2"][:].unsqueeze(1).broadcast_to(wide), ALU.add)\
                 .then_inc(biased, 1)
                if n >= 1:
                    center(n - 1)
                if n >= 2:
                    scale(n - 2)
            center(LAST_STEPS - 1)
            scale(LAST_STEPS - 2)
            scale(LAST_STEPS - 1)

        @block.scalar
        def _(act):
            def square(n):
                act.wait_ge(centered, n + 1)
                if n >= 2:
                    act.wait_ge(var_ready, n - 1)
                act.activation(sq[n % 2][:], y[n][:], ACT.Square).then_inc(squared, 1)

            def root(n):
                act.wait_ge(var_ready, n + 1)
                act.activation(rstd[n][:], m[n][:], ACT.Sqrt, bias=c["eps"][:], scale=1.0 / H).then_inc(root_ready, 1)

            for n in range(LAST_STEPS):
                act.wait_ge(biased, n + 1)
                act.activation(y[n][:], y[n][:], ACT.Relu).then_inc(relued, 1)
                if n >= 1:
                    square(n - 1)
                if n >= 2:
                    root(n - 2)
            square(LAST_STEPS - 1)
            root(LAST_STEPS - 2)
            root(LAST_STEPS - 1)


def program(nc, t):
    with ExitStack() as ctx:
        def sb(name, shape, dt=F32):
            return ctx.enter_context(nc.sbuf_tensor(name, shape, dt))

        def dram(name, shape, dt=F32):
            return nc.dram_tensor(name, shape, dt).ap()

        t["window_rows"] = dram("window_rows", [NP, WW], BF16)
        t["ids16"] = dram("ids16", [NG, 3, GE], I16)
        t["ids8"] = dram("ids8", [NG, GE], U8)
        t["pack0"] = dram("pack0", [P, NG, 2, TILES])
        t["pack1"] = dram("pack1", [P, NG, 2, TILES])
        t["row"] = dram("row_of_edge", [P, NG, TILES], I32)
        t["acc0"] = [dram(f"acc0_{k}", [NP, MW]) for k in range(TILES)]
        t["acc1"] = [dram(f"acc1_{k}", [NP, H]) for k in range(TILES)]
        t["x1"] = dram("x1_rows", [NP, H])
        t["h2_wide"] = dram("h2_rows", [NP, RELS * H])
        t["h2"] = t["h2_wide"].rearrange("n (r f) -> (n r) f", r=RELS)
        c = {
            "iota_p": sb("iota_p", [P, 1], I32), "iota_row": sb("iota_row", [P, P], I32), "dump": sb("dump", [P, 1], I32),
            "iota_pf": sb("iota_pf", [P, 1]), "iota_rowf": sb("iota_rowf", [P, P]), "dumpf": sb("dumpf", [P, 1]),
            "ones": sb("ones", [P, P]), "ones_bf": sb("ones_bf", [P, P], BF16), "eps": sb("eps", [P, 1]),
            "powers": sb("powers", [P, 1]), "powers_bf": sb("powers_bf", [P, 1], BF16), "bounds": sb("bounds", [P, 1]),
            "earlier_mask": sb("earlier_mask", [P, P]), "ident": sb("ident", [P, P]),
            "sorted": sb("sorted", [1, 1], I32), "z_table": sb("z_table", [HIGH, LOW], BF16),
            "emb_parts": sb("emb_parts", [Z, PARTS, G], BF16), "block": sb("block", [1, NG], I32),
            "in_first": sb("in_first", [P, NG]), "in_next": sb("in_next", [P, NG]), "agg": sb("agg", [P, BLOCKS, H]),
            "x1": sb("x1", [P, BLOCKS, H]), "x1_loaded": ctx.enter_context(nc.semaphore("x1_loaded")),
            "gather_sums": ctx.enter_context(nc.semaphore("gather_sums")),
            "node_of_ready": ctx.enter_context(nc.semaphore("node_of_ready")),
            "silu": sb("silu", [SIDE + H + 1, 2, GE // 2]),
            "w1t": sb("w1t", [SIDE + R, SIDE + H]), "b1": sb("b1", [SIDE + H, 1]),
            "w2b": sb("w2b", [SIDE + H + 1, 2 * H]),
            "gamma": sb("gamma", [P, H]), "beta": sb("beta", [P, H]), "bias2": sb("bias2", [P, H]),
            "wa": sb("wa", [H, RELS * H]), "ba": sb("ba", [2 * H, 1]), "wb": sb("wb", [2 * H, RELS // 2, 2 * H]),
            "acc0_done": [ctx.enter_context(nc.semaphore(f"acc0_done{k}")) for k in range(TILES)],
            "acc1_done": [ctx.enter_context(nc.semaphore(f"acc1_done{k}")) for k in range(TILES)],
            "waits_passed": ctx.enter_context(nc.semaphore("waits_passed")),
            "wb_done": ctx.enter_context(nc.semaphore("wb_done")),
        }
        prepare_edges(nc, t, c)
        prepare_nodes(nc, t, c)
        layer0_edges(nc, t, c)
        layer0_nodes(nc, t, c)
        zero_tables(nc, t, c)
        layer1_edges(nc, t, c)
        collect_tables(nc, t, c)
        layer1_nodes(nc, t, c)


def kernel(x, src, dst, edge_attr_40, edge_type_8, edge_weight, edge_weight1, node_type_119, node_vec,
           L0_gnn_W1, L0_gnn_b1, L0_gnn_W2, L0_gnn_b2, L0_gnn_emb, L0_gnn_adaptW, L0_gnn_gamma, L0_gnn_beta,
           L1_gnn_weight1, L1_gnn_weight2, L1_gnn_bias1, L1_gnn_bias2):
    import numpy as np
    import concourse.bacc as bacc
    from concourse.bass_utils import run_bass_kernel_spmd as run

    def edges(a, fill):
        flat = np.full(NG * GE, fill, a.dtype)
        flat[:E] = a.reshape(E)
        return np.ascontiguousarray(flat.reshape(NG, TILES, P).transpose(2, 0, 1)), flat

    def nodes(a):
        rows = np.zeros((NP, *a.shape[1:]), a.dtype)
        rows[:N] = a
        return rows

    src_cols, src_flat = edges(np.asarray(src), PAD_NODE)
    dst_cols, dst_flat = edges(np.asarray(dst), PAD_NODE)
    attr = np.zeros((R, NG * GE), np.float32)
    attr[:, :E] = np.asarray(edge_attr_40).T
    wa = np.asarray(L1_gnn_weight1)
    arrays = {
        "src": src_cols, "dst": dst_cols, "src_flat": src_flat, "dst_flat": dst_flat,
        "rel": edges(np.asarray(edge_type_8), 0)[0], "dist": edges(np.asarray(edge_weight), 0)[0],
        "norm": edges(np.asarray(edge_weight1), 0)[0], "attr": attr,
        "x": nodes(np.asarray(x)), "z": nodes(np.asarray(node_type_119)), 
        "x_mult": nodes(np.concatenate([np.asarray(x), np.asarray(node_vec)[:, None]], 1)),
        "w1t": np.asarray(L0_gnn_W1).T, "b1": np.asarray(L0_gnn_b1)[:, None], "w2t": np.asarray(L0_gnn_W2).T,
        "b2": np.asarray(L0_gnn_b2)[None, :], "emb": np.asarray(L0_gnn_emb), "embT": np.asarray(L0_gnn_emb).T,
        "adaptT": np.asarray(L0_gnn_adaptW).T, "gamma": np.asarray(L0_gnn_gamma), "beta": np.asarray(L0_gnn_beta),
        "bias2": np.asarray(L1_gnn_bias2), "ba": np.tile(np.asarray(L1_gnn_bias1), 2)[:, None],
        "powers": (2.0 ** (P // 2 - np.arange(P, dtype=np.float32)))[:, None].astype(np.float32),
        "wa": wa.transpose(1, 0, 2).reshape(H, RELS * H), "wb": np.asarray(L1_gnn_weight2),
    }
    arrays = {name: np.ascontiguousarray(a) for name, a in arrays.items()}
    nc = bacc.Bacc("TRN2", target_bir_lowering=False, num_devices=1)
    t = {name: nc.dram_tensor(f"in_{name}", a.shape, mybir.dt.from_np(a.dtype), kind="ExternalInput").ap()
         for name, a in arrays.items()}
    t["out"] = nc.dram_tensor("result", (P, BLOCKS, H), F32, kind="ExternalOutput").ap()
    program(nc, t)
    r = run(nc, [{f"in_{name}": a for name, a in arrays.items()}], core_ids=[0])
    return r.results[0]["result"].transpose(1, 0, 2).reshape(NP, H)[:N]
```
